# Optimizing a Trainium2 kernel written in Bass

```python
import numpy as np
import jax
import jax.numpy as jnp

def _softmax(x, axis=-1):
    return jax.nn.softmax(x, axis=axis)
def _gelu(x):
    return jax.nn.gelu(x, approximate=True)
def _silu(x):
    return jax.nn.silu(x)
def _sigmoid(x):
    return jax.nn.sigmoid(x)
def _layernorm(x, axis=-1, eps=1e-5):
    m = jnp.mean(x, axis=axis, keepdims=True)
    v = jnp.var(x, axis=axis, keepdims=True)
    return (x - m) / jnp.sqrt(v + eps)
def _scatter_add(tgt, idx, src, axis=0):
    return tgt.at[idx].add(src)
def _segment_sum(src, seg, n):
    return jax.ops.segment_sum(src, seg, n)

kernel_name = 'mk_adj_preln_d4_adj_256_88546c'

def setup_inputs(seed: int = 0):
    np.random.seed(seed)
    _w = jnp.asarray
    def _rec_inputs():
        import jax
        import jax.numpy as jnp
        _gk = jax.random.key(seed)
        x = 7.22e-05 + 1 * jax.random.normal(jax.random.fold_in(_gk, 1), (32, 512, 256), jnp.float32)
        _a = jax.random.bernoulli(jax.random.fold_in(_gk, 2), 0.03125, (32, 512, 512))
        _a = jnp.logical_or(_a, jnp.swapaxes(_a, -1, -2))
        _a = jnp.logical_or(_a, jnp.eye(512, dtype=bool))
        _af = _a.astype(jnp.float32)
        _af = _af * jax.random.uniform(jax.random.fold_in(_gk, 3), (32, 512, 512), jnp.float32, 0.05, 1)
        adj = _af
        return x, adj
    x, adj = _rec_inputs()
    def _L0_gnn_setup():
        import jax, jax.numpy as jnp
        import numpy as np
        BN_EPS = 1e-05
        key = jax.random.key(seed)
        k = jax.random.split(key, 4)
        B, N, H = (16, 2048, 256)
        h = jax.random.normal(k[0], (B, N, H), dtype=jnp.float32)
        adj = jax.random.uniform(k[1], (B, N, N), dtype=jnp.float32)
        W = jax.random.normal(k[2], (H, H), dtype=jnp.float32) * (1.0 / np.sqrt(H))
        b = jnp.zeros((H,), dtype=jnp.float32)
        bn_weight = jnp.ones((H,), dtype=jnp.float32)
        bn_bias = jnp.zeros((H,), dtype=jnp.float32)
        res_weight = jnp.zeros((), dtype=jnp.float32)
        return {'h': h, 'adj': adj, 'W': W, 'b': b, 'bn_weight': bn_weight, 'bn_bias': bn_bias, 'res_weight': res_weight}
    _L0_gnn_all = _L0_gnn_setup()
    _L0_gnn_in = {k: v for k, v in _L0_gnn_all.items() if k in ('W', 'b', 'bn_weight', 'bn_bias', 'res_weight', )}
    del _L0_gnn_all

    def _L1_gnn_setup():
        import jax, jax.numpy as jnp
        import numpy as np
        B, N, D_IN = (2, 2048, 256)
        H, DH = (8, 32)
        key = jax.random.key(seed)
        ks = jax.random.split(key, 7)
        s = 1.0 / np.sqrt(D_IN)
        x = jax.random.normal(ks[0], (B, N, D_IN), dtype=jnp.float32)
        adj = jax.random.randint(ks[1], (B, N, N), 0, 2).astype(jnp.float32)
        eye = jnp.eye(N, dtype=jnp.float32)[None]
        adj = jnp.maximum(adj, eye)
        Wq = jax.random.normal(ks[2], (H * DH, D_IN), dtype=jnp.float32) * s
        Wk = jax.random.normal(ks[3], (H * DH, D_IN), dtype=jnp.float32) * s
        Wv = jax.random.normal(ks[4], (H * DH, D_IN), dtype=jnp.float32) * s
        Wo = jax.random.normal(ks[5], (H * DH, H * DH), dtype=jnp.float32) * s
        bo = jnp.zeros((H * DH,), dtype=jnp.float32)
        return {'x': x, 'adj': adj, 'Wq': Wq, 'Wk': Wk, 'Wv': Wv, 'Wo': Wo, 'bo': bo}
    _L1_gnn_all = _L1_gnn_setup()
    _L1_gnn_in = {k: v for k, v in _L1_gnn_all.items() if k in ('Wq', 'Wk', 'Wv', 'Wo', 'bo', )}
    del _L1_gnn_all

    def _L2_gnn_setup():
        import jax, jax.numpy as jnp
        import numpy as np
        B, N, D, H = (8, 2048, 256, 1024)
        RMS_EPS = 1e-06

        def _rmsnorm(h, w, eps=RMS_EPS):
            var = jnp.mean(jnp.square(h), axis=-1, keepdims=True)
            return h * jax.lax.rsqrt(var + eps) * w
        key = jax.random.key(seed)
        ks = jax.random.split(key, 5)
        x = jax.random.normal(ks[0], (B, N, D), dtype=jnp.float32)
        adjacency = jax.random.uniform(ks[1], (B, N, N), dtype=jnp.float32)
        epsilon = jnp.zeros((), dtype=jnp.float32)
        W1 = jax.random.normal(ks[2], (D, H), dtype=jnp.float32) * (1.0 / np.sqrt(D))
        b1 = jnp.zeros((H,), dtype=jnp.float32)
        rms_weight = jnp.ones((H,), dtype=jnp.float32)
        W2 = jax.random.normal(ks[3], (H, D), dtype=jnp.float32) * (1.0 / np.sqrt(H))
        b2 = jnp.zeros((D,), dtype=jnp.float32)
        return {'x': x, 'adjacency': adjacency, 'epsilon': epsilon, 'W1': W1, 'b1': b1, 'rms_weight': rms_weight, 'W2': W2, 'b2': b2}
    _L2_gnn_all = _L2_gnn_setup()
    _L2_gnn_in = {k: v for k, v in _L2_gnn_all.items() if k in ('epsilon', 'W1', 'b1', 'rms_weight', 'W2', 'b2', )}
    del _L2_gnn_all

    def _L3_gnn_setup():
        import jax, jax.numpy as jnp
        import numpy as np
        B, N, IN_DIM, OUT_DIM, H = (8, 1024, 256, 256, 4)
        D = OUT_DIM // H
        NEG_INF = -9000000000000000.0
        LRELU_SLOPE = 0.2
        key = jax.random.key(seed)
        k1, k2, k3, k4 = jax.random.split(key, 4)
        x = jax.random.normal(k1, (B, N, IN_DIM), dtype=jnp.float32)
        adj = jax.random.randint(k2, (B, N, N), 0, 2).astype(jnp.float32)
        W = jax.random.normal(k3, (IN_DIM, H * D), dtype=jnp.float32) * jnp.sqrt(2.0 / (IN_DIM + H * D))
        a = jax.random.normal(k4, (H, 2 * D), dtype=jnp.float32) * jnp.sqrt(2.0 / (H + 2 * D))
        return {'x': x, 'adj': adj, 'W': W, 'a': a}
    _L3_gnn_all = _L3_gnn_setup()
    _L3_gnn_in = {k: v for k, v in _L3_gnn_all.items() if k in ('W', 'a', )}
    del _L3_gnn_all

    return {
        "x": x,
        "adj": adj,
        "L0_gnn_W": _L0_gnn_in["W"],
        "L0_gnn_b": _L0_gnn_in["b"],
        "L0_gnn_bn_weight": _L0_gnn_in["bn_weight"],
        "L0_gnn_bn_bias": _L0_gnn_in["bn_bias"],
        "L0_gnn_res_weight": _L0_gnn_in["res_weight"],
        "L1_gnn_Wq": _L1_gnn_in["Wq"],
        "L1_gnn_Wk": _L1_gnn_in["Wk"],
        "L1_gnn_Wv": _L1_gnn_in["Wv"],
        "L1_gnn_Wo": _L1_gnn_in["Wo"],
        "L1_gnn_bo": _L1_gnn_in["bo"],
        "L2_gnn_epsilon": _L2_gnn_in["epsilon"],
        "L2_gnn_W1": _L2_gnn_in["W1"],
        "L2_gnn_b1": _L2_gnn_in["b1"],
        "L2_gnn_rms_weight": _L2_gnn_in["rms_weight"],
        "L2_gnn_W2": _L2_gnn_in["W2"],
        "L2_gnn_b2": _L2_gnn_in["b2"],
        "L3_gnn_W": _L3_gnn_in["W"],
        "L3_gnn_a": _L3_gnn_in["a"],
    }

def reference(x, adj, L0_gnn_W, L0_gnn_b, L0_gnn_bn_weight, L0_gnn_bn_bias, L0_gnn_res_weight, L1_gnn_Wq, L1_gnn_Wk, L1_gnn_Wv, L1_gnn_Wo, L1_gnn_bo, L2_gnn_epsilon, L2_gnn_W1, L2_gnn_b1, L2_gnn_rms_weight, L2_gnn_W2, L2_gnn_b2, L3_gnn_W, L3_gnn_a):
    import jax
    import jax.numpy as jnp
    def _L0_gnn_ref(h, adj, W, b, bn_weight, bn_bias, res_weight):
        import jax, jax.numpy as jnp
        import numpy as np
        BN_EPS = 1e-05
        B, N, H = h.shape
        A = adj + jnp.eye(N, dtype=adj.dtype)
        deg = A.sum(axis=-1)
        dis = deg ** (-0.5)
        dis = jnp.where(jnp.isinf(dis), 0.0, dis)
        A_hat = dis[:, :, None] * A * dis[:, None, :]
        h_lin = jnp.einsum('bnd,hd->bnh', h, W) + b
        out = jnp.einsum('bmn,bnh->bmh', A_hat, h_lin)
        flat = out.reshape(B * N, H)
        mean = flat.mean(axis=0)
        var = flat.var(axis=0)
        flat = (flat - mean) * jax.lax.rsqrt(var + BN_EPS) * bn_weight + bn_bias
        out = flat.reshape(B, N, H)
        out = jax.nn.relu(out)
        return out + res_weight * h

    def _L1_gnn_ref(x, adj, Wq, Wk, Wv, Wo, bo):
        import jax, jax.numpy as jnp
        import numpy as np
        B, N, D_IN = (2, 2048, 256)
        H, DH = (8, 32)
        b, n, _ = x.shape
        Q = (x @ Wq.T).reshape(b, n, H, DH).transpose(0, 2, 1, 3)
        K = (x @ Wk.T).reshape(b, n, H, DH).transpose(0, 2, 1, 3)
        V = (x @ Wv.T).reshape(b, n, H, DH).transpose(0, 2, 1, 3)
        scores = jnp.einsum('bhnd,bhmd->bhnm', Q, K) / jnp.sqrt(jnp.float32(DH))
        mask = adj[:, None, :, :] == 0
        scores = jnp.where(mask, -jnp.inf, scores)
        attn = jax.nn.softmax(scores, axis=-1)
        out = jnp.einsum('bhnm,bhmd->bhnd', attn, V)
        out = out.transpose(0, 2, 1, 3).reshape(b, n, H * DH)
        return out @ Wo.T + bo

    def _L2_gnn_ref(x, adjacency, epsilon, W1, b1, rms_weight, W2, b2):
        import jax, jax.numpy as jnp
        import numpy as np
        B, N, D, H = (8, 2048, 256, 1024)
        RMS_EPS = 1e-06

        def _rmsnorm(h, w, eps=RMS_EPS):
            var = jnp.mean(jnp.square(h), axis=-1, keepdims=True)
            return h * jax.lax.rsqrt(var + eps) * w
        neighbor_sum = jnp.einsum('bnm,bmd->bnd', adjacency, x)
        agg = epsilon * x + neighbor_sum
        h = jnp.einsum('bnd,dh->bnh', agg, W1) + b1
        h = jax.nn.silu(_rmsnorm(h, rms_weight))
        out = jnp.einsum('bnh,hd->bnd', h, W2) + b2
        return out

    def _L3_gnn_ref(x, adj, W, a):
        import jax, jax.numpy as jnp
        import numpy as np
        B, N, IN_DIM, OUT_DIM, H = (8, 1024, 256, 256, 4)
        D = OUT_DIM // H
        NEG_INF = -9000000000000000.0
        LRELU_SLOPE = 0.2
        h = jnp.einsum('bni,io->bno', x, W).reshape(x.shape[0], x.shape[1], H, D)
        h = h.transpose(0, 2, 1, 3)
        a1, a2 = (a[:, :D], a[:, D:])
        e_i = jnp.einsum('bhnd,hd->bhn', h, a1)
        e_j = jnp.einsum('bhmd,hd->bhm', h, a2)
        e = e_i[:, :, :, None] + e_j[:, :, None, :]
        e = jnp.where(e > 0, e, LRELU_SLOPE * e)
        e = jnp.where(adj[:, None, :, :] > 0, e, NEG_INF)
        attn = jax.nn.softmax(e, axis=-1)
        out = jnp.einsum('bhnm,bhmd->bhnd', attn, h)
        out = out.transpose(0, 2, 1, 3).reshape(x.shape[0], x.shape[1], H * D)
        return out

    h = jnp.maximum(_layernorm(x, axis=-1), 0.0)
    x = x + _L0_gnn_ref(h, adj, L0_gnn_W, L0_gnn_b, L0_gnn_bn_weight, L0_gnn_bn_bias, L0_gnn_res_weight)
    h = jnp.maximum(_layernorm(x, axis=-1), 0.0)
    x = x + _L1_gnn_ref(h, adj, L1_gnn_Wq, L1_gnn_Wk, L1_gnn_Wv, L1_gnn_Wo, L1_gnn_bo)
    h = jnp.maximum(_layernorm(x, axis=-1), 0.0)
    x = x + _L2_gnn_ref(h, adj, L2_gnn_epsilon, L2_gnn_W1, L2_gnn_b1, L2_gnn_rms_weight, L2_gnn_W2, L2_gnn_b2)
    h = jnp.maximum(_layernorm(x, axis=-1), 0.0)
    x = x + _L3_gnn_ref(h, adj, L3_gnn_W, L3_gnn_a)
    return x


_drawn_inputs = setup_inputs


def setup_inputs(seed=0):
    import zlib

    import numpy as np

    out = dict(_drawn_inputs(seed))
    spreads = {'L0_gnn_b': (0.0, 0.1),
     'L0_gnn_bn_weight': (1.0, 0.2),
     'L0_gnn_bn_bias': (0.0, 0.1),
     'L1_gnn_bo': (0.0, 0.1),
     'L2_gnn_b1': (0.0, 0.8),
     'L2_gnn_rms_weight': (1.0, 0.2),
     'L2_gnn_b2': (0.0, 0.1)}
    factors = {}
    for name, (base, spread) in spreads.items():
        noise = np.random.default_rng([zlib.crc32(name.encode()), seed]).standard_normal(out[name].shape)
        drawn = base * np.exp(spread * noise) if base else spread * noise
        out[name] = jnp.asarray(drawn.astype(out[name].dtype))
    for name, factor in factors.items():
        out[name] = (out[name] * factor).astype(out[name].dtype)
    return out
```

```python
import concourse.bass as bass
from concourse import mybir
from contextlib import ExitStack
import numpy as np

P = 128
G, N, D = 32, 512, 256
T = N // P
K = D // P
H1, DH1 = 8, 32
HID = 1024
KH = HID // P
H3, DH3 = 4, 64
LN_EPS, BN_EPS, RMS_EPS = 1e-5, 1e-5, 1e-6
MASKED = -1e30
SLOPE = 0.2
ROW_SHIFT = 3 * DH1
A_FILLS = 19
O_FILLS = 1 + H1
B_FILLS = 11


class Signal:

    def __init__(self, sem, per, unit=1):
        self.sem, self.per, self.unit = sem, per * unit, unit

    def upto(self, g, k):
        return self.sem, g.loop * (g.step * self.per) + (g.off * self.per + k * self.unit)


class Graph:

    def __init__(self, loop, off=0, step=1):
        self.loop, self.off, self.step = loop, off, step

    def plus(self, n):
        return Graph(self.loop, self.off + n, self.step)

    def half(self):
        if isinstance(self.loop, int):
            return Graph((self.loop * self.step + self.off) // 2)
        return Graph(self.loop, self.off // 2)

    def index(self):
        return self.loop * self.step + self.off

    def below(self, n):
        return isinstance(self.loop, int) and self.index() < n


def first(g):
    return g.below(1)


def merged(a, b):
    order = [((i + 0.5) / a, "a", i) for i in range(a)] + [((i + 0.5) / b, "b", i) for i in range(b)]
    return [(s, i) for _, s, i in sorted(order)]


def gnn_stack(nc, x, adjT, w0T, b0, bn_w, bn_b, res_w, wqT, wkT, wvT, woT, bo, eps, w1, b1, rms_w, w2, b2,
              w3, att, out):
    f32, bf16, f32r = mybir.dt.float32, mybir.dt.bfloat16, mybir.dt.float32r
    ALU, ACT, AX = mybir.AluOpType, mybir.ActivationFunctionType, mybir.AxisListType
    ctx = ExitStack()
    with ctx:
        def sb(name, *shape, dt=f32):
            return ctx.enter_context(nc.sbuf_tensor(name, list(shape), dt))

        def signal(name, per=1, unit=1):
            return Signal(ctx.enter_context(nc.semaphore(name)), per, unit)

        pre_bn = nc.dram_tensor("pre_bn", [G, N, D], f32, kind="Internal").ap()
        x_res = nc.dram_tensor("x_res", [G, N, D], f32, kind="Internal").ap()

        def nodes(t, g):
            return t[g.index()].rearrange("(t p) d -> p t d", p=P)

        ident = sb("ident", P, P)
        ident16 = sb("ident16", P, P, dt=bf16)
        ones = sb("ones", P, P)
        minus_half = sb("minus_half", P, D)
        sel3 = sb("sel3", H3, H3, P)
        w0_s, wq_s, wk_s, wv_s, wo_s, w3_s = (sb(n, P, K, D) for n in ("w0_s", "wq_s", "wk_s", "wv_s", "wo_s", "w3_s"))
        w1_s = sb("w1_s", P, K, HID)
        w2_s = sb("w2_s", P, KH, D)
        b0_s, bo_s, b2_s, bnw_s, bnb_s = (sb(n, P, D) for n in ("b0_s", "bo_s", "b2_s", "bnw_s", "bnb_s"))
        b1_s = sb("b1_s", P, KH)
        rms_s = sb("rms_s", P, KH)
        resw_s = sb("resw_s", P, 1)
        eps_s = sb("eps_s", P, 1)
        eps_ident = sb("eps_ident", P, P)
        half_rms = sb("half_rms", P, KH)
        att_s = sb("att_s", P, H3, 2 * DH3)
        att_w = sb("att_w", P, 2, K, H3)
        att_t = sb("att_t", P, H3, DH3)

        c_deg = sb("c_deg", P, 4, T)
        c_dis = sb("c_dis", P, 2, T)
        bn_scale = sb("bn_scale", P, D)
        bn_shift = sb("bn_shift", P, D)

        ln = {s: {n: sb(f"{s}_{n}", P, T, w) for n, w in (("st", 6), ("mv", 2), ("ve", 1), ("rs", 1), ("sh", 1))}
              for s in "cabd"}

        a_xr = sb("a_xr", P, T, D)
        a_o = sb("a_o", P, T, D)
        a_at = sb("a_at", P, T, N)
        a_x1 = sb("a_x1", P, T, D)
        a_h = sb("a_h", P, T, D)
        a_hT = sb("a_hT", P, K, N)
        q_parts = sb("q_parts", P, H1, N, dt=f32r)
        k_parts = sb("k_parts", P, H1, N, dt=f32r)
        v1 = sb("v1", P, T * H1, DH1 + 1)
        maskT = sb("maskT", P, T, N, dt=bf16)
        minus_max = sb("minus_max", P, T, H1)
        shiftT = sb("shiftT", H1, N, dt=f32r)
        pT = sb("pT", P, 2, T, N)
        rden1 = sb("rden1", P, 2, T, 1)
        x_mid = sb("x_mid", P, T, D)

        b_at = sb("b_at", P, T, N)
        edge = sb("edge", P, T, N, dt=bf16)
        b_xb2 = sb("b_xb2", P, T, D)
        b_h = sb("b_h", P, T, D)
        aggT = sb("aggT", P, K, N)
        hid = sb("hid", P, KH, N)
        hsq = sb("hsq", P, KH, N)
        ms = sb("ms", P, T)
        rrms = sb("rrms", P, T)
        diag = sb("diag", P, T, P)
        x3 = sb("x3", P, T, D)
        v3 = sb("v3", P, T * H3, DH3 + 1)
        top = sb("top", H3, 2)
        vcol = sb("vcol", P, 2, T, H3)
        rden3 = sb("rden3", P, 2, T, 1)

        a_xbo = a_x1
        att1, att1T = a_h, a_hT
        d_h, d_hT, att3 = b_h, aggT, b_xb2
        rows_of = lambda t: t[0:H3].rearrange("p a b -> p (a b)").rearrange("p (a b) -> p a b", a=2)
        vT, uT, zz = rows_of(b_h), rows_of(aggT), rows_of(aggT)
        z8 = diag[0:H3].rearrange("p a b -> p (a b)")
        x_out = x3
        parts = pT[:, :, :, :].rearrange("p a (s k) n -> p (a s) k n", k=K)
        q_high, q_low, k_high, k_low = (parts[:, i] for i in range(4))
        low = hsq[:, :, :].rearrange("p (a t) n -> p a t n", a=2)
        p3T = hid[:, :, :].rearrange("p (a t) n -> p a t n", a=2)

        def two(t, a, b):
            return t[:, a:b, :].rearrange("p (c a) (b d) -> p c (a b) d", c=2, d=D)

        c_at = pT
        c_x, c_xres = two(hid, 0, 4), two(hid, 4, 8)
        c_o, c_sq = two(hsq, 0, 4), two(hsq, 4, 8)
        c_h, c_hT, c_hs = a_h, a_hT, a_x1
        sum_o, sum_sq, bn_t = b_h, aggT[:, :, :].rearrange("p k (b d) -> p (k b) d", d=D), x3

        pair = [ctx.enter_context(nc.psum_tensor(f"pair{i}", [P, 2, N], f32)) for i in range(2)]
        obank = ctx.enter_context(nc.psum_tensor("obank", [P, N], f32))
        bank = [ctx.enter_context(nc.psum_tensor(f"bank{i}", [P, N], f32)) for i in range(3)]

        n_loads = 18
        weights_in = signal("weights_in", n_loads, 16)
        consts = signal("consts", 11)
        setup = signal("setup", 14)
        eps_done = signal("eps_done", 1)

        c_x_in = [signal(f"c_x_in{i}", 1, 16) for i in range(2)]
        c_at_in = [signal(f"c_at_in{i}", 1, 16) for i in range(2)]
        c_eye = signal("c_eye")
        c_deg_sum = signal("c_deg_sum")
        c_deg_in = signal("c_deg_in", 2)
        c_deg_ok = signal("c_deg_ok")
        c_pow = signal("c_pow")
        c_dis_ok = signal("c_dis_ok")
        c_hT_sum = signal("c_hT_sum")
        c_hT_ok = signal("c_hT_ok")
        c_lin = signal("c_lin")
        c_scaled = signal("c_scaled")
        c_hs_ok = signal("c_hs_ok")
        c_agg = signal("c_agg")
        c_o_ok = signal("c_o_ok")
        c_sq_ok = signal("c_sq_ok")
        c_xres_ok = signal("c_xres_ok")
        c_added = [signal(f"c_added{i}", 2) for i in range(2)]
        c_o_out = [signal(f"c_o_out{i}", 1, 16) for i in range(2)]
        c_xres_out = [signal(f"c_xres_out{i}", 1, 16) for i in range(2)]
        c_sums = signal("c_sums", 2)
        bn_steps = signal("bn_steps", 6)
        bn_pow = signal("bn_pow", 1)

        lns = {s: {n: signal(f"{s}_{n}_ok", 1 + (n == "mv")) for n in ("st", "mv", "ve", "rs", "sh", "h")} for s in "cabd"}

        a_x_in = signal("a_x_in", 2, 16)
        a_at_in = signal("a_at_in", 1, 16)
        a_x1_step = signal("a_x1_step", 3)
        a_xbo_ok = signal("a_xbo_ok")
        a_mask_ok = signal("a_mask_ok")
        a_high_ok = signal("a_high_ok", 2)
        a_qk_in = signal("a_qk_in", 24, 16)
        a_shift_in = signal("a_shift_in", H1, 16)
        a_filled = [signal(f"a_filled{i}", A_FILLS) for i in range(2)]
        a_copied = [signal(f"a_copied{i}", A_FILLS) for i in range(2)]
        o_filled = signal("o_filled", O_FILLS)
        o_copied = signal("o_copied", O_FILLS)
        a_rden = signal("a_rden", H1)

        b_at_in = signal("b_at_in", 1, 16)
        b_edge_ok = signal("b_edge_ok")
        b_eye = signal("b_eye")
        b_xb2_ok = signal("b_xb2_ok")
        b_filled = [signal(f"b_filled{i}", B_FILLS) for i in range(3)]
        b_copied = [signal(f"b_copied{i}", B_FILLS) for i in range(3)]
        b_rrms = signal("b_rrms")
        b_diag = signal("b_diag")
        b_norm = signal("b_norm", KH)
        b_tanh = signal("b_tanh", KH)
        b_act = signal("b_act", KH)
        b_top = signal("b_top", 2)
        b_z8 = signal("b_z8")
        b_zz = signal("b_zz")
        b_uT = signal("b_uT")
        b_low = signal("b_low", H3)
        b_max = signal("b_max", H3)
        b_p3 = signal("b_p3", H3)
        b_rden = signal("b_rden", H3)
        b_out = signal("b_out")
        b_stored = signal("b_stored", 1, 16)

        def a_unit(u):
            return u % 2, u // 2

        def b_unit(u):
            return u % 3, u // 3

        U_HT, U_Q, U_K, U_V, U_NAT, U_ST, U_OT, U_WO = 0, 1, 2, 3, 4, 20, 36, 37
        V_AGG, V_HID, V_MS, V_RB, V_OUT, V_HT, V_V3, V_EI, V_EJ, V_VT, V_HEAD = 0, 2, 10, 11, 12, 14, 16, 18, 19, 20, 21

        def second_pass(eng, a, b):
            def both_streams(g, before):
                for s, i in merged(len(a), len(b)):
                    if s == "a":
                        a[i](g)
                    else:
                        b[i](before)

            for f in a:
                f(Graph(0))
            both_streams(Graph(1), Graph(0))
            with eng.Fori(2, G) as g:
                both_streams(Graph(g), Graph(g, -1))
            for f in b:
                f(Graph(G - 1))

        def first_pass(eng, fore, mid, back):
            fore(Graph(0), 0)
            back(Graph(0), 0)
            for o in (1, 2):
                fore(Graph(o), o % 2)
                mid(Graph(o - 1), (o - 1) % 2)
                back(Graph(o), o % 2)
            with eng.Fori(1, G // 2 - 1) as i:
                for o in (1, 2):
                    fore(Graph(i, o, 2), o % 2)
                    mid(Graph(i, o - 1, 2), (o - 1) % 2)
                    back(Graph(i, o, 2), o % 2)
            fore(Graph(G - 1), 1)
            mid(Graph(G - 2), 0)
            back(Graph(G - 1), 1)
            mid(Graph(G - 1), 1)

        block = ctx.enter_context(nc.Block())

        @block.sync
        def _(sp):
            def bcast(v, n):
                return v.rearrange("(a n) -> a n", a=1).broadcast_to([P, n])

            loads = [(w, s[:, :, :]) for w, s in ((w0T, w0_s), (wqT, wq_s), (wkT, wk_s), (wvT, wv_s), (woT, wo_s), (w3, w3_s),
                                               (w1, w1_s), (w2, w2_s))]
            for w, s in loads:
                sp.dma_start(s, w.rearrange("(k p) n -> p k n", p=P)).then_inc(weights_in.sem, 16)
            for v, s in ((b0, b0_s), (bo, bo_s), (b2, b2_s), (bn_w, bnw_s), (bn_b, bnb_s)):
                sp.dma_start(s[:, :], bcast(v, D)).then_inc(weights_in.sem, 16)
            sp.dma_start(resw_s[:, :], bcast(res_w, 1)).then_inc(weights_in.sem, 16)
            sp.dma_start(eps_s[:, :], bcast(eps, 1)).then_inc(weights_in.sem, 16)
            sp.dma_start(b1_s[:, :], b1).then_inc(weights_in.sem, 16)
            sp.dma_start(rms_s[:, :], rms_w).then_inc(weights_in.sem, 16)
            sp.dma_start(att_s[:, :, :].rearrange("p h d -> p (h d)"), bcast(att, H3 * 2 * DH3)).then_inc(weights_in.sem, 16)

            def load(g, par):
                if not g.below(2):
                    sp.wait_ge(*c_agg.upto(g.plus(-1), 0))
                    sp.wait_ge(*c_xres_ok.upto(g.plus(-1), 0))
                sp.dma_start(c_x[:, par], nodes(x, g)).then_inc(c_x_in[par].sem, 16)
                sp.dma_start(c_at[:, par], nodes(adjT, g)).then_inc(c_at_in[par].sem, 16)

            def store_res(g, par):
                sp.wait_ge(*c_xres_ok.upto(g, 1))
                sp.dma_start(nodes(x_res, g), c_xres[:, par]).then_inc(c_xres_out[par].sem, 16)

            def store_o(g, par):
                sp.wait_ge(*c_o_ok.upto(g, 1))
                sp.dma_start(nodes(pre_bn, g), c_o[:, par]).then_inc(c_o_out[par].sem, 16)

            load(Graph(0), 0)
            load(Graph(1), 1)
            store_res(Graph(0), 0)
            with sp.Fori(0, G // 2 - 1) as i:
                for o in (1, 2):
                    store_o(Graph(i, o - 1, 2), (o - 1) % 2)
                    load(Graph(i, o + 1, 2), (o + 1) % 2)
                    store_res(Graph(i, o, 2), o % 2)
            store_res(Graph(G - 1), 1)
            store_o(Graph(G - 2), 0)
            store_o(Graph(G - 1), 1)
            for par in range(2):
                sp.wait_ge(c_o_out[par].sem, G // 2 * 16)
                sp.wait_ge(c_xres_out[par].sem, G // 2 * 16)

            def load_a(g):
                if not first(g):
                    sp.wait_ge(*a_x1_step.upto(g, 0))
                sp.dma_start(a_o[:, :, :], nodes(pre_bn, g)).then_inc(a_x_in.sem, 16)
                sp.dma_start(a_xr[:, :, :], nodes(x_res, g)).then_inc(a_x_in.sem, 16)
                if not first(g):
                    sp.wait_ge(*a_mask_ok.upto(g, 0))
                sp.dma_start(a_at[:, :, :], nodes(adjT, g)).then_inc(a_at_in.sem, 16)

            def load_b(g):
                if not first(g):
                    sp.wait_ge(*b_filled[1].upto(g.plus(-1), 1))
                sp.dma_start(b_at[:, :, :], nodes(adjT, g)).then_inc(b_at_in.sem, 16)

            def store(g):
                sp.wait_ge(*b_out.upto(g, 1))
                sp.dma_start(nodes(out, g), x_out[:, :, :]).then_inc(b_stored.sem, 16)

            def sort_parts(g):
                r = DH1
                for u, dst, srcs in ((U_Q, q_parts, (q_high, q_high, q_low)), (U_K, k_parts, (k_high, k_low, k_high))):
                    p, n = a_unit(u)
                    sp.wait_ge(*a_copied[p].upto(g, n + 1))
                    if u == U_Q and not first(g):
                        for i in range(2):
                            sp.wait_ge(*a_filled[i].upto(g, 0))
                    for c, src in enumerate(srcs):
                        for i in range(P // r):
                            sp.dma_start(dst[c * r:(c + 1) * r, i::P // r, :].bitcast(f32),
                                         src[i * r:(i + 1) * r]).then_inc(a_qk_in.sem, 16)

            def put_shift(g):
                sp.wait_ge(*o_copied.upto(g, 1))
                for h in range(H1):
                    sp.dma_start(q_parts[ROW_SHIFT:ROW_SHIFT + 1, h, :].bitcast(f32),
                                 shiftT[h:h + 1, :].bitcast(f32)).then_inc(a_shift_in.sem, 16)

            load_a(Graph(0))
            load_b(Graph(0))
            sort_parts(Graph(0))
            load_a(Graph(1))
            put_shift(Graph(0))
            with sp.Fori(1, G - 1) as g:
                load_b(Graph(g))
                sort_parts(Graph(g))
                load_a(Graph(g, 1))
                put_shift(Graph(g))
                store(Graph(g, -1))
            load_b(Graph(G - 1))
            sort_parts(Graph(G - 1))
            put_shift(Graph(G - 1))
            store(Graph(G - 2))
            store(Graph(G - 1))
            sp.wait_ge(b_stored.sem, G * 16)

        @block.gpsimd
        def _(pool):
            nc.gpsimd.memset(ident[:, :], 0.0).then_inc(consts.sem, 1)
            nc.gpsimd.memset(ones[:, :], 1.0).then_inc(consts.sem, 1)
            nc.gpsimd.memset(minus_half[:, :], -0.5).then_inc(consts.sem, 1)
            nc.gpsimd.memset(sel3[:, :, :], 0.0).then_inc(consts.sem, 1)
            nc.gpsimd.memset(sum_o[:, :, :], 0.0).then_inc(consts.sem, 1)
            nc.gpsimd.memset(sum_sq[:, :, :], 0.0).then_inc(consts.sem, 1)
            nc.gpsimd.memset(v1[:, :, DH1:DH1 + 1], 1.0).then_inc(consts.sem, 1)
            nc.gpsimd.memset(v3[:, :, DH3:DH3 + 1], 1.0).then_inc(consts.sem, 1)
            pool.wait_ge(consts.sem, 8)
            nc.gpsimd.memset(k_parts[ROW_SHIFT:ROW_SHIFT + 1, :, :].bitcast(f32), 1.0).then_inc(consts.sem, 1)
            pool.wait_ge(consts.sem, 9)
            nc.gpsimd.affine_select(out=sel3[:, :, :], in_=sel3[:, :, :], compare_op=ALU.not_equal, fill=1.0, base=0,
                                    pattern=[[-1, H3], [0, P]], channel_multiplier=1).then_inc(consts.sem, 1)
            nc.gpsimd.affine_select(out=ident[:, :], in_=ident[:, :], compare_op=ALU.not_equal, fill=1.0, base=0,
                                    pattern=[[-1, P]], channel_multiplier=1).then_inc(consts.sem, 1)
            pool.wait_ge(consts.sem, 11)

            def power(out_ap, in_ap, n):
                return nc.gpsimd.tensor_tensor(out_ap, in_ap, minus_half[:, 0:n], ALU.pow)

            def rstd(s, g):
                pool.wait_ge(*lns[s]["ve"].upto(g, 1))
                power(ln[s]["rs"][:, :, 0], ln[s]["ve"][:, :, 0], T).then_inc(lns[s]["rs"].sem, 1)

            def fore(g, par):
                pool.wait_ge(*c_deg_ok.upto(g, 1))
                power(c_deg[:, 3, :], c_deg[:, 1, :], T).then_inc(c_pow.sem, 1)
                rstd("c", g)

            def mid(g, par):
                pool.wait_ge(*c_o_ok.upto(g, 1))
                if not first(g):
                    pool.wait_ge(*c_added[1 - par].upto(g.half(), 2 * par))
                nc.gpsimd.tensor_tensor(sum_o[:, :, :], sum_o[:, :, :], c_o[:, par], ALU.add).then_inc(c_added[par].sem, 1)
                pool.wait_ge(*c_sq_ok.upto(g, 1))
                nc.gpsimd.tensor_tensor(sum_sq[:, :, :], sum_sq[:, :, :], c_sq[:, par], ALU.add).then_inc(c_added[par].sem, 1)

            first_pass(pool, fore, mid, lambda g, par: None)
            pool.wait_ge(bn_steps.sem, 4)
            nc.gpsimd.tensor_tensor(bn_t[:, 3, :], bn_t[:, 2, :], minus_half[:, :], ALU.pow).then_inc(bn_pow.sem, 1)

            def a_ln(g):
                rstd("a", g)
                pool.wait_ge(*lns["a"]["h"].upto(g, 1))
                nc.gpsimd.tensor_tensor(a_xbo[:, :, :], a_x1[:, :, :], bo_s[:, None, :].broadcast_to([P, T, D]),
                                        ALU.add).then_inc(a_xbo_ok.sem, 1)

            def b_ln(g):
                rstd("b", g)
                pool.wait_ge(*a_copied[1].upto(g, A_FILLS))
                nc.gpsimd.tensor_tensor(b_xb2[:, :, :], x_mid[:, :, :], b2_s[:, None, :].broadcast_to([P, T, D]),
                                        ALU.add).then_inc(b_xb2_ok.sem, 1)

            def b_ms(g):
                pool.wait_ge(*b_copied[V_MS % 3].upto(g, V_MS // 3 + 1))
                power(rrms[:, :], ms[:, :], T).then_inc(b_rrms.sem, 1)

            none = lambda g: None
            a = [a_ln] + [none] * 21
            b = [b_ln, none] + [none] * 4 + [b_ms, none, none, none, lambda g: rstd("d", g)] + [none] * 9
            second_pass(pool, a, b)

        @block.scalar
        def _(act):
            def normalise(s, g, dst, src, wait=None):
                act.wait_ge(*lns[s]["sh"].upto(g, 1))
                for t in range(T):
                    i = nc.scalar.activation(dst[:, t, :], src[:, t, :], ACT.Relu, bias=ln[s]["sh"][:, t, :],
                                             scale=ln[s]["rs"][:, t, :])
                i.then_inc(lns[s]["h"].sem, 1)

            def fore(g, par):
                if not first(g):
                    act.wait_ge(*c_xres_ok.upto(g, 0))
                normalise("c", g, c_h, c_x[:, par, :, :])
                act.wait_ge(*c_hT_sum.upto(g, 1))
                nc.scalar.activation(c_hT[:, :, :], pair[0][:, :, :], ACT.Copy).then_inc(c_hT_ok.sem, 1)

            def mid(g, par):
                act.wait_ge(*c_agg.upto(g, 1))
                if not g.below(2):
                    act.wait_ge(*c_o_out[par].upto(g.half(), 0))
                    act.wait_ge(*c_added[par].upto(g.half(), 0))
                for t in range(T):
                    src = (obank if t < 2 else bank[2])[:, (t % 2) * D:(t % 2 + 1) * D]
                    i = nc.scalar.activation(c_o[:, par, t, :], src, ACT.Copy, scale=c_dis[:, par, t:t + 1])
                i.then_inc(c_o_ok.sem, 1)
                act.wait_ge(*c_o_ok.upto(g, 1))
                nc.scalar.activation(c_sq[:, par], c_o[:, par], ACT.Square).then_inc(c_sq_ok.sem, 1)

            def back(g, par):
                act.wait_ge(*c_lin.upto(g, 1))
                act.wait_ge(*c_dis_ok.upto(g, 1))
                for t in range(T):
                    i = nc.scalar.activation(c_hs[:, t, :], pair[1][:, t // 2, (t % 2) * D:(t % 2 + 1) * D], ACT.Copy,
                                             scale=c_dis[:, par, t:t + 1])
                i.then_inc(c_scaled.sem, 1)

            first_pass(act, fore, mid, back)

            def a_take(g, u, dst, func=ACT.Copy, **more):
                p, n = a_unit(u)
                act.wait_ge(*a_filled[p].upto(g, n + 1))
                nc.scalar.activation(dst, pair[p][:, :, :], func, **more).then_inc(a_copied[p].sem, 1)

            def a_qkv(g):
                for u, high in ((U_Q, q_high), (U_K, k_high)):
                    p, n = a_unit(u)
                    act.wait_ge(*a_filled[p].upto(g, n + 1))
                    nc.scalar.activation(high.bitcast(f32r), pair[p][:, :, :], ACT.Copy).then_inc(a_high_ok.sem, 1)
                p, n = a_unit(U_V)
                act.wait_ge(*a_filled[p].upto(g, n + 1))
                nc.scalar.activation(v1[:, :, 0:DH1], pair[p][:, :, :].rearrange("p a (h d) -> p (a h) d", d=DH1),
                                     ACT.Copy).then_inc(a_copied[p].sem, 1)

            def a_shift(g):
                act.wait_ge(*o_filled.upto(g, 1))
                nc.scalar.activation(shiftT[:, :], obank[0:H1, :], ACT.Copy).then_inc(o_copied.sem, 1)

            def a_exp(h):
                def f(g):
                    if h or not first(g):
                        act.wait_ge(*o_filled.upto(g, h))
                    for q in range(2):
                        a_take(g, U_ST + 2 * h + q, pT[:, h % 2, 2 * q:2 * q + 2, :], ACT.Exp, scale=DH1 ** -0.5)
                return f

            def b_take(g, u, dst, func=ACT.Copy, src=None, **more):
                p, n = b_unit(u)
                act.wait_ge(*b_filled[p].upto(g, n + 1))
                nc.scalar.activation(dst, bank[p][:, :] if src is None else src, func, **more).then_inc(b_copied[p].sem, 1)

            def b_hid(i):
                def f(g):
                    for t in (2 * i, 2 * i + 1):
                        p, n = b_unit(V_HID + t)
                        act.wait_ge(*b_filled[p].upto(g, n + 1))
                        nc.scalar.activation(hid[:, t, :], bank[p][:, :], ACT.Identity, bias=b1_s[:, t:t + 1])
                        nc.scalar.activation(hsq[:, t, :], bank[p][:, :], ACT.Square,
                                             bias=b1_s[:, t:t + 1]).then_inc(b_copied[p].sem, 1)
                return f

            def b_tanhs(g):
                for t in range(KH):
                    act.wait_ge(*b_norm.upto(g, t + 1))
                    nc.scalar.activation(hsq[:, t, :], hid[:, t, :], ACT.Tanh,
                                         scale=half_rms[:, t:t + 1]).then_inc(b_tanh.sem, 1)

            def b_v3(g):
                for i in range(2):
                    b_take(g, V_V3 + i, v3[:, 2 * H3 * i:2 * H3 * (i + 1), 0:DH3],
                           src=bank[(V_V3 + i) % 3][:, :].rearrange("p (h d) -> p h d", d=DH3))

            def b_exps(g):
                act.wait_ge(*b_top.upto(g, 2))
                nc.scalar.activation(vT[:, 0, :], bank[V_EJ % 3][0:H3, :], ACT.Exp, bias=top[:, 0:1])
                nc.scalar.activation(vT[:, 1, :], bank[V_EJ % 3][0:H3, :], ACT.Exp, bias=top[:, 1:2],
                                     scale=SLOPE).then_inc(b_copied[V_EJ % 3].sem, 1)
                act.wait_ge(*b_zz.upto(g, 1))
                nc.scalar.activation(uT[:, :, :], zz[:, :, :], ACT.Exp).then_inc(b_uT.sem, 1)

            def b_low3(h):
                def f(g):
                    p, n = b_unit(V_HEAD + 3 * h + 1)
                    act.wait_ge(*b_filled[p].upto(g, n + 1))
                    act.wait_ge(*b_copied[V_VT % 3].upto(g, V_VT // 3 + 1))
                    if h >= 2:
                        act.wait_ge(*b_max.upto(g, h - 1))
                    for k in range(T):
                        i = nc.scalar.activation(low[:, h % 2, k, :], bank[p][:, :], ACT.Copy, scale=vcol[:, 1, k, h:h + 1])
                    i.then_inc(b_copied[p].sem, 1)
                return f

            none = lambda g: None
            a = [lambda g: normalise("a", g, a_h, a_x1), lambda g: a_take(g, U_HT, a_hT[:, :, :]), a_qkv] + [none] * 8 \
                + [a_shift] + [a_exp(h) for h in range(H1)] + [lambda g: a_take(g, U_OT, att1T[:, :, :]), none]
            b = [lambda g: normalise("b", g, b_h, x_mid),
                 lambda g: [b_take(g, V_AGG + j, aggT[:, j, :]) for j in range(K)]] + [b_hid(i) for i in range(4)] \
                + [none, none, b_tanhs, none, lambda g: normalise("d", g, d_h, x3),
                   lambda g: [b_take(g, V_HT + j, d_hT[:, j, :]) for j in range(K)], b_v3, b_exps, none] \
                + [b_low3(h) for h in range(H3)] + [none]
            second_pass(act, a, b)

        @block.vector
        def _(dve):
            dve.wait_ge(weights_in.sem, n_loads * 16)
            dve.wait_ge(consts.sem, 11)
            nc.vector.tensor_copy(ident16[:, :], ident[:, :]).then_inc(setup.sem, 1)
            nc.vector.tensor_scalar(eps_ident[:, :], ident[:, :], eps_s[:, 0:1], None, ALU.mult).then_inc(setup.sem, 1)
            nc.vector.tensor_scalar(half_rms[:, :], rms_s[:, :], 0.5, None, ALU.mult).then_inc(setup.sem, 1)
            dve.wait_ge(setup.sem, 3)
            for t in range(KH):
                nc.vector.tensor_scalar(w2_s[:, t, :], w2_s[:, t, :], half_rms[:, t:t + 1], None, ALU.mult)
            n = 3
            for s in range(2):
                for k in range(K):
                    if n > 3:
                        dve.wait_ge(setup.sem, n)
                    nc.vector.tensor_tensor(att_t[:, :, :], w3_s[:, k, :].rearrange("p (h d) -> p h d", d=DH3),
                                            att_s[:, :, s * DH3:(s + 1) * DH3], ALU.mult).then_inc(setup.sem, 1)
                    dve.wait_ge(setup.sem, n + 1)
                    nc.vector.tensor_reduce(att_w[:, s, k, :], att_t[:, :, :], AX.X, ALU.add).then_inc(setup.sem, 1)
                    n += 2

            def stats(s, g, src):
                for t in range(T):
                    i = nc.vector.bn_stats(out=ln[s]["st"][:, t, :], in_=src[:, t, :])
                i.then_inc(lns[s]["st"].sem, 1)
                dve.wait_ge(*lns[s]["st"].upto(g, 1))
                st, mv, q4 = ln[s]["st"], ln[s]["mv"], ln[s]["rs"]
                nc.vector.tensor_tensor(mv[:, :, 0], st[:, :, 1], st[:, :, 4], ALU.add)
                nc.vector.scalar_tensor_tensor(out=mv[:, :, 1], in0=st[:, :, 2], scalar=D * LN_EPS, in1=st[:, :, 5],
                                               op0=ALU.add, op1=ALU.add)
                nc.vector.tensor_tensor(ln[s]["sh"][:, :, 0], st[:, :, 1], st[:, :, 4],
                                        ALU.subtract).then_inc(lns[s]["mv"].sem, 1)
                dve.wait_ge(*lns[s]["mv"].upto(g, 1))
                nc.vector.scalar_tensor_tensor(out=q4[:, :, 0], in0=ln[s]["sh"][:, :, 0], scalar=0.25,
                                               in1=ln[s]["sh"][:, :, 0], op0=ALU.mult,
                                               op1=ALU.mult).then_inc(lns[s]["mv"].sem, 1)
                dve.wait_ge(*lns[s]["mv"].upto(g, 2))
                nc.vector.scalar_tensor_tensor(out=ln[s]["ve"][:, :, 0], in0=mv[:, :, 1], scalar=1.0 / D,
                                               in1=q4[:, :, 0], op0=ALU.mult, op1=ALU.add).then_inc(lns[s]["ve"].sem, 1)

            def shift(s, g):
                dve.wait_ge(*lns[s]["rs"].upto(g, 1))
                nc.vector.scalar_tensor_tensor(out=ln[s]["sh"][:, :, 0], in0=ln[s]["mv"][:, :, 0], scalar=-0.5,
                                               in1=ln[s]["rs"][:, :, 0], op0=ALU.mult,
                                               op1=ALU.mult).then_inc(lns[s]["sh"].sem, 1)

            def fore(g, par):
                dve.wait_ge(*c_at_in[par].upto(g.half(), 1))
                for t in range(T):
                    d = c_at[:, par, t, t * P:(t + 1) * P]
                    i = nc.vector.tensor_tensor(d, d, ident[:, :], ALU.add)
                i.then_inc(c_eye.sem, 1)
                dve.wait_ge(*c_x_in[par].upto(g.half(), 1))
                stats("c", g, c_x[:, par, :, :])
                dve.wait_ge(*c_deg_sum.upto(g, 1))
                nc.vector.tensor_scalar(c_deg[:, 0, :], bank[0][:, 0:T], 0.0, None, ALU.is_equal).then_inc(c_deg_in.sem, 1)
                dve.wait_ge(*c_deg_in.upto(g, 1))
                nc.vector.tensor_scalar(c_deg[:, 2, :], c_deg[:, 0, :], -1.0, 1.0, ALU.mult, ALU.add).then_inc(c_deg_in.sem, 1)
                nc.vector.tensor_tensor(c_deg[:, 1, :], bank[0][:, 0:T], c_deg[:, 0, :], ALU.add).then_inc(c_deg_ok.sem, 1)
                shift("c", g)
                dve.wait_ge(*c_pow.upto(g, 1))
                dve.wait_ge(*c_deg_in.upto(g, 2))
                nc.vector.tensor_tensor(c_dis[:, par, :], c_deg[:, 3, :], c_deg[:, 2, :], ALU.mult).then_inc(c_dis_ok.sem, 1)
                dve.wait_ge(*lns["c"]["h"].upto(g, 1))
                if not g.below(2):
                    dve.wait_ge(*c_xres_out[par].upto(g.half(), 0))
                nc.vector.scalar_tensor_tensor(out=c_xres[:, par], in0=c_h[:, :, :], scalar=resw_s[:, 0:1],
                                               in1=c_x[:, par], op0=ALU.mult, op1=ALU.add).then_inc(c_xres_ok.sem, 1)

            def back(g, par):
                dve.wait_ge(*c_scaled.upto(g, 1))
                dve.wait_ge(*c_dis_ok.upto(g, 1))
                for t in range(T):
                    i = nc.vector.scalar_tensor_tensor(out=c_hs[:, t, :], in0=b0_s[:, :], scalar=c_dis[:, par, t:t + 1],
                                                       in1=c_hs[:, t, :], op0=ALU.mult, op1=ALU.add)
                i.then_inc(c_hs_ok.sem, 1)

            first_pass(dve, fore, lambda g, par: None, back)

            dve.wait_ge(c_sums.sem, 2)
            rows = 1.0 / (G * N)
            mean, var = bn_t[:, 0, :], bn_t[:, 2, :]
            nc.vector.tensor_scalar(mean, obank[:, 0:D], rows, None, ALU.mult).then_inc(bn_steps.sem, 1)
            dve.wait_ge(bn_steps.sem, 1)
            nc.vector.tensor_tensor(bn_t[:, 1, :], mean, mean, ALU.mult).then_inc(bn_steps.sem, 1)
            dve.wait_ge(bn_steps.sem, 2)
            nc.vector.scalar_tensor_tensor(out=var, in0=obank[:, D:2 * D], scalar=rows, in1=bn_t[:, 1, :], op0=ALU.mult,
                                           op1=ALU.subtract).then_inc(bn_steps.sem, 1)
            dve.wait_ge(bn_steps.sem, 3)
            nc.vector.tensor_scalar(var, var, 0.0, BN_EPS, ALU.max, ALU.add).then_inc(bn_steps.sem, 1)
            dve.wait_ge(bn_pow.sem, 1)
            nc.vector.tensor_tensor(bn_scale[:, :], bn_t[:, 3, :], bnw_s[:, :], ALU.mult).then_inc(bn_steps.sem, 1)
            dve.wait_ge(bn_steps.sem, 5)
            nc.vector.tensor_tensor(bn_t[:, 1, :], mean, bn_scale[:, :], ALU.mult).then_inc(bn_steps.sem, 1)
            dve.wait_ge(bn_steps.sem, 6)
            nc.vector.tensor_tensor(bn_shift[:, :], bnb_s[:, :], bn_t[:, 1, :], ALU.subtract).then_inc(bn_steps.sem, 1)
            dve.wait_ge(bn_steps.sem, 7)

            def a_ln(g):
                wide = [P, T, D]
                dve.wait_ge(*a_x_in.upto(g, 2))
                if not first(g):
                    dve.wait_ge(*lns["a"]["h"].upto(g, 0))
                    dve.wait_ge(*a_xbo_ok.upto(g, 0))
                nc.vector.tensor_tensor(a_o[:, :, :], a_o[:, :, :], bn_scale[:, None, :].broadcast_to(wide),
                                        ALU.mult).then_inc(a_x1_step.sem, 1)
                dve.wait_ge(*a_x1_step.upto(g, 1))
                nc.vector.tensor_tensor(a_o[:, :, :], a_o[:, :, :], bn_shift[:, None, :].broadcast_to(wide),
                                        ALU.add).then_inc(a_x1_step.sem, 1)
                dve.wait_ge(*a_x1_step.upto(g, 2))
                nc.vector.scalar_tensor_tensor(out=a_x1[:, :, :], in0=a_o[:, :, :], scalar=0.0, in1=a_xr[:, :, :],
                                               op0=ALU.max, op1=ALU.add).then_inc(a_x1_step.sem, 1)
                dve.wait_ge(*a_x1_step.upto(g, 3))
                stats("a", g, a_x1)
                dve.wait_ge(*a_at_in.upto(g, 1))
                nc.vector.tensor_scalar(maskT[:, :, :], a_at[:, :, :], 0.0, MASKED, ALU.is_equal,
                                        ALU.mult).then_inc(a_mask_ok.sem, 1)
                shift("a", g)

            def a_split(g):
                for i, (u, high, low_part) in enumerate(((U_Q, q_high, q_low), (U_K, k_high, k_low))):
                    p, n = a_unit(u)
                    dve.wait_ge(*a_high_ok.upto(g, i + 1))
                    nc.vector.tensor_tensor(low_part.bitcast(f32r), pair[p][:, :, :], high,
                                            ALU.subtract).then_inc(a_copied[p].sem, 1)

            def a_max(h):
                def f(g):
                    for q in range(2):
                        p, n = a_unit(U_NAT + 2 * h + q)
                        dve.wait_ge(*a_filled[p].upto(g, n + 1))
                        nc.vector.tensor_reduce(minus_max[:, 2 * q:2 * q + 2, h], pair[p][:, :, :], AX.X, ALU.max,
                                                negate=True).then_inc(a_copied[p].sem, 1)
                return f

            def a_head(h):
                def f(g):
                    dve.wait_ge(*o_filled.upto(g, 2 + h))
                    o = obank[:, 0:T * (DH1 + 1)].rearrange("p (t d) -> p t d", d=DH1 + 1)
                    nc.vector.reciprocal(rden1[:, h % 2], o[:, :, DH1:DH1 + 1]).then_inc(a_rden.sem, 1)
                    dve.wait_ge(*a_rden.upto(g, h + 1))
                    nc.vector.tensor_tensor(att1[:, :, h * DH1:(h + 1) * DH1], o[:, :, 0:DH1],
                                            rden1[:, h % 2].broadcast_to([P, T, DH1]), ALU.mult).then_inc(o_copied.sem, 1)
                return f

            def a_wo(g):
                p, n = a_unit(U_WO)
                dve.wait_ge(*a_filled[p].upto(g, n + 1))
                dve.wait_ge(*a_xbo_ok.upto(g, 1))
                if not first(g):
                    dve.wait_ge(*lns["b"]["h"].upto(g, 0))
                    dve.wait_ge(*b_xb2_ok.upto(g, 0))
                nc.vector.tensor_tensor(x_mid[:, :, :], pair[p][:, :, :].rearrange("p a (b d) -> p (a b) d", d=D),
                                        a_xbo[:, :, :], ALU.add).then_inc(a_copied[p].sem, 1)

            def b_ln(g):
                dve.wait_ge(*a_copied[1].upto(g, A_FILLS))
                stats("b", g, x_mid)
                dve.wait_ge(*b_at_in.upto(g, 1))
                nc.vector.tensor_scalar(edge[:, :, :], b_at[:, :, :], 0.0, None, ALU.is_gt).then_inc(b_edge_ok.sem, 1)
                dve.wait_ge(*b_edge_ok.upto(g, 1))
                for t in range(T):
                    d = b_at[:, t, t * P:(t + 1) * P]
                    i = nc.vector.tensor_tensor(d, d, eps_ident[:, :], ALU.add)
                i.then_inc(b_eye.sem, 1)
                shift("b", g)

            def b_ms(g):
                p, n = b_unit(V_MS)
                dve.wait_ge(*b_filled[p].upto(g, n + 1))
                nc.vector.tensor_scalar(ms[:, :], bank[p][:, 0:T], 1.0 / HID, RMS_EPS, ALU.mult,
                                        ALU.add).then_inc(b_copied[p].sem, 1)

            def b_diags(g):
                dve.wait_ge(*b_rrms.upto(g, 1))
                for t in range(T):
                    i = nc.vector.tensor_scalar(diag[:, t, :], ident[:, :], rrms[:, t:t + 1], None, ALU.mult)
                i.then_inc(b_diag.sem, 1)

            def b_silu(g):
                p, n = b_unit(V_RB)
                dve.wait_ge(*b_filled[p].upto(g, n + 1))
                for t in range(KH):
                    nc.vector.tensor_tensor(hid[:, t, :], hid[:, t, :], bank[p][:, :], ALU.mult).then_inc(b_norm.sem, 1)
                for t in range(KH):
                    dve.wait_ge(*b_tanh.upto(g, t + 1))
                    i = nc.vector.scalar_tensor_tensor(out=hid[:, t, :], in0=hsq[:, t, :], scalar=1.0, in1=hid[:, t, :],
                                                       op0=ALU.add, op1=ALU.mult)
                    i.then_inc(b_act.sem, 1) if t < KH - 1 else i.then_inc(b_copied[p].sem, 1)

            def b_x3(g):
                dve.wait_ge(*b_xb2_ok.upto(g, 1))
                if not first(g):
                    dve.wait_ge(*b_stored.upto(g, 0))
                for q in range(2):
                    p, n = b_unit(V_OUT + q)
                    dve.wait_ge(*b_filled[p].upto(g, n + 1))
                    nc.vector.tensor_tensor(x3[:, 2 * q:2 * q + 2, :], bank[p][:, :].rearrange("p (b d) -> p b d", d=D),
                                            b_xb2[:, 2 * q:2 * q + 2, :], ALU.add).then_inc(b_copied[p].sem, 1)

            def d_ln(g):
                for q in range(2):
                    p, n = b_unit(V_OUT + q)
                    dve.wait_ge(*b_copied[p].upto(g, n + 1))
                stats("d", g, x3)
                shift("d", g)

            def b_factors(g):
                pi, ni = b_unit(V_EI)
                pj, nj = b_unit(V_EJ)
                dve.wait_ge(*b_filled[pj].upto(g, nj + 1))
                nc.vector.tensor_reduce(top[:, 0:1], bank[pj][0:H3, :], AX.X, ALU.max, negate=True).then_inc(b_top.sem, 1)
                dve.wait_ge(*b_top.upto(g, 1))
                nc.vector.tensor_scalar(top[:, 1:2], top[:, 0:1], SLOPE, None, ALU.mult).then_inc(b_top.sem, 1)
                nc.vector.tensor_scalar(z8[:, :], bank[pi][0:H3, :], top[:, 0:1], 1.0 - SLOPE, ALU.subtract,
                                        ALU.mult).then_inc(b_copied[pi].sem, 1)
                dve.wait_ge(*b_copied[pi].upto(g, ni + 1))
                nc.vector.tensor_scalar(zz[:, 0, :], z8[:, :], 0.0, None, ALU.min)
                nc.vector.tensor_scalar(zz[:, 1, :], z8[:, :], -1.0, 0.0, ALU.mult, ALU.min).then_inc(b_zz.sem, 1)

            def b_vcol(g):
                p, n = b_unit(V_VT)
                dve.wait_ge(*b_filled[p].upto(g, n + 1))
                nc.vector.tensor_copy(vcol[:, :, :, :].rearrange("p s t h -> p (s t h)"),
                                      bank[p][:, 0:2 * T * H3]).then_inc(b_copied[p].sem, 1)

            def b_prob(h):
                def f(g):
                    p, n = b_unit(V_HEAD + 3 * h)
                    pl, nl = b_unit(V_HEAD + 3 * h + 1)
                    dve.wait_ge(*b_filled[p].upto(g, n + 1))
                    dve.wait_ge(*b_copied[pl].upto(g, nl + 1))
                    dve.wait_ge(*b_copied[V_VT % 3].upto(g, V_VT // 3 + 1))
                    for k in range(T):
                        i = nc.vector.scalar_tensor_tensor(out=low[:, h % 2, k, :], in0=bank[p][:, :],
                                                           scalar=vcol[:, 0, k, h:h + 1], in1=low[:, h % 2, k, :],
                                                           op0=ALU.mult, op1=ALU.max)
                        if k == T - 1:
                            i.then_inc(b_copied[p].sem, 1)
                    dve.wait_ge(*b_copied[p].upto(g, n + 1))
                    if h >= 2:
                        po, no = b_unit(V_HEAD + 3 * (h - 2) + 2)
                        dve.wait_ge(*b_filled[po].upto(g, no + 1))
                    nc.vector.tensor_tensor(p3T[:, h % 2], low[:, h % 2], edge[:, :, :], ALU.mult).then_inc(b_max.sem, 1)
                return f

            def b_head(h):
                def f(g):
                    p, n = b_unit(V_HEAD + 3 * h + 2)
                    dve.wait_ge(*b_filled[p].upto(g, n + 1))
                    o = bank[p][:, 0:T * (DH3 + 1)].rearrange("p (t d) -> p t d", d=DH3 + 1)
                    nc.vector.reciprocal(rden3[:, h % 2], o[:, :, DH3:DH3 + 1]).then_inc(b_rden.sem, 1)
                    dve.wait_ge(*b_rden.upto(g, h + 1))
                    nc.vector.tensor_tensor(att3[:, :, h * DH3:(h + 1) * DH3], o[:, :, 0:DH3],
                                            rden3[:, h % 2].broadcast_to([P, T, DH3]), ALU.mult).then_inc(b_copied[p].sem, 1)
                return f

            def b_final(g):
                b_head(H3 - 1)(g)
                dve.wait_ge(*b_copied[2].upto(g, B_FILLS))
                nc.vector.tensor_tensor(x_out[:, :, :], att3[:, :, :], x3[:, :, :], ALU.add).then_inc(b_out.sem, 1)

            def both(*fs):
                return lambda g: [f(g) for f in fs]

            none = lambda g: None
            a = [a_ln, none, a_split] + [a_max(h) for h in range(H1)] + [none, none] + [a_head(h) for h in range(H1)] + [a_wo]
            b = [b_ln, none] + [none] * 4 + [b_ms, b_diags, b_silu, b_x3, d_ln, none, none, b_factors, b_vcol] \
                + [b_prob(0)] + [both(b_prob(h), b_head(h - 1)) for h in range(1, H3)] + [b_final]
            second_pass(dve, a, b)

        @block.tensor
        def _(pe):
            pe.wait_ge(weights_in.sem, n_loads * 16)
            pe.wait_ge(setup.sem, 11)

            def flip(dst, src, k):
                for t in range(T):
                    i = nc.tensor.transpose(dst[:, t * P:(t + 1) * P], src[:, t, k * P:(k + 1) * P], ident[:, :])
                return i

            def fore(g, par):
                pe.wait_ge(*c_eye.upto(g, 1))
                if not first(g):
                    pe.wait_ge(*c_deg_ok.upto(g, 0))
                for t in range(T):
                    for k in range(T):
                        i = nc.tensor.matmul(bank[0][:, t:t + 1], c_at[:, par, k, t * P:(t + 1) * P], ones[:, 0:1],
                                             start=k == 0, stop=k == T - 1)
                i.then_inc(c_deg_sum.sem, 1)
                pe.wait_ge(*lns["c"]["h"].upto(g, 1))
                if not first(g):
                    pe.wait_ge(*c_hT_ok.upto(g, 0))
                for k in range(K):
                    i = flip(pair[0][:, k, :], c_h, k)
                i.then_inc(c_hT_sum.sem, 1)

            def mid(g, par):
                pe.wait_ge(*c_hs_ok.upto(g, 1))
                if not first(g):
                    pe.wait_ge(*c_o_ok.upto(g, 0))
                for t in range(T):
                    dst = (obank if t < 2 else bank[2])[:, (t % 2) * D:(t % 2 + 1) * D]
                    for k in range(T):
                        i = nc.tensor.matmul(dst, c_at[:, par, k, t * P:(t + 1) * P], c_hs[:, k, :],
                                             start=k == 0, stop=k == T - 1)
                i.then_inc(c_agg.sem, 1)

            def back(g, par):
                pe.wait_ge(*c_hT_ok.upto(g, 1))
                if not first(g):
                    pe.wait_ge(*c_scaled.upto(g, 0))
                for t in range(T):
                    for k in range(K):
                        i = nc.tensor.matmul(pair[1][:, t // 2, (t % 2) * D:(t % 2 + 1) * D],
                                             c_hT[:, k, t * P:(t + 1) * P], w0_s[:, k, :], start=k == 0, stop=k == K - 1)
                i.then_inc(c_lin.sem, 1)

            first_pass(pe, fore, mid, back)

            for par in range(2):
                pe.wait_ge(c_added[par].sem, G)
            pe.wait_ge(*c_o_ok.upto(Graph(G), 0))
            for n, s in enumerate((sum_o, sum_sq)):
                for t in range(T):
                    i = nc.tensor.matmul(obank[:, n * D:(n + 1) * D], ones[:, :], s[:, t, :], start=t == 0, stop=t == T - 1)
                i.then_inc(c_sums.sem, 1)
            pe.wait_ge(bn_steps.sem, 7)

            def a_free(g, u):
                p, n = a_unit(u)
                if n or not first(g):
                    pe.wait_ge(*a_copied[p].upto(g, n))
                return pair[p], a_filled[p].sem

            def b_free(g, u):
                p, n = b_unit(u)
                if n or not first(g):
                    pe.wait_ge(*b_copied[p].upto(g, n))
                return bank[p], b_filled[p].sem

            def o_free(g, n):
                if n or not first(g):
                    pe.wait_ge(*o_copied.upto(g, n))
                return obank, o_filled.sem

            def a_flip(src, u, ready):
                def f(g):
                    for s, k in ready:
                        pe.wait_ge(*s.upto(g, k))
                    dst, full = a_free(g, u)
                    for k in range(K):
                        i = flip(dst[:, k, :], src, k)
                    i.then_inc(full, 1)
                return f

            def rows(dst, hT, w):
                for t in range(T):
                    for k in range(K):
                        i = nc.tensor.matmul(dst[:, t // 2, (t % 2) * D:(t % 2 + 1) * D], hT[:, k, t * P:(t + 1) * P],
                                             w[:, k, :], start=k == 0, stop=k == K - 1)
                return i

            def a_qkv(g):
                pe.wait_ge(*a_copied[0].upto(g, 1))
                for u, w in ((U_Q, wq_s), (U_K, wk_s)):
                    dst, full = a_free(g, u)
                    for j in range(K):
                        for k in range(K):
                            i = nc.tensor.matmul(dst[:, j, :], w[:, k, j * P:(j + 1) * P], a_hT[:, k, :],
                                                 start=k == 0, stop=k == K - 1)
                    i.then_inc(full, 1)
                dst, full = a_free(g, U_V)
                rows(dst, a_hT, wv_s).then_inc(full, 1)

            def a_nat(h):
                def f(g):
                    pe.wait_ge(*a_qk_in.upto(g, 24))
                    for q in range(2):
                        dst, full = a_free(g, U_NAT + 2 * h + q)
                        for b in range(2):
                            t = 2 * q + b
                            i = nc.tensor.matmul(dst[:, b, :], q_parts[0:ROW_SHIFT, h, t * P:(t + 1) * P],
                                                 k_parts[0:ROW_SHIFT, h, :], start=True, stop=True)
                        i.then_inc(full, 1)
                return f

            def a_shift(g):
                for p in range(2):
                    pe.wait_ge(*a_copied[p].upto(g, U_ST // 2))
                dst, full = o_free(g, 0)
                for t in range(T):
                    i = nc.tensor.transpose(dst[0:H1, t * P:(t + 1) * P], minus_max[:, t, :], ident[:, :])
                i.then_inc(full, 1)

            def a_scores(h):
                def f(g):
                    pe.wait_ge(*a_shift_in.upto(g, H1))
                    pe.wait_ge(*a_mask_ok.upto(g, 1))
                    for q in range(2):
                        dst, full = a_free(g, U_ST + 2 * h + q)
                        for b in range(2):
                            k = 2 * q + b
                            nc.tensor.matmul(dst[:, b, :], ident16[:, :], maskT[:, k, :], start=True, stop=False)
                            i = nc.tensor.matmul(dst[:, b, :], k_parts[0:ROW_SHIFT + 1, h, k * P:(k + 1) * P],
                                                 q_parts[0:ROW_SHIFT + 1, h, :], start=False, stop=True)
                        i.then_inc(full, 1)
                return f

            def a_values(h):
                def f(g):
                    for p in range(2):
                        pe.wait_ge(*a_copied[p].upto(g, U_ST // 2 + h + 1))
                    dst, full = o_free(g, 1 + h)
                    for t in range(T):
                        for k in range(T):
                            i = nc.tensor.matmul(dst[:, t * (DH1 + 1):(t + 1) * (DH1 + 1)], pT[:, h % 2, k, t * P:(t + 1) * P],
                                                 v1[:, k * H1 + h, :], start=k == 0, stop=k == T - 1)
                    i.then_inc(full, 1)
                return f

            def a_wo(g):
                pe.wait_ge(*a_copied[0].upto(g, A_FILLS))
                dst, full = a_free(g, U_WO)
                rows(dst, att1T, wo_s).then_inc(full, 1)

            def b_agg(g):
                pe.wait_ge(*lns["b"]["h"].upto(g, 1))
                pe.wait_ge(*b_eye.upto(g, 1))
                for j in range(K):
                    dst, full = b_free(g, V_AGG + j)
                    for k in range(T):
                        i = nc.tensor.matmul(dst[:, :], b_h[:, k, j * P:(j + 1) * P], b_at[:, k, :],
                                             start=k == 0, stop=k == T - 1)
                    i.then_inc(full, 1)

            def b_hid(n):
                def f(g):
                    for j in range(K):
                        pe.wait_ge(*b_copied[j].upto(g, 1))
                    for t in (2 * n, 2 * n + 1):
                        dst, full = b_free(g, V_HID + t)
                        for k in range(K):
                            i = nc.tensor.matmul(dst[:, :], w1_s[:, k, t * P:(t + 1) * P], aggT[:, k, :],
                                                 start=k == 0, stop=k == K - 1)
                        i.then_inc(full, 1)
                return f

            def b_ms(g):
                for u in (V_HID + KH - 3, V_HID + KH - 2, V_HID + KH - 1):
                    p, n = b_unit(u)
                    pe.wait_ge(*b_copied[p].upto(g, n + 1))
                dst, full = b_free(g, V_MS)
                for t in range(T):
                    for k in range(KH):
                        i = nc.tensor.matmul(dst[:, t:t + 1], hsq[:, k, t * P:(t + 1) * P], ones[:, 0:1],
                                             start=k == 0, stop=k == KH - 1)
                i.then_inc(full, 1)

            def b_rb(g):
                pe.wait_ge(*b_diag.upto(g, 1))
                dst, full = b_free(g, V_RB)
                nc.tensor.matmul(dst[:, :], ones[:, :], diag[:, :, :].rearrange("p t n -> p (t n)"),
                                 start=True, stop=True).then_inc(full, 1)

            def b_out2(g):
                p, n = b_unit(V_RB)
                pe.wait_ge(*b_copied[p].upto(g, n + 1))
                for q in range(2):
                    dst, full = b_free(g, V_OUT + q)
                    for t in (2 * q, 2 * q + 1):
                        for k in range(KH):
                            i = nc.tensor.matmul(dst[:, (t % 2) * D:(t % 2 + 1) * D], hid[:, k, t * P:(t + 1) * P],
                                                 w2_s[:, k, :], start=k == 0, stop=k == KH - 1)
                    i.then_inc(full, 1)

            def d_flip(g):
                pe.wait_ge(*lns["d"]["h"].upto(g, 1))
                for k in range(K):
                    dst, full = b_free(g, V_HT + k)
                    flip(dst, d_h, k).then_inc(full, 1)

            def b_v3(g):
                for j in range(K):
                    p, n = b_unit(V_HT + j)
                    pe.wait_ge(*b_copied[p].upto(g, n + 1))
                for q in range(2):
                    dst, full = b_free(g, V_V3 + q)
                    for t in (2 * q, 2 * q + 1):
                        for k in range(K):
                            i = nc.tensor.matmul(dst[:, (t % 2) * D:(t % 2 + 1) * D], d_hT[:, k, t * P:(t + 1) * P],
                                                 w3_s[:, k, :], start=k == 0, stop=k == K - 1)
                    i.then_inc(full, 1)
                for s, u in enumerate((V_EI, V_EJ)):
                    dst, full = b_free(g, u)
                    for k in range(K):
                        i = nc.tensor.matmul(dst[0:H3, :], att_w[:, s, k, :], d_hT[:, k, :], start=k == 0, stop=k == K - 1)
                    i.then_inc(full, 1)

            def b_vt(g):
                p, n = b_unit(V_EJ)
                pe.wait_ge(*b_copied[p].upto(g, n + 1))
                dst, full = b_free(g, V_VT)
                for s in range(2):
                    for t in range(T):
                        c = (s * T + t) * H3
                        i = nc.tensor.matmul(dst[:, c:c + H3], vT[:, s, t * P:(t + 1) * P], ident[0:H3, 0:H3], start=True, stop=True)
                i.then_inc(full, 1)

            def b_spread(h):
                def f(g):
                    pe.wait_ge(*b_uT.upto(g, 1))
                    for s in range(2):
                        dst, full = b_free(g, V_HEAD + 3 * h + s)
                        nc.tensor.matmul(dst[:, :], sel3[:, h, :], uT[:, s, :], start=True, stop=True).then_inc(full, 1)
                return f

            def b_values(h):
                def f(g):
                    pe.wait_ge(*b_max.upto(g, h + 1))
                    dst, full = b_free(g, V_HEAD + 3 * h + 2)
                    w = DH3 + 1
                    for t in range(T):
                        for k in range(T):
                            i = nc.tensor.matmul(dst[:, t * w:(t + 1) * w], p3T[:, h % 2, k, t * P:(t + 1) * P],
                                                 v3[:, k * H3 + h, :], start=k == 0, stop=k == T - 1)
                    i.then_inc(full, 1)
                return f

            def both(*fs):
                return lambda g: [f(g) for f in fs]

            none = lambda g: None
            a = [none, a_flip(a_h, U_HT, [(lns["a"]["h"], 1)]), a_qkv] + [a_nat(h) for h in range(H1)] + [a_shift] \
                + [a_scores(0)] + [both(a_scores(h), a_values(h - 1)) for h in range(1, H1)] \
                + [both(a_values(H1 - 1), a_flip(att1, U_OT, [(o_copied, O_FILLS)])), a_wo]
            b = [none, b_agg] + [b_hid(n) for n in range(4)] + [b_ms, b_rb, none, b_out2, none, d_flip, b_v3, none, b_vt] \
                + [b_spread(0)] + [both(b_spread(h), b_values(h - 1)) for h in range(1, H3)] + [b_values(H3 - 1)]
            second_pass(pe, a, b)


def kernel(**inputs):
    import concourse.bacc as _bacc
    from concourse.bass_utils import run_bass_kernel_spmd as _run

    i = inputs
    t2 = lambda w: w.T
    laid = {
        "x": i["x"], "adjT": i["adj"].transpose(0, 2, 1), "w0T": t2(i["L0_gnn_W"]), "b0": i["L0_gnn_b"],
        "bn_w": i["L0_gnn_bn_weight"], "bn_b": i["L0_gnn_bn_bias"], "res_w": i["L0_gnn_res_weight"].reshape(1),
        "wqT": t2(i["L1_gnn_Wq"]), "wkT": t2(i["L1_gnn_Wk"]), "wvT": t2(i["L1_gnn_Wv"]), "woT": t2(i["L1_gnn_Wo"]),
        "bo": i["L1_gnn_bo"], "eps": i["L2_gnn_epsilon"].reshape(1), "w1": i["L2_gnn_W1"],
        "b1": i["L2_gnn_b1"].reshape(KH, P).T, "rms_w": i["L2_gnn_rms_weight"].reshape(KH, P).T, "w2": i["L2_gnn_W2"],
        "b2": i["L2_gnn_b2"], "w3": i["L3_gnn_W"], "att": i["L3_gnn_a"].reshape(-1),
    }
    nc = _bacc.Bacc("TRN2", target_bir_lowering=False, num_devices=1)
    arrays = {f"in_{k}": np.ascontiguousarray(v) for k, v in laid.items()}
    aps = [nc.dram_tensor(n, a.shape, mybir.dt.from_np(a.dtype), kind="ExternalInput").ap() for n, a in arrays.items()]
    aps.append(nc.dram_tensor("out_0", (G, N, D), mybir.dt.float32, kind="ExternalOutput").ap())
    gnn_stack(nc, *aps)
    return _run(nc, [arrays], core_ids=[0]).results[0]["out_0"]
```

```python
import concourse.bass as bass
from concourse import mybir
from contextlib import ExitStack
import numpy as np

P = 128
G, N, D = 32, 512, 256
T = N // P
K = D // P
H1, DH1 = 8, 32
HID = 1024
KH = HID // P
H3, DH3 = 4, 64
LN_EPS, BN_EPS, RMS_EPS = 1e-5, 1e-5, 1e-6
SLOPE = 0.2
ROW_SHIFT = 3 * DH1
ROW_LOW = 32
A_FILLS = 19
O_FILLS = 1 + H1
B_FILLS = 11


class Signal:

    def __init__(self, sem, per, unit=1):
        self.sem, self.per, self.unit = sem, per * unit, unit

    def upto(self, g, k):
        return self.sem, g.loop * (g.step * self.per) + (g.off * self.per + k * self.unit)


class Graph:

    def __init__(self, loop, off=0, step=1):
        self.loop, self.off, self.step = loop, off, step

    def plus(self, n):
        return Graph(self.loop, self.off + n, self.step)

    def half(self):
        if isinstance(self.loop, int):
            return Graph((self.loop * self.step + self.off) // 2)
        return Graph(self.loop, self.off // 2)

    def index(self):
        return self.loop * self.step + self.off

    def below(self, n):
        return isinstance(self.loop, int) and self.index() < n


def first(g):
    return g.below(1)


ORDER = """
a.x1 a.rstd a.center h.spread0 h.low0 h.prob0 b.load b.stats a.edges a.norm a.flip a.flipc h.spread1 h.low1 a.q
a.qhigh h.values0 a.qlow h.prob1 b.rstd a.k a.khigh h.spread2 h.head0 a.v h.values1 b.center a.klow h.low2 h.prob2
h.spread3 h.head1 h.values2 a.vc a.sortq h.low3 a.sortk a.nat0 h.prob3 a.max0 h.head2 a.nat1 a.max1 h.values3 a.nat2
b.edges a.max2 a.load h.head3 a.nat3 b.norm b.agg a.max3 a.nat4 a.max4 h.out b.aggc b.hid0 a.nat5 b.hidc0 b.sumsq0
a.max5 a.nat6 a.max6 b.hid1 b.hidc1 a.nat7 a.max7 a.shift a.shiftc a.putshift b.hid2 b.hidc2 a.scores0 b.sumsq1
a.bias b.hid3 b.sumsq2 a.exp0 a.vmask0 a.scores1 a.exp1 a.mask0 a.values0 a.mask1 a.vmask1 b.hidc3 a.head0 a.scores2
a.exp2 a.vmask2 a.values1 a.scores3 b.sumsq3 b.sum a.head1 a.mask2 a.values2 b.ms b.rrms b.diag a.exp3 a.vmask3
b.spread a.head2 a.scores4 a.exp4 b.scale a.mask3 a.values3 a.head3 b.bias a.scores5 a.vmask4 a.exp5 a.mask4 a.mask5
b.tanh a.vmask5 a.values4 a.head4 a.scores6 a.exp6 b.silu a.vmask6 a.mask6 a.values5 a.scores7 a.exp7 a.vmask7
a.mask7 a.head5 b.out2 h.store b.x3 b.stats3 a.values6 a.head6 b.rstd3 b.center3 a.values7 b.norm3 b.flip3 a.head7
a.ot b.flip3c b.v3 b.factors a.otc a.wo a.xmid b.v3c b.exps b.vt b.vcol
""".split()


def gnn_stack(nc, x, adjT, w0T, b0, bn_w, bn_b, res_w, wqT, wkT, wvT, woT, bo, eps, w1, b1, rms_w, w2, b2,
              w3, att, out):
    f32, bf16, f32r = mybir.dt.float32, mybir.dt.bfloat16, mybir.dt.float32r
    ALU, ACT, AX = mybir.AluOpType, mybir.ActivationFunctionType, mybir.AxisListType
    ctx = ExitStack()
    with ctx:
        def sb(name, *shape, dt=f32):
            return ctx.enter_context(nc.sbuf_tensor(name, list(shape), dt))

        def signal(name, per=1, unit=1):
            return Signal(ctx.enter_context(nc.semaphore(name)), per, unit)

        pre_bn = nc.dram_tensor("pre_bn", [G, N, D], f32, kind="Internal").ap()
        x_res = nc.dram_tensor("x_res", [G, N, D], f32, kind="Internal").ap()

        def nodes(t, g):
            return t[g.index()].rearrange("(t p) d -> p t d", p=P)

        ident = sb("ident", P, P)
        ones = sb("ones", P, P)
        minus_half = sb("minus_half", P, D)
        sel3 = sb("sel3", ROW_LOW + H3, H3, P, dt=f32r)
        att3 = sb("att3", P, T, D)
        u_parts = sb("u_parts", ROW_LOW + H3, 2, N, dt=f32r)
        w0_s, wq_s, wk_s, wv_s, wo_s, w3_s = (sb(n, P, K, D) for n in ("w0_s", "wq_s", "wk_s", "wv_s", "wo_s", "w3_s"))
        w1_s = sb("w1_s", P, K, HID)
        w2_s = sb("w2_s", P, KH, D)
        b0_s, bo_s, b2_s, bnw_s, bnb_s = (sb(n, P, D) for n in ("b0_s", "bo_s", "b2_s", "bnw_s", "bnb_s"))
        b1_s = sb("b1_s", P, KH)
        rms_s = sb("rms_s", P, KH)
        resw_s = sb("resw_s", P, 1)
        eps_s = sb("eps_s", P, 1)
        eps_ident = sb("eps_ident", P, P)
        half_rms = sb("half_rms", P, KH)
        att_w = sb("att_w", P, K, ROW_LOW + H3)

        c_deg = sb("c_deg", P, 4, T)
        c_dis = sb("c_dis", P, 2, T)
        bn_scale = sb("bn_scale", P, D)
        bn_shift = sb("bn_shift", P, D)

        ln = {s: {n: sb(f"{s}_{n}", P, T, w) for n, w in (("st", 6), ("mv", 2), ("ve", 1), ("rs", 1), ("sh", 1))}
              for s in "cabd"}

        a_xr = sb("a_xr", P, T, D)
        a_o = sb("a_o", P, T, D)
        a_at = sb("a_at", P, T, N)
        a_x1 = sb("a_x1", P, T, D)
        a_h = sb("a_h", P, T, D)
        a_hT = sb("a_hT", P, K, N)
        q_parts = sb("q_parts", P, H1, N, dt=f32r)
        k_parts = sb("k_parts", P, H1, N, dt=f32r)
        v1 = sb("v1", P, T * H1, DH1 + 1)
        node_edge = sb("node_edge", P, T, N, dt=bf16)
        minus_max = sb("minus_max", P, T, H1)
        shiftT = sb("shiftT", H1, N, dt=f32r)
        pT = sb("pT", P, 2, T, N)
        rden1 = sb("rden1", P, 2, T, 1)
        x_mid = sb("x_mid", P, T, D)

        b_at = sb("b_at", P, T, N)
        edge = sb("edge", P, T, N, dt=bf16)
        b_xb2 = sb("b_xb2", P, T, D)
        b_h = sb("b_h", P, T, D)
        aggT = sb("aggT", P, K, N)
        hid = sb("hid", P, KH, N)
        hsq = sb("hsq", P, KH, N)
        ms = sb("ms", P, T)
        rrms = sb("rrms", P, T)
        diag = sb("diag", P, T, P)
        x3 = sb("x3", P, T, D)
        v3 = sb("v3", P, T * H3, DH3 + 1)
        top = sb("top", ROW_LOW + H3, 2)
        vcol = sb("vcol", P, 2, T, H3)
        rden3 = sb("rden3", P, 2, T, 1)

        a_xbo = a_x1
        att1, att1T = a_h, a_hT
        d_h, d_hT = b_h, aggT
        rows_of = lambda t, r: t[r:r + H3].rearrange("p a b -> p (a b)").rearrange("p (a b) -> p a b", a=2)
        vT, uT = rows_of(b_h, ROW_LOW), rows_of(aggT, 0)
        hsum = diag[:, :, :].rearrange("p a b -> p (a b)")
        z8 = diag[0:H3].rearrange("p a b -> p (a b)")
        x_out = x3
        parts = pT[:, :, :, :].rearrange("p a (s k) n -> p (a s) k n", k=K)
        q_high, q_low, k_high, k_low = (parts[:, i] for i in range(4))
        low = hsq[:, :, :].rearrange("p (a t) n -> p a t n", a=2)
        p3T = hid[:, :, :].rearrange("p (a t) n -> p a t n", a=2)

        att_s = x_mid[:, 0:2, :].rearrange("p a b -> p (a b)").rearrange("p (h d) -> p h d", h=H3)
        att_t = x_mid[:, 2, :].rearrange("p (h d) -> p h d", h=H3)

        def two(t, a, b):
            return t[:, a:b, :].rearrange("p (c a) (b d) -> p c (a b) d", c=2, d=D)

        c_at = pT
        c_x, c_xres = two(hid, 0, 4), two(hid, 4, 8)
        c_o, c_sq = two(hsq, 0, 4), two(hsq, 4, 8)
        c_h, c_hT, c_hs = a_h, a_hT, a_x1
        sum_o, sum_sq, bn_t = b_h, aggT[:, :, :].rearrange("p k (b d) -> p (k b) d", d=D), x3

        pair = [ctx.enter_context(nc.psum_tensor(f"pair{i}", [P, 2, N], f32)) for i in range(2)]
        obank = ctx.enter_context(nc.psum_tensor("obank", [P, N], f32))
        bank = [ctx.enter_context(nc.psum_tensor(f"bank{i}", [P, N], f32)) for i in range(3)]

        n_loads = 18
        weights_in = signal("weights_in", n_loads, 16)
        consts = signal("consts", 11)
        setup = signal("setup", 14)
        eps_done = signal("eps_done", 1)

        c_x_in = [signal(f"c_x_in{i}", 1, 16) for i in range(2)]
        c_at_in = [signal(f"c_at_in{i}", 1, 16) for i in range(2)]
        c_eye = signal("c_eye")
        c_deg_sum = signal("c_deg_sum")
        c_deg_in = signal("c_deg_in", 2)
        c_deg_ok = signal("c_deg_ok")
        c_pow = signal("c_pow")
        c_dis_ok = signal("c_dis_ok")
        c_hT_sum = signal("c_hT_sum")
        c_hT_ok = signal("c_hT_ok")
        c_lin = signal("c_lin")
        c_scaled = signal("c_scaled")
        c_hs_ok = signal("c_hs_ok")
        c_agg = signal("c_agg")
        c_o_ok = signal("c_o_ok")
        c_sq_ok = signal("c_sq_ok")
        c_xres_ok = signal("c_xres_ok")
        c_added = [signal(f"c_added{i}", 2) for i in range(2)]
        c_o_out = [signal(f"c_o_out{i}", 1, 16) for i in range(2)]
        c_xres_out = [signal(f"c_xres_out{i}", 1, 16) for i in range(2)]
        c_sums = signal("c_sums", 2)
        bn_steps = signal("bn_steps", 6)
        bn_pow = signal("bn_pow", 1)

        lns = {s: {n: signal(f"{s}_{n}_ok", 1 + (n == "mv")) for n in ("st", "mv", "ve", "rs", "sh", "h")} for s in "cabd"}

        a_x_in = signal("a_x_in", 2, 16)
        a_at_in = signal("a_at_in", 1, 16)
        a_x1_step = signal("a_x1_step", 3)
        a_xbo_ok = signal("a_xbo_ok")
        a_mask_ok = signal("a_mask_ok")
        a_high_ok = signal("a_high_ok", 2)
        a_qk_in = signal("a_qk_in", 24, 16)
        a_shift_in = signal("a_shift_in", H1, 16)
        a_filled = [signal(f"a_filled{i}", A_FILLS) for i in range(2)]
        a_copied = [signal(f"a_copied{i}", A_FILLS) for i in range(2)]
        o_filled = signal("o_filled", O_FILLS)
        o_copied = signal("o_copied", O_FILLS)
        a_rden = signal("a_rden", H1)
        a_masked = [signal(f"a_masked{i}", H1) for i in range(2)]

        b_at_in = signal("b_at_in", 1, 16)
        b_edge_ok = signal("b_edge_ok")
        b_eye = signal("b_eye")
        b_xb2_ok = signal("b_xb2_ok")
        b_filled = [signal(f"b_filled{i}", B_FILLS) for i in range(3)]
        b_copied = [signal(f"b_copied{i}", B_FILLS) for i in range(3)]
        b_summed = signal("b_summed", KH - 1)
        b_rrms = signal("b_rrms")
        b_diag = signal("b_diag")
        b_norm = signal("b_norm", KH)
        b_tanh = signal("b_tanh", KH)
        b_top = signal("b_top", 2)
        b_z8 = signal("b_z8")
        b_zz = signal("b_zz")
        b_uT = signal("b_uT", 2)
        b_u_parts = signal("b_u_parts")
        b_low = signal("b_low", H3)
        b_max = signal("b_max", H3)
        b_p3 = signal("b_p3", H3)
        b_rden = signal("b_rden", H3)
        b_out = signal("b_out")
        b_stored = signal("b_stored", 1, 16)

        def a_unit(u):
            return u % 2, u // 2

        def b_unit(u):
            return u % 3, u // 3

        U_HT, U_Q, U_K, U_V, U_NAT, U_ST, U_OT, U_WO = 0, 1, 2, 3, 4, 20, 36, 37
        V_AGG, V_HID, V_MS, V_RB, V_OUT, V_HT, V_V3, V_E, V_VT, V_HEAD = 0, 2, 10, 11, 12, 14, 16, 18, 19, 21

        def second_pass(eng, steps):
            assert set(steps) <= set(ORDER), set(steps) - set(ORDER)

            def step(at):
                for name in ORDER:
                    g = at("abh".index(name[0]))
                    if name in steps and (not isinstance(g.loop, int) or 0 <= g.index() < G):
                        steps[name](g)

            for n in range(3):
                step(lambda lag: Graph(n - lag))
            with eng.Fori(3, G - 1) as n:
                step(lambda lag: Graph(n, -lag))
            for n in range(G - 1, G + 2):
                step(lambda lag: Graph(n - lag))

        def first_pass(eng, fore, mid, back):
            fore(Graph(0), 0)
            back(Graph(0), 0)
            for o in (1, 2):
                fore(Graph(o), o % 2)
                mid(Graph(o - 1), (o - 1) % 2)
                back(Graph(o), o % 2)
            with eng.Fori(1, G // 2 - 1) as i:
                for o in (1, 2):
                    fore(Graph(i, o, 2), o % 2)
                    mid(Graph(i, o - 1, 2), (o - 1) % 2)
                    back(Graph(i, o, 2), o % 2)
            fore(Graph(G - 1), 1)
            mid(Graph(G - 2), 0)
            back(Graph(G - 1), 1)
            mid(Graph(G - 1), 1)

        block = ctx.enter_context(nc.Block())

        @block.sync
        def _(sp):
            def bcast(v, n):
                return v.rearrange("(a n) -> a n", a=1).broadcast_to([P, n])

            loads = [(w, s[:, :, :]) for w, s in ((w0T, w0_s), (wqT, wq_s), (wkT, wk_s), (wvT, wv_s), (woT, wo_s), (w3, w3_s),
                                               (w1, w1_s), (w2, w2_s))]
            for w, s in loads:
                sp.dma_start(s, w.rearrange("(k p) n -> p k n", p=P)).then_inc(weights_in.sem, 16)
            for v, s in ((b0, b0_s), (bo, bo_s), (b2, b2_s), (bn_w, bnw_s), (bn_b, bnb_s)):
                sp.dma_start(s[:, :], bcast(v, D)).then_inc(weights_in.sem, 16)
            sp.dma_start(resw_s[:, :], bcast(res_w, 1)).then_inc(weights_in.sem, 16)
            sp.dma_start(eps_s[:, :], bcast(eps, 1)).then_inc(weights_in.sem, 16)
            sp.dma_start(b1_s[:, :], b1).then_inc(weights_in.sem, 16)
            sp.dma_start(rms_s[:, :], rms_w).then_inc(weights_in.sem, 16)
            sp.dma_start(att_s[:, :, :].rearrange("p h d -> p (h d)"), bcast(att, H3 * 2 * DH3)).then_inc(weights_in.sem, 16)

            def load(g, par):
                if not g.below(2):
                    sp.wait_ge(*c_agg.upto(g.plus(-1), 0))
                    sp.wait_ge(*c_xres_ok.upto(g.plus(-1), 0))
                sp.dma_start(c_x[:, par], nodes(x, g)).then_inc(c_x_in[par].sem, 16)
                sp.dma_start(c_at[:, par], nodes(adjT, g)).then_inc(c_at_in[par].sem, 16)

            def store_res(g, par):
                sp.wait_ge(*c_xres_ok.upto(g, 1))
                sp.dma_start(nodes(x_res, g), c_xres[:, par]).then_inc(c_xres_out[par].sem, 16)

            def store_o(g, par):
                sp.wait_ge(*c_o_ok.upto(g, 1))
                sp.dma_start(nodes(pre_bn, g), c_o[:, par]).then_inc(c_o_out[par].sem, 16)

            load(Graph(0), 0)
            load(Graph(1), 1)
            store_res(Graph(0), 0)
            with sp.Fori(0, G // 2 - 1) as i:
                for o in (1, 2):
                    store_o(Graph(i, o - 1, 2), (o - 1) % 2)
                    load(Graph(i, o + 1, 2), (o + 1) % 2)
                    store_res(Graph(i, o, 2), o % 2)
            store_res(Graph(G - 1), 1)
            store_o(Graph(G - 2), 0)
            store_o(Graph(G - 1), 1)
            for par in range(2):
                sp.wait_ge(c_o_out[par].sem, G // 2 * 16)
                sp.wait_ge(c_xres_out[par].sem, G // 2 * 16)

            def load_a(g):
                if not first(g):
                    sp.wait_ge(*a_x1_step.upto(g, 0))
                sp.dma_start(a_o[:, :, :], nodes(pre_bn, g)).then_inc(a_x_in.sem, 16)
                sp.dma_start(a_xr[:, :, :], nodes(x_res, g)).then_inc(a_x_in.sem, 16)
                if not first(g):
                    sp.wait_ge(*a_mask_ok.upto(g, 0))
                sp.dma_start(a_at[:, :, :], nodes(adjT, g)).then_inc(a_at_in.sem, 16)

            def load_b(g):
                if not first(g):
                    sp.wait_ge(*b_filled[1].upto(g.plus(-1), 1))
                sp.dma_start(b_at[:, :, :], nodes(adjT, g)).then_inc(b_at_in.sem, 16)

            def store(g):
                sp.wait_ge(*b_out.upto(g, 1))
                sp.dma_start(nodes(out, g), x_out[:, :, :]).then_inc(b_stored.sem, 16)

            def sort_parts(u, dst, srcs):
                def f(g):
                    r = DH1
                    p, n = a_unit(u)
                    sp.wait_ge(*a_copied[p].upto(g, n + 1))
                    if u == U_Q and not first(g):
                        for i in range(2):
                            sp.wait_ge(*a_filled[i].upto(g, 0))
                    for c, src in enumerate(srcs):
                        for i in range(P // r):
                            sp.dma_start(dst[c * r:(c + 1) * r, i::P // r, :].bitcast(f32),
                                         src[i * r:(i + 1) * r]).then_inc(a_qk_in.sem, 16)
                return f

            def put_shift(g):
                sp.wait_ge(*o_copied.upto(g, 1))
                for h in range(H1):
                    sp.dma_start(q_parts[ROW_SHIFT:ROW_SHIFT + 1, h, :].bitcast(f32),
                                 shiftT[h:h + 1, :].bitcast(f32)).then_inc(a_shift_in.sem, 16)

            def load_next(g):
                if not g.below(G - 1) and isinstance(g.loop, int):
                    return
                load_a(g.plus(1))

            load_a(Graph(0))
            second_pass(sp, {
                "a.load": load_next, "b.load": load_b,
                "a.sortq": sort_parts(U_Q, q_parts, (q_high, q_high, q_low)),
                "a.sortk": sort_parts(U_K, k_parts, (k_high, k_low, k_high)),
                "a.putshift": put_shift, "h.store": store})
            sp.wait_ge(b_stored.sem, G * 16)

        @block.gpsimd
        def _(pool):
            nc.gpsimd.memset(ident[:, :], 0.0).then_inc(consts.sem, 1)
            nc.gpsimd.memset(ones[:, :], 1.0).then_inc(consts.sem, 1)
            nc.gpsimd.memset(minus_half[:, :], -0.5).then_inc(consts.sem, 1)
            nc.gpsimd.memset(sel3[:, :, :].bitcast(f32), 0.0).then_inc(consts.sem, 1)
            nc.gpsimd.memset(sum_o[:, :, :], 0.0).then_inc(consts.sem, 1)
            nc.gpsimd.memset(sum_sq[:, :, :], 0.0).then_inc(consts.sem, 1)
            nc.gpsimd.memset(v1[:, :, DH1:DH1 + 1], 1.0).then_inc(consts.sem, 1)
            nc.gpsimd.memset(v3[:, :, DH3:DH3 + 1], 1.0).then_inc(consts.sem, 1)
            pool.wait_ge(consts.sem, 8)
            nc.gpsimd.memset(k_parts[ROW_SHIFT:ROW_SHIFT + 1, :, :].bitcast(f32), 1.0).then_inc(consts.sem, 1)
            pool.wait_ge(consts.sem, 9)
            for n, r in enumerate((0, ROW_LOW)):
                rows = sel3[r:r + H3, :, :]
                pool.wait_ge(consts.sem, 9 + n)
                nc.gpsimd.affine_select(out=rows, in_=rows.bitcast(f32), compare_op=ALU.not_equal, fill=1.0, base=0,
                                        pattern=[[-1, H3], [0, P]], channel_multiplier=1).then_inc(consts.sem, 1)
            pool.wait_ge(consts.sem, 11)
            nc.gpsimd.memset(u_parts[:, :, :].bitcast(f32), 0.0).then_inc(consts.sem, 1)
            pool.wait_ge(consts.sem, 12)
            nc.gpsimd.affine_select(out=ident[:, :], in_=ident[:, :], compare_op=ALU.not_equal, fill=1.0, base=0,
                                    pattern=[[-1, P]], channel_multiplier=1).then_inc(consts.sem, 1)
            pool.wait_ge(consts.sem, 13)

            def power(out_ap, in_ap, n):
                return nc.gpsimd.tensor_tensor(out_ap, in_ap, minus_half[:, 0:n], ALU.pow)

            def rstd(s, g):
                pool.wait_ge(*lns[s]["ve"].upto(g, 1))
                power(ln[s]["rs"][:, :, 0], ln[s]["ve"][:, :, 0], T).then_inc(lns[s]["rs"].sem, 1)

            def fore(g, par):
                pool.wait_ge(*c_deg_ok.upto(g, 1))
                power(c_deg[:, 3, :], c_deg[:, 1, :], T).then_inc(c_pow.sem, 1)
                rstd("c", g)

            def mid(g, par):
                pool.wait_ge(*c_o_ok.upto(g, 1))
                if not first(g):
                    pool.wait_ge(*c_added[1 - par].upto(g.half(), 2 * par))
                nc.gpsimd.tensor_tensor(sum_o[:, :, :], sum_o[:, :, :], c_o[:, par], ALU.add).then_inc(c_added[par].sem, 1)
                pool.wait_ge(*c_sq_ok.upto(g, 1))
                nc.gpsimd.tensor_tensor(sum_sq[:, :, :], sum_sq[:, :, :], c_sq[:, par], ALU.add).then_inc(c_added[par].sem, 1)

            first_pass(pool, fore, mid, lambda g, par: None)
            pool.wait_ge(bn_steps.sem, 4)
            nc.gpsimd.tensor_tensor(bn_t[:, 3, :], bn_t[:, 2, :], minus_half[:, :], ALU.pow).then_inc(bn_pow.sem, 1)

            def a_bias(g):
                pool.wait_ge(*lns["a"]["h"].upto(g, 1))
                nc.gpsimd.tensor_tensor(a_xbo[:, :, :], a_x1[:, :, :], bo_s[:, None, :].broadcast_to([P, T, D]),
                                        ALU.add).then_inc(a_xbo_ok.sem, 1)

            def b_bias(g):
                pool.wait_ge(*a_copied[1].upto(g, A_FILLS))
                nc.gpsimd.tensor_tensor(b_xb2[:, :, :], x_mid[:, :, :], b2_s[:, None, :].broadcast_to([P, T, D]),
                                        ALU.add).then_inc(b_xb2_ok.sem, 1)

            def b_ms(g):
                pool.wait_ge(*b_copied[V_MS % 3].upto(g, V_MS // 3 + 1))
                power(rrms[:, :], ms[:, :], T).then_inc(b_rrms.sem, 1)

            def a_mask(h):
                def f(g):
                    pool.wait_ge(*a_copied[0].upto(g, U_ST // 2 + h + 1))
                    pool.wait_ge(*a_mask_ok.upto(g, 1))
                    half = pT[:, h % 2, 0:2]
                    nc.gpsimd.tensor_tensor(half, half, node_edge[:, 0:2, :], ALU.mult).then_inc(a_masked[0].sem, 1)
                return f

            def b_sumsq(i):
                def f(g):
                    for t in (2 * i, 2 * i + 1):
                        p, n = b_unit(V_HID + t)
                        pool.wait_ge(*b_copied[p].upto(g, n + 1))
                        if t == 0:
                            continue
                        if t > 1:
                            pool.wait_ge(*b_summed.upto(g, t - 1))
                        nc.gpsimd.tensor_tensor(hsum[:, :], hsum[:, :] if t > 1 else hsq[:, 0, :], hsq[:, t, :],
                                                ALU.add).then_inc(b_summed.sem, 1)
                return f

            second_pass(pool, {
                "a.rstd": lambda g: rstd("a", g), "b.rstd": lambda g: rstd("b", g), "b.rstd3": lambda g: rstd("d", g),
                "a.bias": a_bias, "b.bias": b_bias, "b.rrms": b_ms,
                **{f"a.mask{h}": a_mask(h) for h in range(H1)}, **{f"b.sumsq{i}": b_sumsq(i) for i in range(4)}})

        @block.scalar
        def _(act):
            def normalise(s, g, dst, src, wait=None):
                act.wait_ge(*lns[s]["sh"].upto(g, 1))
                for t in range(T):
                    i = nc.scalar.activation(dst[:, t, :], src[:, t, :], ACT.Relu, bias=ln[s]["sh"][:, t, :],
                                             scale=ln[s]["rs"][:, t, :])
                i.then_inc(lns[s]["h"].sem, 1)

            def fore(g, par):
                if not first(g):
                    act.wait_ge(*c_xres_ok.upto(g, 0))
                normalise("c", g, c_h, c_x[:, par, :, :])

            def mid(g, par):
                act.wait_ge(*c_agg.upto(g, 1))
                if not g.below(2):
                    act.wait_ge(*c_o_out[par].upto(g.half(), 0))
                    act.wait_ge(*c_added[par].upto(g.half(), 0))
                for t in range(T):
                    src = (obank if t < 2 else bank[2])[:, (t % 2) * D:(t % 2 + 1) * D]
                    i = nc.scalar.activation(c_o[:, par, t, :], src, ACT.Copy, scale=c_dis[:, par, t:t + 1])
                i.then_inc(c_o_ok.sem, 1)
                act.wait_ge(*c_o_ok.upto(g, 1))
                nc.scalar.activation(c_sq[:, par], c_o[:, par], ACT.Square).then_inc(c_sq_ok.sem, 1)

            def back(g, par):
                act.wait_ge(*c_hT_sum.upto(g, 1))
                nc.scalar.activation(c_hT[:, :, :], pair[0][:, :, :], ACT.Copy).then_inc(c_hT_ok.sem, 1)
                act.wait_ge(*c_lin.upto(g, 1))
                act.wait_ge(*c_dis_ok.upto(g, 1))
                for t in range(T):
                    i = nc.scalar.activation(c_hs[:, t, :], pair[1][:, t // 2, (t % 2) * D:(t % 2 + 1) * D], ACT.Copy,
                                             scale=c_dis[:, par, t:t + 1])
                i.then_inc(c_scaled.sem, 1)

            first_pass(act, fore, mid, back)

            def a_take(g, u, dst, func=ACT.Copy, **more):
                p, n = a_unit(u)
                act.wait_ge(*a_filled[p].upto(g, n + 1))
                nc.scalar.activation(dst, pair[p][:, :, :], func, **more).then_inc(a_copied[p].sem, 1)

            def a_high(i, u, high):
                def f(g):
                    p, n = a_unit(u)
                    act.wait_ge(*a_filled[p].upto(g, n + 1))
                    nc.scalar.activation(high.bitcast(f32r), pair[p][:, :, :], ACT.Copy).then_inc(a_high_ok.sem, 1)
                return f

            def a_v(g):
                p, n = a_unit(U_V)
                act.wait_ge(*a_filled[p].upto(g, n + 1))
                nc.scalar.activation(v1[:, :, 0:DH1], pair[p][:, :, :].rearrange("p a (h d) -> p (a h) d", d=DH1),
                                     ACT.Copy).then_inc(a_copied[p].sem, 1)

            def a_shift(g):
                act.wait_ge(*o_filled.upto(g, 1))
                nc.scalar.activation(shiftT[:, :], obank[0:H1, :], ACT.Copy).then_inc(o_copied.sem, 1)

            def a_exp(h):
                def f(g):
                    if h or not first(g):
                        act.wait_ge(*o_filled.upto(g, h))
                    for q in range(2):
                        a_take(g, U_ST + 2 * h + q, pT[:, h % 2, 2 * q:2 * q + 2, :], ACT.Exp, scale=DH1 ** -0.5)
                return f

            def b_take(g, u, dst, func=ACT.Copy, src=None, **more):
                p, n = b_unit(u)
                act.wait_ge(*b_filled[p].upto(g, n + 1))
                nc.scalar.activation(dst, bank[p][:, :] if src is None else src, func, **more).then_inc(b_copied[p].sem, 1)

            def b_hid(i):
                def f(g):
                    for t in (2 * i, 2 * i + 1):
                        p, n = b_unit(V_HID + t)
                        act.wait_ge(*b_filled[p].upto(g, n + 1))
                        nc.scalar.activation(hid[:, t, :], bank[p][:, :], ACT.Identity, bias=b1_s[:, t:t + 1])
                        nc.scalar.activation(hsq[:, t, :], bank[p][:, :], ACT.Square,
                                             bias=b1_s[:, t:t + 1]).then_inc(b_copied[p].sem, 1)
                return f

            def b_tanhs(g):
                for t in range(KH):
                    act.wait_ge(*b_norm.upto(g, t + 1))
                    nc.scalar.activation(hsq[:, t, :], hid[:, t, :], ACT.Tanh,
                                         scale=half_rms[:, t:t + 1]).then_inc(b_tanh.sem, 1)

            def b_v3(g):
                for i in range(2):
                    b_take(g, V_V3 + i, v3[:, 2 * H3 * i:2 * H3 * (i + 1), 0:DH3],
                           src=bank[(V_V3 + i) % 3][:, :].rearrange("p (h d) -> p h d", d=DH3))

            def b_exps(g):
                act.wait_ge(*b_top.upto(g, 2))
                keys = slice(ROW_LOW, ROW_LOW + H3)
                nc.scalar.activation(vT[:, 0, :], bank[V_E % 3][keys, :], ACT.Exp, bias=top[keys, 0:1])
                nc.scalar.activation(vT[:, 1, :], bank[V_E % 3][keys, :], ACT.Exp, bias=top[keys, 1:2],
                                     scale=SLOPE).then_inc(b_copied[V_E % 3].sem, 1)
                act.wait_ge(*b_zz.upto(g, 1))
                nc.scalar.activation(uT[:, :, :], uT[:, :, :], ACT.Exp).then_inc(b_uT.sem, 1)
                act.wait_ge(*b_uT.upto(g, 1))
                nc.scalar.activation(u_parts[0:H3], uT[:, :, :], ACT.Copy).then_inc(b_uT.sem, 1)

            def b_low3(h):
                def f(g):
                    p, n = b_unit(V_HEAD + 3 * h + 1)
                    act.wait_ge(*b_filled[p].upto(g, n + 1))
                    for u in (V_VT, V_VT + 1):
                        act.wait_ge(*b_copied[u % 3].upto(g, u // 3 + 1))
                    if h >= 2:
                        act.wait_ge(*b_max.upto(g, h - 1))
                    for k in range(T):
                        i = nc.scalar.activation(low[:, h % 2, k, :], bank[p][:, :], ACT.Copy, scale=vcol[:, 1, k, h:h + 1])
                    i.then_inc(b_copied[p].sem, 1)
                return f

            second_pass(act, {
                "a.norm": lambda g: normalise("a", g, a_h, a_x1), "b.norm": lambda g: normalise("b", g, b_h, x_mid),
                "b.norm3": lambda g: normalise("d", g, d_h, x3),
                "a.flipc": lambda g: a_take(g, U_HT, a_hT[:, :, :]), "a.qhigh": a_high(0, U_Q, q_high),
                "a.khigh": a_high(1, U_K, k_high), "a.vc": a_v, "a.shiftc": a_shift,
                "a.otc": lambda g: a_take(g, U_OT, att1T[:, :, :]),
                "b.aggc": lambda g: [b_take(g, V_AGG + j, aggT[:, j, :]) for j in range(K)], "b.tanh": b_tanhs,
                "b.flip3c": lambda g: [b_take(g, V_HT + j, d_hT[:, j, :]) for j in range(K)], "b.v3c": b_v3,
                "b.exps": b_exps, **{f"a.exp{h}": a_exp(h) for h in range(H1)},
                **{f"b.hidc{i}": b_hid(i) for i in range(4)}, **{f"h.low{h}": b_low3(h) for h in range(H3)}})

        @block.vector
        def _(dve):
            dve.wait_ge(weights_in.sem, n_loads * 16)
            dve.wait_ge(consts.sem, 13)
            nc.vector.tensor_scalar(eps_ident[:, :], ident[:, :], eps_s[:, 0:1], None, ALU.mult).then_inc(setup.sem, 1)
            nc.vector.tensor_scalar(half_rms[:, :], rms_s[:, :], 0.5, None, ALU.mult).then_inc(setup.sem, 1)
            dve.wait_ge(setup.sem, 2)
            for t in range(KH):
                nc.vector.tensor_scalar(w2_s[:, t, :], w2_s[:, t, :], half_rms[:, t:t + 1], None, ALU.mult)
            nc.vector.memset(att_w[:, :, :], 0.0).then_inc(setup.sem, 1)
            dve.wait_ge(setup.sem, 3)
            n = 3
            for s in range(2):
                for k in range(K):
                    if n > 3:
                        dve.wait_ge(setup.sem, n)
                    nc.vector.tensor_tensor(att_t[:, :, :], w3_s[:, k, :].rearrange("p (h d) -> p h d", d=DH3),
                                            att_s[:, :, s * DH3:(s + 1) * DH3], ALU.mult).then_inc(setup.sem, 1)
                    dve.wait_ge(setup.sem, n + 1)
                    nc.vector.tensor_reduce(att_w[:, k, s * ROW_LOW:s * ROW_LOW + H3], att_t[:, :, :], AX.X, ALU.add).then_inc(setup.sem, 1)
                    n += 2

            def stats(s, g, src):
                for t in range(T):
                    i = nc.vector.bn_stats(out=ln[s]["st"][:, t, :], in_=src[:, t, :])
                i.then_inc(lns[s]["st"].sem, 1)
                dve.wait_ge(*lns[s]["st"].upto(g, 1))
                st, mv, q4 = ln[s]["st"], ln[s]["mv"], ln[s]["rs"]
                nc.vector.tensor_tensor(mv[:, :, 0], st[:, :, 1], st[:, :, 4], ALU.add)
                nc.vector.scalar_tensor_tensor(out=mv[:, :, 1], in0=st[:, :, 2], scalar=D * LN_EPS, in1=st[:, :, 5],
                                               op0=ALU.add, op1=ALU.add)
                nc.vector.tensor_tensor(ln[s]["sh"][:, :, 0], st[:, :, 1], st[:, :, 4],
                                        ALU.subtract).then_inc(lns[s]["mv"].sem, 1)
                dve.wait_ge(*lns[s]["mv"].upto(g, 1))
                nc.vector.scalar_tensor_tensor(out=q4[:, :, 0], in0=ln[s]["sh"][:, :, 0], scalar=0.25,
                                               in1=ln[s]["sh"][:, :, 0], op0=ALU.mult,
                                               op1=ALU.mult).then_inc(lns[s]["mv"].sem, 1)
                dve.wait_ge(*lns[s]["mv"].upto(g, 2))
                nc.vector.scalar_tensor_tensor(out=ln[s]["ve"][:, :, 0], in0=mv[:, :, 1], scalar=1.0 / D,
                                               in1=q4[:, :, 0], op0=ALU.mult, op1=ALU.add).then_inc(lns[s]["ve"].sem, 1)

            def shift(s, g):
                dve.wait_ge(*lns[s]["rs"].upto(g, 1))
                nc.vector.scalar_tensor_tensor(out=ln[s]["sh"][:, :, 0], in0=ln[s]["mv"][:, :, 0], scalar=-0.5,
                                               in1=ln[s]["rs"][:, :, 0], op0=ALU.mult,
                                               op1=ALU.mult).then_inc(lns[s]["sh"].sem, 1)

            def fore(g, par):
                dve.wait_ge(*c_at_in[par].upto(g.half(), 1))
                for t in range(T):
                    d = c_at[:, par, t, t * P:(t + 1) * P]
                    i = nc.vector.tensor_tensor(d, d, ident[:, :], ALU.add)
                i.then_inc(c_eye.sem, 1)
                dve.wait_ge(*c_x_in[par].upto(g.half(), 1))
                stats("c", g, c_x[:, par, :, :])
                dve.wait_ge(*c_deg_sum.upto(g, 1))
                nc.vector.tensor_scalar(c_deg[:, 0, :], bank[0][:, 0:T], 0.0, None, ALU.is_equal).then_inc(c_deg_in.sem, 1)
                dve.wait_ge(*c_deg_in.upto(g, 1))
                nc.vector.tensor_scalar(c_deg[:, 2, :], c_deg[:, 0, :], -1.0, 1.0, ALU.mult, ALU.add).then_inc(c_deg_in.sem, 1)
                nc.vector.tensor_tensor(c_deg[:, 1, :], bank[0][:, 0:T], c_deg[:, 0, :], ALU.add).then_inc(c_deg_ok.sem, 1)
                shift("c", g)
                dve.wait_ge(*c_pow.upto(g, 1))
                dve.wait_ge(*c_deg_in.upto(g, 2))
                nc.vector.tensor_tensor(c_dis[:, par, :], c_deg[:, 3, :], c_deg[:, 2, :], ALU.mult).then_inc(c_dis_ok.sem, 1)
                dve.wait_ge(*lns["c"]["h"].upto(g, 1))
                if not g.below(2):
                    dve.wait_ge(*c_xres_out[par].upto(g.half(), 0))
                nc.vector.scalar_tensor_tensor(out=c_xres[:, par], in0=c_h[:, :, :], scalar=resw_s[:, 0:1],
                                               in1=c_x[:, par], op0=ALU.mult, op1=ALU.add).then_inc(c_xres_ok.sem, 1)

            def back(g, par):
                dve.wait_ge(*c_scaled.upto(g, 1))
                dve.wait_ge(*c_dis_ok.upto(g, 1))
                for t in range(T):
                    i = nc.vector.scalar_tensor_tensor(out=c_hs[:, t, :], in0=b0_s[:, :], scalar=c_dis[:, par, t:t + 1],
                                                       in1=c_hs[:, t, :], op0=ALU.mult, op1=ALU.add)
                i.then_inc(c_hs_ok.sem, 1)

            first_pass(dve, fore, lambda g, par: None, back)

            dve.wait_ge(c_sums.sem, 2)
            rows = 1.0 / (G * N)
            mean, var = bn_t[:, 0, :], bn_t[:, 2, :]
            nc.vector.tensor_scalar(mean, obank[:, 0:D], rows, None, ALU.mult).then_inc(bn_steps.sem, 1)
            dve.wait_ge(bn_steps.sem, 1)
            nc.vector.tensor_tensor(bn_t[:, 1, :], mean, mean, ALU.mult).then_inc(bn_steps.sem, 1)
            dve.wait_ge(bn_steps.sem, 2)
            nc.vector.scalar_tensor_tensor(out=var, in0=obank[:, D:2 * D], scalar=rows, in1=bn_t[:, 1, :], op0=ALU.mult,
                                           op1=ALU.subtract).then_inc(bn_steps.sem, 1)
            dve.wait_ge(bn_steps.sem, 3)
            nc.vector.tensor_scalar(var, var, 0.0, BN_EPS, ALU.max, ALU.add).then_inc(bn_steps.sem, 1)
            dve.wait_ge(bn_pow.sem, 1)
            nc.vector.tensor_tensor(bn_scale[:, :], bn_t[:, 3, :], bnw_s[:, :], ALU.mult).then_inc(bn_steps.sem, 1)
            dve.wait_ge(bn_steps.sem, 5)
            nc.vector.tensor_tensor(bn_t[:, 1, :], mean, bn_scale[:, :], ALU.mult).then_inc(bn_steps.sem, 1)
            dve.wait_ge(bn_steps.sem, 6)
            nc.vector.tensor_tensor(bn_shift[:, :], bnb_s[:, :], bn_t[:, 1, :], ALU.subtract).then_inc(bn_steps.sem, 1)
            dve.wait_ge(bn_steps.sem, 7)

            def a_ln(g):
                wide = [P, T, D]
                dve.wait_ge(*a_x_in.upto(g, 2))
                if not first(g):
                    dve.wait_ge(*lns["a"]["h"].upto(g, 0))
                    dve.wait_ge(*a_xbo_ok.upto(g, 0))
                nc.vector.tensor_tensor(a_o[:, :, :], a_o[:, :, :], bn_scale[:, None, :].broadcast_to(wide),
                                        ALU.mult).then_inc(a_x1_step.sem, 1)
                dve.wait_ge(*a_x1_step.upto(g, 1))
                nc.vector.tensor_tensor(a_o[:, :, :], a_o[:, :, :], bn_shift[:, None, :].broadcast_to(wide),
                                        ALU.add).then_inc(a_x1_step.sem, 1)
                dve.wait_ge(*a_x1_step.upto(g, 2))
                nc.vector.scalar_tensor_tensor(out=a_x1[:, :, :], in0=a_o[:, :, :], scalar=0.0, in1=a_xr[:, :, :],
                                               op0=ALU.max, op1=ALU.add).then_inc(a_x1_step.sem, 1)
                dve.wait_ge(*a_x1_step.upto(g, 3))
                stats("a", g, a_x1)

            def a_edges(g):
                dve.wait_ge(*a_at_in.upto(g, 1))
                nc.vector.tensor_scalar(node_edge[:, :, :], a_at[:, :, :], 0.0, None, ALU.not_equal).then_inc(a_mask_ok.sem, 1)

            def a_low(i, u, high, low_part):
                def f(g):
                    p, n = a_unit(u)
                    dve.wait_ge(*a_high_ok.upto(g, i + 1))
                    nc.vector.tensor_tensor(low_part.bitcast(f32r), pair[p][:, :, :], high,
                                            ALU.subtract).then_inc(a_copied[p].sem, 1)
                return f

            def a_mask(h):
                def f(g):
                    dve.wait_ge(*a_copied[1].upto(g, U_ST // 2 + h + 1))
                    dve.wait_ge(*a_mask_ok.upto(g, 1))
                    half = pT[:, h % 2, 2:4]
                    nc.vector.tensor_tensor(half, half, node_edge[:, 2:4, :], ALU.mult).then_inc(a_masked[1].sem, 1)
                return f

            def a_max(h):
                def f(g):
                    for q in range(2):
                        p, n = a_unit(U_NAT + 2 * h + q)
                        dve.wait_ge(*a_filled[p].upto(g, n + 1))
                        nc.vector.tensor_reduce(minus_max[:, 2 * q:2 * q + 2, h], pair[p][:, :, :], AX.X, ALU.max,
                                                negate=True).then_inc(a_copied[p].sem, 1)
                return f

            def a_head(h):
                def f(g):
                    dve.wait_ge(*o_filled.upto(g, 2 + h))
                    o = obank[:, 0:T * (DH1 + 1)].rearrange("p (t d) -> p t d", d=DH1 + 1)
                    nc.vector.reciprocal(rden1[:, h % 2], o[:, :, DH1:DH1 + 1]).then_inc(a_rden.sem, 1)
                    dve.wait_ge(*a_rden.upto(g, h + 1))
                    nc.vector.tensor_tensor(att1[:, :, h * DH1:(h + 1) * DH1], o[:, :, 0:DH1],
                                            rden1[:, h % 2].broadcast_to([P, T, DH1]), ALU.mult).then_inc(o_copied.sem, 1)
                return f

            def a_wo(g):
                p, n = a_unit(U_WO)
                dve.wait_ge(*a_filled[p].upto(g, n + 1))
                dve.wait_ge(*a_xbo_ok.upto(g, 1))
                if not first(g):
                    dve.wait_ge(*lns["b"]["h"].upto(g, 0))
                    dve.wait_ge(*b_xb2_ok.upto(g, 0))
                nc.vector.tensor_tensor(x_mid[:, :, :], pair[p][:, :, :].rearrange("p a (b d) -> p (a b) d", d=D),
                                        a_xbo[:, :, :], ALU.add).then_inc(a_copied[p].sem, 1)

            def b_ln(g):
                dve.wait_ge(*a_copied[1].upto(g, A_FILLS))
                stats("b", g, x_mid)

            def b_edges(g):
                dve.wait_ge(*b_at_in.upto(g, 1))
                nc.vector.tensor_scalar(edge[:, :, :], b_at[:, :, :], 0.0, None, ALU.is_gt).then_inc(b_edge_ok.sem, 1)
                dve.wait_ge(*b_edge_ok.upto(g, 1))
                for t in range(T):
                    d = b_at[:, t, t * P:(t + 1) * P]
                    i = nc.vector.tensor_tensor(d, d, eps_ident[:, :], ALU.add)
                i.then_inc(b_eye.sem, 1)

            def b_ms(g):
                p, n = b_unit(V_MS)
                dve.wait_ge(*b_filled[p].upto(g, n + 1))
                nc.vector.tensor_scalar(ms[:, :], bank[p][:, 0:T], 1.0 / HID, RMS_EPS, ALU.mult,
                                        ALU.add).then_inc(b_copied[p].sem, 1)

            def b_diags(g):
                dve.wait_ge(*b_rrms.upto(g, 1))
                for t in range(T):
                    i = nc.vector.tensor_scalar(diag[:, t, :], ident[:, :], rrms[:, t:t + 1], None, ALU.mult)
                i.then_inc(b_diag.sem, 1)

            def b_scale(g):
                p, n = b_unit(V_RB)
                dve.wait_ge(*b_filled[p].upto(g, n + 1))
                for t in range(KH):
                    i = nc.vector.tensor_tensor(hid[:, t, :], hid[:, t, :], bank[p][:, :], ALU.mult)
                    i.then_inc(b_norm.sem, 1)

            def b_silu(g):
                p, n = b_unit(V_RB)
                for t in range(KH):
                    dve.wait_ge(*b_tanh.upto(g, t + 1))
                    i = nc.vector.scalar_tensor_tensor(out=hid[:, t, :], in0=hsq[:, t, :], scalar=1.0, in1=hid[:, t, :],
                                                       op0=ALU.add, op1=ALU.mult)
                i.then_inc(b_copied[p].sem, 1)

            def b_x3(g):
                dve.wait_ge(*b_xb2_ok.upto(g, 1))
                if not first(g):
                    dve.wait_ge(*b_stored.upto(g, 0))
                for q in range(2):
                    p, n = b_unit(V_OUT + q)
                    dve.wait_ge(*b_filled[p].upto(g, n + 1))
                    nc.vector.tensor_tensor(x3[:, 2 * q:2 * q + 2, :], bank[p][:, :].rearrange("p (b d) -> p b d", d=D),
                                            b_xb2[:, 2 * q:2 * q + 2, :], ALU.add).then_inc(b_copied[p].sem, 1)

            def d_ln(g):
                for q in range(2):
                    p, n = b_unit(V_OUT + q)
                    dve.wait_ge(*b_copied[p].upto(g, n + 1))
                stats("d", g, x3)

            def b_factors(g):
                p, n = b_unit(V_E)
                keys = slice(ROW_LOW, ROW_LOW + H3)
                dve.wait_ge(*b_filled[p].upto(g, n + 1))
                nc.vector.tensor_reduce(top[0:H3, 0:1], bank[p][keys, :], AX.X, ALU.max, negate=True)
                nc.vector.tensor_reduce(top[keys, 0:1], bank[p][keys, :], AX.X, ALU.max, negate=True).then_inc(b_top.sem, 1)
                dve.wait_ge(*b_top.upto(g, 1))
                nc.vector.tensor_scalar(z8[:, :], bank[p][0:H3, :], top[0:H3, 0:1], 1.0 - SLOPE, ALU.subtract,
                                        ALU.mult).then_inc(b_z8.sem, 1)
                nc.vector.tensor_scalar(top[keys, 1:2], top[keys, 0:1], SLOPE, None, ALU.mult).then_inc(b_top.sem, 1)
                dve.wait_ge(*b_z8.upto(g, 1))
                nc.vector.tensor_scalar(uT[:, 0, :], z8[:, :], 0.0, None, ALU.min)
                nc.vector.tensor_scalar(uT[:, 1, :], z8[:, :], -1.0, 0.0, ALU.mult, ALU.min).then_inc(b_zz.sem, 1)

            def b_vcol(g):
                for i in range(2):
                    p, n = b_unit(V_VT + i)
                    dve.wait_ge(*b_filled[p].upto(g, n + 1))
                    nc.vector.tensor_copy(vcol[:, i].rearrange("p t h -> p (t h)"),
                                          bank[p][:, 0:T * H3]).then_inc(b_copied[p].sem, 1)
                dve.wait_ge(*b_uT.upto(g, 2))
                nc.vector.tensor_tensor(u_parts[ROW_LOW:ROW_LOW + H3], uT[:, :, :], u_parts[0:H3].bitcast(f32),
                                        ALU.subtract).then_inc(b_u_parts.sem, 1)

            def b_prob(h):
                def f(g):
                    p, n = b_unit(V_HEAD + 3 * h)
                    pl, nl = b_unit(V_HEAD + 3 * h + 1)
                    dve.wait_ge(*b_filled[p].upto(g, n + 1))
                    dve.wait_ge(*b_copied[pl].upto(g, nl + 1))
                    for u in (V_VT, V_VT + 1):
                        dve.wait_ge(*b_copied[u % 3].upto(g, u // 3 + 1))
                    for k in range(T):
                        i = nc.vector.scalar_tensor_tensor(out=low[:, h % 2, k, :], in0=bank[p][:, :],
                                                           scalar=vcol[:, 0, k, h:h + 1], in1=low[:, h % 2, k, :],
                                                           op0=ALU.mult, op1=ALU.max)
                        if k == T - 1:
                            i.then_inc(b_copied[p].sem, 1)
                    dve.wait_ge(*b_copied[p].upto(g, n + 1))
                    if h >= 2:
                        po, no = b_unit(V_HEAD + 3 * (h - 2) + 2)
                        dve.wait_ge(*b_filled[po].upto(g, no + 1))
                    nc.vector.tensor_tensor(p3T[:, h % 2], low[:, h % 2], edge[:, :, :], ALU.mult).then_inc(b_max.sem, 1)
                return f

            def b_head(h):
                def f(g):
                    p, n = b_unit(V_HEAD + 3 * h + 2)
                    dve.wait_ge(*b_filled[p].upto(g, n + 1))
                    o = bank[p][:, 0:T * (DH3 + 1)].rearrange("p (t d) -> p t d", d=DH3 + 1)
                    nc.vector.reciprocal(rden3[:, h % 2], o[:, :, DH3:DH3 + 1]).then_inc(b_rden.sem, 1)
                    dve.wait_ge(*b_rden.upto(g, h + 1))
                    nc.vector.tensor_tensor(att3[:, :, h * DH3:(h + 1) * DH3], o[:, :, 0:DH3],
                                            rden3[:, h % 2].broadcast_to([P, T, DH3]), ALU.mult).then_inc(b_copied[p].sem, 1)
                return f

            def b_final(g):
                dve.wait_ge(*b_copied[2].upto(g, B_FILLS))
                nc.vector.tensor_tensor(x_out[:, :, :], att3[:, :, :], x3[:, :, :], ALU.add).then_inc(b_out.sem, 1)

            second_pass(dve, {
                "a.x1": a_ln, "a.center": lambda g: shift("a", g), "a.edges": a_edges,
                "a.qlow": a_low(0, U_Q, q_high, q_low), "a.klow": a_low(1, U_K, k_high, k_low), "a.xmid": a_wo,
                "b.stats": b_ln, "b.center": lambda g: shift("b", g), "b.edges": b_edges, "b.ms": b_ms, "b.diag": b_diags,
                "b.scale": b_scale, "b.silu": b_silu, "b.x3": b_x3, "b.stats3": d_ln, "b.center3": lambda g: shift("d", g),
                "b.factors": b_factors, "b.vcol": b_vcol, "h.out": b_final,
                **{f"a.max{h}": a_max(h) for h in range(H1)}, **{f"a.vmask{h}": a_mask(h) for h in range(H1)},
                **{f"a.head{h}": a_head(h) for h in range(H1)}, **{f"h.prob{h}": b_prob(h) for h in range(H3)},
                **{f"h.head{h}": b_head(h) for h in range(H3)}})

        @block.tensor
        def _(pe):
            pe.wait_ge(weights_in.sem, n_loads * 16)
            pe.wait_ge(setup.sem, 11)

            def flip(dst, src, k):
                for t in range(T):
                    i = nc.tensor.transpose(dst[:, t * P:(t + 1) * P], src[:, t, k * P:(k + 1) * P], ident[:, :])
                return i

            def fore(g, par):
                pe.wait_ge(*c_eye.upto(g, 1))
                if not first(g):
                    pe.wait_ge(*c_deg_ok.upto(g, 0))
                for t in range(T):
                    for k in range(T):
                        i = nc.tensor.matmul(bank[0][:, t:t + 1], c_at[:, par, k, t * P:(t + 1) * P], ones[:, 0:1],
                                             start=k == 0, stop=k == T - 1)
                i.then_inc(c_deg_sum.sem, 1)

            def mid(g, par):
                pe.wait_ge(*c_hs_ok.upto(g, 1))
                if not first(g):
                    pe.wait_ge(*c_o_ok.upto(g, 0))
                for t in range(T):
                    dst = (obank if t < 2 else bank[2])[:, (t % 2) * D:(t % 2 + 1) * D]
                    for k in range(T):
                        i = nc.tensor.matmul(dst, c_at[:, par, k, t * P:(t + 1) * P], c_hs[:, k, :],
                                             start=k == 0, stop=k == T - 1)
                i.then_inc(c_agg.sem, 1)

            def back(g, par):
                pe.wait_ge(*lns["c"]["h"].upto(g, 1))
                if not first(g):
                    pe.wait_ge(*c_hT_ok.upto(g, 0))
                for k in range(K):
                    i = flip(pair[0][:, k, :], c_h, k)
                i.then_inc(c_hT_sum.sem, 1)
                pe.wait_ge(*c_hT_ok.upto(g, 1))
                if not first(g):
                    pe.wait_ge(*c_scaled.upto(g, 0))
                for t in range(T):
                    for k in range(K):
                        i = nc.tensor.matmul(pair[1][:, t // 2, (t % 2) * D:(t % 2 + 1) * D],
                                             c_hT[:, k, t * P:(t + 1) * P], w0_s[:, k, :], start=k == 0, stop=k == K - 1)
                i.then_inc(c_lin.sem, 1)

            first_pass(pe, fore, mid, back)

            for par in range(2):
                pe.wait_ge(c_added[par].sem, G)
            pe.wait_ge(*c_o_ok.upto(Graph(G), 0))
            for n, s in enumerate((sum_o, sum_sq)):
                for t in range(T):
                    i = nc.tensor.matmul(obank[:, n * D:(n + 1) * D], ones[:, :], s[:, t, :], start=t == 0, stop=t == T - 1)
                i.then_inc(c_sums.sem, 1)
            pe.wait_ge(bn_steps.sem, 7)

            def a_free(g, u):
                p, n = a_unit(u)
                if n or not first(g):
                    pe.wait_ge(*a_copied[p].upto(g, n))
                return pair[p], a_filled[p].sem

            def b_free(g, u):
                p, n = b_unit(u)
                if n or not first(g):
                    pe.wait_ge(*b_copied[p].upto(g, n))
                return bank[p], b_filled[p].sem

            def o_free(g, n):
                if n or not first(g):
                    pe.wait_ge(*o_copied.upto(g, n))
                return obank, o_filled.sem

            def a_flip(src, u, ready):
                def f(g):
                    for s, k in ready:
                        pe.wait_ge(*s.upto(g, k))
                    dst, full = a_free(g, u)
                    for k in range(K):
                        i = flip(dst[:, k, :], src, k)
                    i.then_inc(full, 1)
                return f

            def rows(dst, hT, w):
                for t in range(T):
                    for k in range(K):
                        i = nc.tensor.matmul(dst[:, t // 2, (t % 2) * D:(t % 2 + 1) * D], hT[:, k, t * P:(t + 1) * P],
                                             w[:, k, :], start=k == 0, stop=k == K - 1)
                return i

            def a_qk(u, w):
                def f(g):
                    pe.wait_ge(*a_copied[0].upto(g, 1))
                    dst, full = a_free(g, u)
                    for j in range(K):
                        for k in range(K):
                            i = nc.tensor.matmul(dst[:, j, :], w[:, k, j * P:(j + 1) * P], a_hT[:, k, :],
                                                 start=k == 0, stop=k == K - 1)
                    i.then_inc(full, 1)
                return f

            def a_v(g):
                dst, full = a_free(g, U_V)
                rows(dst, a_hT, wv_s).then_inc(full, 1)

            def a_nat(h):
                def f(g):
                    pe.wait_ge(*a_qk_in.upto(g, 24))
                    for q in range(2):
                        dst, full = a_free(g, U_NAT + 2 * h + q)
                        for b in range(2):
                            t = 2 * q + b
                            i = nc.tensor.matmul(dst[:, b, :], q_parts[0:ROW_SHIFT, h, t * P:(t + 1) * P],
                                                 k_parts[0:ROW_SHIFT, h, :], start=True, stop=True)
                        i.then_inc(full, 1)
                return f

            def a_shift(g):
                for p in range(2):
                    pe.wait_ge(*a_copied[p].upto(g, U_ST // 2))
                dst, full = o_free(g, 0)
                for t in range(T):
                    i = nc.tensor.transpose(dst[0:H1, t * P:(t + 1) * P], minus_max[:, t, :], ident[:, :])
                i.then_inc(full, 1)

            def a_scores(h):
                def f(g):
                    pe.wait_ge(*a_shift_in.upto(g, H1))
                    for q in range(2):
                        dst, full = a_free(g, U_ST + 2 * h + q)
                        for b in range(2):
                            k = 2 * q + b
                            i = nc.tensor.matmul(dst[:, b, :], k_parts[0:ROW_SHIFT + 1, h, k * P:(k + 1) * P],
                                                 q_parts[0:ROW_SHIFT + 1, h, :], start=True, stop=True)
                        i.then_inc(full, 1)
                return f

            def a_values(h):
                def f(g):
                    for i in range(2):
                        pe.wait_ge(*a_masked[i].upto(g, h + 1))
                    dst, full = o_free(g, 1 + h)
                    for t in range(T):
                        for k in range(T):
                            i = nc.tensor.matmul(dst[:, t * (DH1 + 1):(t + 1) * (DH1 + 1)], pT[:, h % 2, k, t * P:(t + 1) * P],
                                                 v1[:, k * H1 + h, :], start=k == 0, stop=k == T - 1)
                    i.then_inc(full, 1)
                return f

            def a_wo(g):
                pe.wait_ge(*a_copied[0].upto(g, A_FILLS))
                dst, full = a_free(g, U_WO)
                rows(dst, att1T, wo_s).then_inc(full, 1)

            def b_agg(g):
                pe.wait_ge(*lns["b"]["h"].upto(g, 1))
                pe.wait_ge(*b_eye.upto(g, 1))
                for j in range(K):
                    dst, full = b_free(g, V_AGG + j)
                    for k in range(T):
                        i = nc.tensor.matmul(dst[:, :], b_h[:, k, j * P:(j + 1) * P], b_at[:, k, :],
                                             start=k == 0, stop=k == T - 1)
                    i.then_inc(full, 1)

            def b_hid(n):
                def f(g):
                    for j in range(K):
                        pe.wait_ge(*b_copied[j].upto(g, 1))
                    for t in (2 * n, 2 * n + 1):
                        dst, full = b_free(g, V_HID + t)
                        for k in range(K):
                            i = nc.tensor.matmul(dst[:, :], w1_s[:, k, t * P:(t + 1) * P], aggT[:, k, :],
                                                 start=k == 0, stop=k == K - 1)
                        i.then_inc(full, 1)
                return f

            def b_ms(g):
                pe.wait_ge(*b_summed.upto(g, KH - 1))
                dst, full = b_free(g, V_MS)
                for t in range(T):
                    i = nc.tensor.matmul(dst[:, t:t + 1], hsum[:, t * P:(t + 1) * P], ones[:, 0:1], start=True, stop=True)
                i.then_inc(full, 1)

            def b_rb(g):
                pe.wait_ge(*b_diag.upto(g, 1))
                dst, full = b_free(g, V_RB)
                nc.tensor.matmul(dst[:, :], ones[:, :], diag[:, :, :].rearrange("p t n -> p (t n)"),
                                 start=True, stop=True).then_inc(full, 1)

            def b_out2(g):
                p, n = b_unit(V_RB)
                pe.wait_ge(*b_copied[p].upto(g, n + 1))
                for q in range(2):
                    dst, full = b_free(g, V_OUT + q)
                    for t in (2 * q, 2 * q + 1):
                        for k in range(KH):
                            i = nc.tensor.matmul(dst[:, (t % 2) * D:(t % 2 + 1) * D], hid[:, k, t * P:(t + 1) * P],
                                                 w2_s[:, k, :], start=k == 0, stop=k == KH - 1)
                    i.then_inc(full, 1)

            def d_flip(g):
                pe.wait_ge(*lns["d"]["h"].upto(g, 1))
                for k in range(K):
                    dst, full = b_free(g, V_HT + k)
                    flip(dst, d_h, k).then_inc(full, 1)

            def b_v3(g):
                for j in range(K):
                    p, n = b_unit(V_HT + j)
                    pe.wait_ge(*b_copied[p].upto(g, n + 1))
                for q in range(2):
                    dst, full = b_free(g, V_V3 + q)
                    for t in (2 * q, 2 * q + 1):
                        for k in range(K):
                            i = nc.tensor.matmul(dst[:, (t % 2) * D:(t % 2 + 1) * D], d_hT[:, k, t * P:(t + 1) * P],
                                                 w3_s[:, k, :], start=k == 0, stop=k == K - 1)
                    i.then_inc(full, 1)
                dst, full = b_free(g, V_E)
                for k in range(K):
                    i = nc.tensor.matmul(dst[0:ROW_LOW + H3, :], att_w[:, k, :], d_hT[:, k, :], start=k == 0, stop=k == K - 1)
                i.then_inc(full, 1)

            def b_vt(g):
                p, n = b_unit(V_E)
                pe.wait_ge(*b_copied[p].upto(g, n + 1))
                keys = slice(ROW_LOW, ROW_LOW + H3)
                for i in range(2):
                    dst, full = b_free(g, V_VT + i)
                    for t in range(T):
                        last = nc.tensor.matmul(dst[:, t * H3:(t + 1) * H3], vT[:, i, t * P:(t + 1) * P], ident[keys, keys],
                                                start=True, stop=True)
                    last.then_inc(full, 1)

            def b_spread(h):
                def f(g):
                    pe.wait_ge(*b_u_parts.upto(g, 1))
                    for s in range(2):
                        dst, full = b_free(g, V_HEAD + 3 * h + s)
                        nc.tensor.matmul(dst[:, :], sel3[:, h, :], u_parts[:, s, :], start=True, stop=True).then_inc(full, 1)
                return f

            def b_values(h):
                def f(g):
                    pe.wait_ge(*b_max.upto(g, h + 1))
                    dst, full = b_free(g, V_HEAD + 3 * h + 2)
                    w = DH3 + 1
                    for t in range(T):
                        for k in range(T):
                            i = nc.tensor.matmul(dst[:, t * w:(t + 1) * w], p3T[:, h % 2, k, t * P:(t + 1) * P],
                                                 v3[:, k * H3 + h, :], start=k == 0, stop=k == T - 1)
                    i.then_inc(full, 1)
                return f

            second_pass(pe, {
                "a.flip": a_flip(a_h, U_HT, [(lns["a"]["h"], 1)]), "a.q": a_qk(U_Q, wq_s), "a.k": a_qk(U_K, wk_s),
                "a.v": a_v, "a.shift": a_shift, "a.ot": a_flip(att1, U_OT, [(o_copied, O_FILLS)]), "a.wo": a_wo,
                "b.agg": b_agg, "b.sum": b_ms, "b.spread": b_rb, "b.out2": b_out2, "b.flip3": d_flip, "b.v3": b_v3,
                "b.vt": b_vt, **{f"a.nat{h}": a_nat(h) for h in range(H1)},
                **{f"a.scores{h}": a_scores(h) for h in range(H1)}, **{f"a.values{h}": a_values(h) for h in range(H1)},
                **{f"b.hid{i}": b_hid(i) for i in range(4)}, **{f"h.spread{h}": b_spread(h) for h in range(H3)},
                **{f"h.values{h}": b_values(h) for h in range(H3)}})


def kernel(**inputs):
    import concourse.bacc as _bacc
    from concourse.bass_utils import run_bass_kernel_spmd as _run

    i = inputs
    t2 = lambda w: w.T
    laid = {
        "x": i["x"], "adjT": i["adj"].transpose(0, 2, 1), "w0T": t2(i["L0_gnn_W"]), "b0": i["L0_gnn_b"],
        "bn_w": i["L0_gnn_bn_weight"], "bn_b": i["L0_gnn_bn_bias"], "res_w": i["L0_gnn_res_weight"].reshape(1),
        "wqT": t2(i["L1_gnn_Wq"]), "wkT": t2(i["L1_gnn_Wk"]), "wvT": t2(i["L1_gnn_Wv"]), "woT": t2(i["L1_gnn_Wo"]),
        "bo": i["L1_gnn_bo"], "eps": i["L2_gnn_epsilon"].reshape(1), "w1": i["L2_gnn_W1"],
        "b1": i["L2_gnn_b1"].reshape(KH, P).T, "rms_w": i["L2_gnn_rms_weight"].reshape(KH, P).T, "w2": i["L2_gnn_W2"],
        "b2": i["L2_gnn_b2"], "w3": i["L3_gnn_W"], "att": i["L3_gnn_a"].reshape(-1),
    }
    nc = _bacc.Bacc("TRN2", target_bir_lowering=False, num_devices=1)
    arrays = {f"in_{k}": np.ascontiguousarray(v) for k, v in laid.items()}
    aps = [nc.dram_tensor(n, a.shape, mybir.dt.from_np(a.dtype), kind="ExternalInput").ap() for n, a in arrays.items()]
    aps.append(nc.dram_tensor("out_0", (G, N, D), mybir.dt.float32, kind="ExternalOutput").ap())
    gnn_stack(nc, *aps)
    return _run(nc, [arrays], core_ids=[0]).results[0]["out_0"]
```

```python
import concourse.bass as bass
from concourse import mybir
from contextlib import ExitStack
import numpy as np

P = 128
G, N, D = 32, 512, 256
T = N // P
K = D // P
H1, DH1 = 8, 32
HID = 1024
KH = HID // P
H3, DH3 = 4, 64
LN_EPS, BN_EPS, RMS_EPS = 1e-5, 1e-5, 1e-6
SLOPE = 0.2
ROW_SHIFT = 3 * DH1
ROW_LOW = 32
A_FILLS = 18
O_FILLS = 1 + H1 // 2 + 2
B_FILLS = 11


class Signal:

    def __init__(self, sem, per, unit=1):
        self.sem, self.per, self.unit = sem, per * unit, unit

    def upto(self, g, k):
        return self.sem, g.loop * (g.step * self.per) + (g.off * self.per + k * self.unit)


class Graph:

    def __init__(self, loop, off=0, step=1):
        self.loop, self.off, self.step = loop, off, step

    def plus(self, n):
        return Graph(self.loop, self.off + n, self.step)

    def half(self):
        if isinstance(self.loop, int):
            return Graph((self.loop * self.step + self.off) // 2)
        return Graph(self.loop, self.off // 2)

    def index(self):
        return self.loop * self.step + self.off

    def below(self, n):
        return isinstance(self.loop, int) and self.index() < n


def first(g):
    return g.below(1)


ORDER = """
a.bias a.nat00 a.nat01 a.max00 a.max01 h.spread0 a.nat10 a.nat11 h.low0 a.max10 a.nat20 a.max11 a.nat21 h.prob0
h.spread1 a.max20 b.load a.max21 a.nat30 a.nat31 a.max30 a.max31 h.mask0 a.nat40 h.low1 a.max40 a.nat41 a.max41
a.nat50 a.nat51 a.max50 a.max51 a.nat60 a.nat61 a.max60 a.max61 a.nat70 a.max70 a.nat71 a.max71 a.shift a.shiftc
h.vmask0 h.values00 h.prob1 h.vmask1 a.putshift h.spread2 h.low2 a.edges h.values01 a.scores00 a.scores01 a.exp00
h.mask1 a.exp01 a.scores10 h.prob2 h.vmask2 a.scores11 a.mask0 a.exp10 a.exp11 a.mask1 h.spread3 h.mask2 a.scores20
a.scores21 h.low3 a.values00 a.exp20 a.mask2 a.load h.head0 b.stats h.values10 a.scores30 h.values11 b.rstd a.vmask0
a.vmask1 a.values01 h.prob3 h.mask3 a.exp21 a.exp30 h.head1 h.values20 b.center a.headc0 h.vmask3 a.vmask2
a.scores31 a.exp31 h.values21 h.head2 a.mask3 a.scores40 a.values10 a.exp40 b.edges h.values30 a.scores41 a.mask4
b.norm h.values31 h.head3 a.scores50 a.vmask3 b.agg0 b.aggc0 b.agg1 a.values11 b.aggc1 a.exp41 a.exp50 b.hid0
b.hidc0 a.mask5 a.headc1 b.hid1 b.hid2 b.hidc1 p.x1 b.hidc2 b.hid3 b.hid4 b.hidc3 b.hid5 p.rstd b.hidc4 h.store
b.hidc5 a.vmask4 b.sumsq1 b.sumsq2 b.sumsq3 b.hid6 p.center b.sumsq4 b.sumsq5 b.hidc6 a.div0 b.hid7 b.hidc7
a.scores51 a.scores60 a.values20 a.exp51 a.vmask5 b.sumsq6 a.scores61 b.sumsq7 b.sum p.norm a.exp60 b.ms b.rrms
a.values21 a.exp61 a.scores70 b.diag a.exp70 b.spread a.mask6 a.vmask6 b.scale0 b.scale1 b.scale2 a.mask7 a.headc2
a.scores71 b.tanh0 b.bias p.flip p.flipc a.exp71 a.values30 b.tanh1 b.silu0 b.tanh2 a.vmask7 b.scale3 p.q0 p.q1
b.tanh3 b.silu1 b.silu2 a.values31 b.silu3 b.out20 a.headc3 a.div1 p.qhigh p.qlow b.out21 b.x30 b.out22 b.out23
b.x31 b.stats3 p.k0 b.rstd3 b.center3 p.k1 p.khigh p.klow b.norm3 a.wo0 a.xmid0 p.v0 b.flip3 b.flip3c0 b.flip3c1
b.v30 b.v31 b.e b.v3c0 b.v3c1 p.v1 b.factors b.exps a.wo1 b.vt p.vc a.xmid1 b.vcol p.sortq p.sortk
""".split()


def gnn_stack(nc, x, adjT, w0T, b0, bn_w, bn_b, res_w, wqT, wkT, wvT, woT, bo, eps, w1, b1, rms_w, w2, b2,
              w3, att, out):
    f32, bf16, f32r = mybir.dt.float32, mybir.dt.bfloat16, mybir.dt.float32r
    ALU, ACT, AX = mybir.AluOpType, mybir.ActivationFunctionType, mybir.AxisListType
    ctx = ExitStack()
    with ctx:
        def sb(name, *shape, dt=f32):
            return ctx.enter_context(nc.sbuf_tensor(name, list(shape), dt))

        def signal(name, per=1, unit=1):
            return Signal(ctx.enter_context(nc.semaphore(name)), per, unit)

        pre_bn = nc.dram_tensor("pre_bn", [G, N, D], f32, kind="Internal").ap()
        x_res = nc.dram_tensor("x_res", [G, N, D], f32, kind="Internal").ap()

        def nodes(t, g):
            return t[g.index()].rearrange("(t p) d -> p t d", p=P)

        ident = sb("ident", P, P)
        ones = sb("ones", P, P)
        minus_half = sb("minus_half", P, D)
        sel3 = sb("sel3", ROW_LOW + H3, H3, P, dt=f32r)
        u_parts = sb("u_parts", ROW_LOW + H3, 2, N, dt=f32r)
        w0_s, wq_s, wk_s, wv_s, wo_s, w3_s = (sb(n, P, K, D) for n in ("w0_s", "wq_s", "wk_s", "wv_s", "wo_s", "w3_s"))
        w1_s = sb("w1_s", P, K, HID)
        w2_s = sb("w2_s", P, KH, D)
        b0_s, bo_s, b2_s, bnw_s, bnb_s = (sb(n, P, D) for n in ("b0_s", "bo_s", "b2_s", "bnw_s", "bnb_s"))
        b1_s = sb("b1_s", P, KH)
        rms_s = sb("rms_s", P, KH)
        resw_s = sb("resw_s", P, 1)
        eps_s = sb("eps_s", P, 1)
        eps_ident = sb("eps_ident", P, P)
        half_rms = sb("half_rms", P, KH)
        att_w = sb("att_w", P, K, ROW_LOW + H3)

        c_deg = sb("c_deg", P, 4, T)
        c_dis = sb("c_dis", P, 2, T)
        bn_scale = sb("bn_scale", P, D)
        bn_shift = sb("bn_shift", P, D)

        ln = {s: {n: sb(f"{s}_{n}", P, T, w) for n, w in (("st", 6), ("mv", 2), ("ve", 1), ("rs", 1), ("sh", 1))}
              for s in "cabd"}

        a_xr = sb("a_xr", P, T, D)
        a_o = sb("a_o", P, T, D)
        a_at = sb("a_at", P, T, N)
        a_xbo = sb("a_xbo", P, T, D)
        a_h = sb("a_h", P, T, D)
        a_hT = sb("a_hT", P, K, N)
        q_parts = sb("q_parts", P, H1, N, dt=f32r)
        k_parts = sb("k_parts", P, H1, N, dt=f32r)
        v1 = sb("v1", P, T * H1 // 2, 3, DH1)
        node_edge = sb("node_edge", P, T, N, dt=bf16)
        minus_max = sb("minus_max", P, T, H1)
        shiftT = sb("shiftT", H1, N, dt=f32r)
        pT = sb("pT", P, 2, T, N)
        att1T = sb("att1T", P, K, N)
        rden1 = sb("rden1", P, K, N)
        x_mid = sb("x_mid", P, T, D)

        b_at = sb("b_at", P, T, N)
        edge = sb("edge", P, T, N, dt=bf16)
        b_h = sb("b_h", P, T, D)
        aggT = sb("aggT", P, K, N)
        hid = sb("hid", P, KH, N)
        hsq = sb("hsq", P, KH, N)
        ms = sb("ms", P, T)
        rrms = sb("rrms", P, T)
        diag = sb("diag", P, T, P)
        x3 = sb("x3", P, T, D)
        v3 = sb("v3", P, T * H3, DH3 + 1)
        top = sb("top", ROW_LOW + H3, 2)
        vcol = sb("vcol", P, 2, T, H3)
        rden3 = sb("rden3", P, 2, T, 1)

        d_h, d_hT = b_h, aggT
        rows_of = lambda t, r: t[r:r + H3].rearrange("p a b -> p (a b)").rearrange("p (a b) -> p a b", a=2)
        vT, uT = rows_of(b_h, ROW_LOW), rows_of(aggT, 0)
        hsum = diag[:, :, :].rearrange("p a b -> p (a b)")
        z8 = diag[0:H3].rearrange("p a b -> p (a b)")
        x_out = x3
        parts = pT[:, :, :, :].rearrange("p a (s k) n -> p (a s) k n", k=K)
        q_high, q_low, k_high, k_low = (parts[:, i] for i in range(4))
        low = hsq[:, :, :].rearrange("p (a t) n -> p a t n", a=2)
        p3T = hid[:, :, :].rearrange("p (a t) n -> p a t n", a=2)

        att_s = x_mid[:, 0:2, :].rearrange("p a b -> p (a b)").rearrange("p (h d) -> p h d", h=H3)
        att_t = x_mid[:, 2, :].rearrange("p (h d) -> p h d", h=H3)

        def two(t, a, b):
            return t[:, a:b, :].rearrange("p (c a) (b d) -> p c (a b) d", c=2, d=D)

        c_at = pT
        c_x, c_xres = two(hid, 0, 4), two(hid, 4, 8)
        c_o, c_sq = two(hsq, 0, 4), two(hsq, 4, 8)
        c_h, c_hT, c_hs = a_h, a_hT, a_xbo
        sum_o, sum_sq, bn_t = b_h, aggT[:, :, :].rearrange("p k (b d) -> p (k b) d", d=D), x3

        pair = [ctx.enter_context(nc.psum_tensor(f"pair{i}", [P, 2, N], f32)) for i in range(2)]
        obank = ctx.enter_context(nc.psum_tensor("obank", [P, N], f32))
        bank = [ctx.enter_context(nc.psum_tensor(f"bank{i}", [P, N], f32)) for i in range(3)]

        n_loads = 18
        weights_in = signal("weights_in", n_loads, 16)
        consts = signal("consts", 13)
        setup = signal("setup", 11)

        c_x_in = [signal(f"c_x_in{i}", 1, 16) for i in range(2)]
        c_at_in = [signal(f"c_at_in{i}", 1, 16) for i in range(2)]
        c_eye = signal("c_eye")
        c_deg_sum = signal("c_deg_sum")
        c_deg_in = signal("c_deg_in", 2)
        c_deg_ok = signal("c_deg_ok")
        c_pow = signal("c_pow")
        c_dis_ok = signal("c_dis_ok")
        c_hT_sum = signal("c_hT_sum")
        c_hT_ok = signal("c_hT_ok")
        c_lin = signal("c_lin", 2)
        c_scaled = signal("c_scaled", 2)
        c_hs_ok = signal("c_hs_ok")
        c_agg = signal("c_agg")
        c_o_ok = signal("c_o_ok")
        c_sq_ok = signal("c_sq_ok")
        c_xres_ok = signal("c_xres_ok")
        c_added = [signal(f"c_added{i}", 2) for i in range(2)]
        c_o_out = [signal(f"c_o_out{i}", 1, 16) for i in range(2)]
        c_xres_out = [signal(f"c_xres_out{i}", 1, 16) for i in range(2)]
        c_sums = signal("c_sums", 2)
        bn_steps = signal("bn_steps", 6)
        bn_pow = signal("bn_pow", 1)

        lns = {s: {n: signal(f"{s}_{n}_ok", 1 + (n == "mv")) for n in ("st", "mv", "ve", "rs", "sh", "h")} for s in "cabd"}

        a_x_in = signal("a_x_in", 2, 16)
        a_at_in = signal("a_at_in", 1, 16)
        a_x1_step = signal("a_x1_step", 3)
        a_xbo_ok = signal("a_xbo_ok")
        a_mask_ok = signal("a_mask_ok")
        a_high_ok = signal("a_high_ok", 2)
        a_qk_in = signal("a_qk_in", 24, 16)
        a_shift_in = signal("a_shift_in", H1, 16)
        a_filled = [signal(f"a_filled{i}", A_FILLS) for i in range(2)]
        a_copied = [signal(f"a_copied{i}", A_FILLS) for i in range(2)]
        wo_sum = signal("wo_sum", 2)
        shift_sum = signal("shift_sum")
        o_copied = signal("o_copied", O_FILLS)
        a_used = signal("a_used", H1)
        a_rden = signal("a_rden", K)
        a_divided = signal("a_divided", K)
        a_masked = [signal(f"a_masked{i}", H1) for i in range(2)]

        b_at_in = signal("b_at_in", 1, 16)
        b_edge_ok = signal("b_edge_ok")
        b_eye = signal("b_eye")
        b_xb2_ok = signal("b_xb2_ok")
        b_filled = [signal(f"b_filled{i}", B_FILLS) for i in range(3)]
        b_copied = [signal(f"b_copied{i}", B_FILLS) for i in range(3)]
        b_summed = signal("b_summed", KH - 1)
        b_rrms = signal("b_rrms")
        b_diag = signal("b_diag")
        b_norm = signal("b_norm", KH)
        b_tanh = signal("b_tanh", KH)
        b_top = signal("b_top", 2)
        b_z8 = signal("b_z8")
        b_zz = signal("b_zz")
        b_uT = signal("b_uT", 2)
        b_u_parts = signal("b_u_parts")
        b_masked = [signal(f"b_masked{i}", H3) for i in range(2)]
        b_rden = signal("b_rden", H3)
        b_stored = signal("b_stored", 1, 16)

        def a_unit(u):
            return u % 2, u // 2

        def b_unit(u):
            return u % 3, u // 3

        U_HT, U_Q, U_K, U_V, U_NAT, U_ST = 0, 1, 2, 3, 4, 20
        V_AGG, V_HID, V_MS, V_RB, V_OUT, V_HT, V_V3, V_E, V_VT, V_HEAD = 0, 2, 10, 11, 12, 14, 16, 18, 19, 21

        def second_pass(eng, steps):
            assert set(steps) <= set(ORDER), set(steps) - set(ORDER)

            def step(at):
                for name in ORDER:
                    g = at("pabh".index(name[0]))
                    if name in steps and (not isinstance(g.loop, int) or 0 <= g.index() < G):
                        steps[name](g)

            for n in range(4):
                step(lambda lag: Graph(n - lag))
            with eng.Fori(4, G) as n:
                step(lambda lag: Graph(n, -lag))
            for n in range(G, G + 3):
                step(lambda lag: Graph(n - lag))

        def first_pass(eng, parts):
            def step(s, par):
                for ahead, part in parts:
                    g = Graph(s.loop, s.off + ahead, s.step)
                    if not isinstance(s.loop, int) or 0 <= g.index() < G:
                        part(g, (par + ahead) % 2)

            for n in range(-2, 2):
                step(Graph(n), n % 2)
            with eng.Fori(1, G // 2 - 1) as i:
                for o in range(2):
                    step(Graph(i, o, 2), o)
            for n in range(G - 2, G + 1):
                step(Graph(n), n % 2)

        block = ctx.enter_context(nc.Block())

        @block.sync
        def _(sp):
            def bcast(v, n):
                return v.rearrange("(a n) -> a n", a=1).broadcast_to([P, n])

            loads = [(w, s[:, :, :]) for w, s in ((w0T, w0_s), (wqT, wq_s), (wkT, wk_s), (wvT, wv_s), (woT, wo_s),
                                                  (w3, w3_s), (w1, w1_s), (w2, w2_s))]
            for w, s in loads:
                sp.dma_start(s, w.rearrange("(k p) n -> p k n", p=P)).then_inc(weights_in.sem, 16)
            for v, s in ((b0, b0_s), (bo, bo_s), (b2, b2_s), (bn_w, bnw_s), (bn_b, bnb_s)):
                sp.dma_start(s[:, :], bcast(v, D)).then_inc(weights_in.sem, 16)
            sp.dma_start(resw_s[:, :], bcast(res_w, 1)).then_inc(weights_in.sem, 16)
            sp.dma_start(eps_s[:, :], bcast(eps, 1)).then_inc(weights_in.sem, 16)
            sp.dma_start(b1_s[:, :], b1).then_inc(weights_in.sem, 16)
            sp.dma_start(rms_s[:, :], rms_w).then_inc(weights_in.sem, 16)
            sp.dma_start(att_s[:, :, :].rearrange("p h d -> p (h d)"), bcast(att, H3 * 2 * DH3)).then_inc(weights_in.sem, 16)

            def load_x(g, par):
                if not g.below(2):
                    sp.wait_ge(*c_xres_ok.upto(g.plus(-1), 0))
                sp.dma_start(c_x[:, par], nodes(x, g)).then_inc(c_x_in[par].sem, 16)

            def load_at(g, par):
                if not g.below(2):
                    sp.wait_ge(*c_agg.upto(g.plus(-1), 0))
                sp.dma_start(c_at[:, par], nodes(adjT, g)).then_inc(c_at_in[par].sem, 16)

            def store_res(g, par):
                sp.wait_ge(*c_xres_ok.upto(g, 1))
                sp.dma_start(nodes(x_res, g), c_xres[:, par]).then_inc(c_xres_out[par].sem, 16)

            def store_o(g, par):
                sp.wait_ge(*c_o_ok.upto(g, 1))
                sp.dma_start(nodes(pre_bn, g), c_o[:, par]).then_inc(c_o_out[par].sem, 16)

            first_pass(sp, [(2, load_x), (1, load_at), (-1, store_o), (1, store_res)])
            for par in range(2):
                sp.wait_ge(c_o_out[par].sem, G // 2 * 16)
                sp.wait_ge(c_xres_out[par].sem, G // 2 * 16)

            def load_a(g):
                if not first(g):
                    sp.wait_ge(*lns["a"]["h"].upto(g, 0))
                    sp.wait_ge(*a_xbo_ok.upto(g, 0))
                sp.dma_start(a_o[:, :, :], nodes(pre_bn, g)).then_inc(a_x_in.sem, 16)
                sp.dma_start(a_xr[:, :, :], nodes(x_res, g)).then_inc(a_x_in.sem, 16)
                if not first(g):
                    sp.wait_ge(*a_mask_ok.upto(g, 0))
                sp.dma_start(a_at[:, :, :], nodes(adjT, g)).then_inc(a_at_in.sem, 16)

            def load_b(g):
                if not first(g):
                    sp.wait_ge(*b_filled[1].upto(g.plus(-1), 1))
                sp.dma_start(b_at[:, :, :], nodes(adjT, g)).then_inc(b_at_in.sem, 16)

            def store(g):
                sp.wait_ge(*b_copied[2].upto(g, B_FILLS))
                sp.dma_start(nodes(out, g), x_out[:, :, :]).then_inc(b_stored.sem, 16)

            def sort_parts(u, dst, srcs):
                def f(g):
                    r = DH1
                    p, n = a_unit(u)
                    sp.wait_ge(*a_copied[p].upto(g, n + 1))
                    for c, src in enumerate(srcs):
                        for i in range(P // r):
                            sp.dma_start(dst[c * r:(c + 1) * r, i::P // r, :].bitcast(f32),
                                         src[i * r:(i + 1) * r]).then_inc(a_qk_in.sem, 16)
                return f

            def put_shift(g):
                sp.wait_ge(*o_copied.upto(g, 1))
                for h in range(H1):
                    sp.dma_start(q_parts[ROW_SHIFT:ROW_SHIFT + 1, h, :].bitcast(f32),
                                 shiftT[h:h + 1, :].bitcast(f32)).then_inc(a_shift_in.sem, 16)

            def load_next(g):
                if not isinstance(g.loop, int) or g.below(G - 1):
                    load_a(g.plus(1))

            load_a(Graph(0))
            second_pass(sp, {
                "a.load": load_next, "b.load": load_b,
                "p.sortq": sort_parts(U_Q, q_parts, (q_high, q_high, q_low)),
                "p.sortk": sort_parts(U_K, k_parts, (k_high, k_low, k_high)),
                "a.putshift": put_shift, "h.store": store})
            sp.wait_ge(b_stored.sem, G * 16)

        @block.gpsimd
        def _(pool):
            nc.gpsimd.memset(ident[:, :], 0.0).then_inc(consts.sem, 1)
            nc.gpsimd.memset(ones[:, :], 1.0).then_inc(consts.sem, 1)
            nc.gpsimd.memset(minus_half[:, :], -0.5).then_inc(consts.sem, 1)
            nc.gpsimd.memset(sel3[:, :, :].bitcast(f32), 0.0).then_inc(consts.sem, 1)
            nc.gpsimd.memset(sum_o[:, :, :], 0.0).then_inc(consts.sem, 1)
            nc.gpsimd.memset(sum_sq[:, :, :], 0.0).then_inc(consts.sem, 1)
            nc.gpsimd.memset(v1[:, :, 1, :], 1.0).then_inc(consts.sem, 1)
            nc.gpsimd.memset(v3[:, :, DH3:DH3 + 1], 1.0).then_inc(consts.sem, 1)
            pool.wait_ge(consts.sem, 8)
            nc.gpsimd.memset(k_parts[ROW_SHIFT:ROW_SHIFT + 1, :, :].bitcast(f32), 1.0).then_inc(consts.sem, 1)
            pool.wait_ge(consts.sem, 9)
            for n, r in enumerate((0, ROW_LOW)):
                rows = sel3[r:r + H3, :, :]
                pool.wait_ge(consts.sem, 9 + n)
                nc.gpsimd.affine_select(out=rows, in_=rows.bitcast(f32), compare_op=ALU.not_equal, fill=1.0, base=0,
                                        pattern=[[-1, H3], [0, P]], channel_multiplier=1).then_inc(consts.sem, 1)
            pool.wait_ge(consts.sem, 11)
            nc.gpsimd.memset(u_parts[:, :, :].bitcast(f32), 0.0).then_inc(consts.sem, 1)
            pool.wait_ge(consts.sem, 12)
            nc.gpsimd.affine_select(out=ident[:, :], in_=ident[:, :], compare_op=ALU.not_equal, fill=1.0, base=0,
                                    pattern=[[-1, P]], channel_multiplier=1).then_inc(consts.sem, 1)
            pool.wait_ge(consts.sem, 13)

            def power(out_ap, in_ap, n):
                return nc.gpsimd.tensor_tensor(out_ap, in_ap, minus_half[:, 0:n], ALU.pow)

            def rstd(s, g):
                pool.wait_ge(*lns[s]["ve"].upto(g, 1))
                power(ln[s]["rs"][:, :, 0], ln[s]["ve"][:, :, 0], T).then_inc(lns[s]["rs"].sem, 1)

            def add_o(g, par):
                pool.wait_ge(*c_o_ok.upto(g, 1))
                if not first(g):
                    pool.wait_ge(*c_added[1 - par].upto(g.half(), 2 * par))
                nc.gpsimd.tensor_tensor(sum_o[:, :, :], sum_o[:, :, :], c_o[:, par], ALU.add).then_inc(c_added[par].sem, 1)

            def add_sq(g, par):
                pool.wait_ge(*c_sq_ok.upto(g, 1))
                nc.gpsimd.tensor_tensor(sum_sq[:, :, :], sum_sq[:, :, :], c_sq[:, par], ALU.add).then_inc(c_added[par].sem, 1)

            def degree_power(g, par):
                pool.wait_ge(*c_deg_ok.upto(g, 1))
                power(c_deg[:, 3, :], c_deg[:, 1, :], T).then_inc(c_pow.sem, 1)

            first_pass(pool, [(-1, add_o), (-1, add_sq), (2, lambda g, par: rstd("c", g)), (1, degree_power)])
            pool.wait_ge(bn_steps.sem, 4)
            nc.gpsimd.tensor_tensor(bn_t[:, 3, :], bn_t[:, 2, :], minus_half[:, :], ALU.pow).then_inc(bn_pow.sem, 1)

            def a_bias(g):
                pool.wait_ge(*a_x1_step.upto(g, 3))
                if not first(g):
                    pool.wait_ge(*o_copied.upto(g, 0))
                nc.gpsimd.tensor_tensor(a_xbo[:, :, :], a_o[:, :, :], bo_s[:, None, :].broadcast_to([P, T, D]),
                                        ALU.add).then_inc(a_xbo_ok.sem, 1)

            def b_bias(g):
                pool.wait_ge(*lns["b"]["h"].upto(g, 1))
                nc.gpsimd.tensor_tensor(x_mid[:, :, :], x_mid[:, :, :], b2_s[:, None, :].broadcast_to([P, T, D]),
                                        ALU.add).then_inc(b_xb2_ok.sem, 1)

            def b_ms(g):
                pool.wait_ge(*b_copied[V_MS % 3].upto(g, V_MS // 3 + 1))
                power(rrms[:, :], ms[:, :], T).then_inc(b_rrms.sem, 1)

            def a_mask(h):
                def f(g):
                    pool.wait_ge(*a_copied[0].upto(g, U_ST // 2 + h + 1))
                    pool.wait_ge(*a_mask_ok.upto(g, 1))
                    half = pT[:, h % 2, 0:2]
                    nc.gpsimd.tensor_tensor(half, half, node_edge[:, 0:2, :], ALU.mult).then_inc(a_masked[0].sem, 1)
                return f

            def b_mask(h):
                def f(g):
                    p, n = b_unit(V_HEAD + 3 * h)
                    pool.wait_ge(*b_copied[p].upto(g, n + 1))
                    if h >= 2:
                        po, no = b_unit(V_HEAD + 3 * (h - 2) + 2)
                        pool.wait_ge(*b_filled[po].upto(g, no + 1))
                    half = slice(0, 2)
                    nc.gpsimd.tensor_tensor(p3T[:, h % 2, half], low[:, h % 2, half], edge[:, half, :],
                                            ALU.mult).then_inc(b_masked[0].sem, 1)
                return f

            def b_sumsq(t):
                def f(g):
                    for done in ((0, 1) if t == 1 else (t,)):
                        p, n = b_unit(V_HID + done)
                        pool.wait_ge(*b_copied[p].upto(g, n + 1))
                    if t > 1:
                        pool.wait_ge(*b_summed.upto(g, t - 1))
                    nc.gpsimd.tensor_tensor(hsum[:, :], hsum[:, :] if t > 1 else hsq[:, 0, :], hsq[:, t, :],
                                            ALU.add).then_inc(b_summed.sem, 1)
                return f

            second_pass(pool, {
                "p.rstd": lambda g: rstd("a", g), "b.rstd": lambda g: rstd("b", g), "b.rstd3": lambda g: rstd("d", g),
                "a.bias": a_bias, "b.bias": b_bias, "b.rrms": b_ms,
                **{f"a.mask{h}": a_mask(h) for h in range(H1)}, **{f"b.sumsq{t}": b_sumsq(t) for t in range(1, KH)},
                **{f"h.mask{h}": b_mask(h) for h in range(H3)}})

        @block.scalar
        def _(act):
            def normalise(s, g, dst, src, wait=None):
                act.wait_ge(*lns[s]["sh"].upto(g, 1))
                for t in range(T):
                    i = nc.scalar.activation(dst[:, t, :], src[:, t, :], ACT.Relu, bias=ln[s]["sh"][:, t, :],
                                             scale=ln[s]["rs"][:, t, :])
                i.then_inc(lns[s]["h"].sem, 1)

            def norm(g, par):
                if not first(g):
                    act.wait_ge(*c_xres_ok.upto(g, 0))
                normalise("c", g, c_h, c_x[:, par, :, :])

            def scale_o(g, par):
                act.wait_ge(*c_agg.upto(g, 1))
                if not g.below(2):
                    act.wait_ge(*c_o_out[par].upto(g.half(), 0))
                    act.wait_ge(*c_added[par].upto(g.half(), 0))
                for t in range(T):
                    src = (obank if t < 2 else bank[2])[:, (t % 2) * D:(t % 2 + 1) * D]
                    i = nc.scalar.activation(c_o[:, par, t, :], src, ACT.Copy, scale=c_dis[:, par, t:t + 1])
                i.then_inc(c_o_ok.sem, 1)

            def square(g, par):
                act.wait_ge(*c_o_ok.upto(g, 1))
                nc.scalar.activation(c_sq[:, par], c_o[:, par], ACT.Square).then_inc(c_sq_ok.sem, 1)

            def copy_hT(g, par):
                act.wait_ge(*c_hT_sum.upto(g, 1))
                nc.scalar.activation(c_hT[:, :, :], pair[0][:, :, :], ACT.Copy).then_inc(c_hT_ok.sem, 1)

            def scale_lin(g, par):
                act.wait_ge(*c_dis_ok.upto(g, 1))
                if not first(g):
                    act.wait_ge(*c_agg.upto(g, 0))
                for q in range(2):
                    act.wait_ge(*c_lin.upto(g, q + 1))
                    for t in (2 * q, 2 * q + 1):
                        i = nc.scalar.activation(c_hs[:, t, :], pair[1][:, t // 2, (t % 2) * D:(t % 2 + 1) * D], ACT.Copy,
                                                 scale=c_dis[:, par, t:t + 1])
                    i.then_inc(c_scaled.sem, 1)

            first_pass(act, [(-1, scale_o), (0, scale_lin), (1, copy_hT), (-1, square), (2, norm)])

            def a_take(g, u, dst, func=ACT.Copy, **more):
                p, n = a_unit(u)
                act.wait_ge(*a_filled[p].upto(g, n + 1))
                nc.scalar.activation(dst, pair[p][:, :, :], func, **more).then_inc(a_copied[p].sem, 1)

            def a_high(i, u, high):
                def f(g):
                    p, n = a_unit(u)
                    act.wait_ge(*a_filled[p].upto(g, n + 1))
                    if not first(g):
                        act.wait_ge(*a_used.upto(g, 0))
                    nc.scalar.activation(high.bitcast(f32r), pair[p][:, :, :], ACT.Copy).then_inc(a_high_ok.sem, 1)
                return f

            def a_v(g):
                p, n = a_unit(U_V)
                act.wait_ge(*a_filled[p].upto(g, n + 1))
                if not first(g):
                    act.wait_ge(*a_used.upto(g, 0))
                nc.scalar.activation(v1[:, :, 0::2, :], pair[p][:, :, :].rearrange("p a (h c d) -> p (a h) c d", c=2, d=DH1),
                                     ACT.Copy).then_inc(a_copied[p].sem, 1)

            def a_shift(g):
                act.wait_ge(*shift_sum.upto(g, 1))
                nc.scalar.activation(shiftT[:, :], obank[0:H1, :], ACT.Copy).then_inc(o_copied.sem, 1)

            def a_exp(h, q):
                def f(g):
                    if h >= 2:
                        act.wait_ge(*a_used.upto(g, 2 * (h // 2 - 1) + q + 1))
                    a_take(g, U_ST + 2 * h + q, pT[:, h % 2, 2 * q:2 * q + 2, :], ACT.Exp, scale=DH1 ** -0.5)
                return f

            def a_head(n):
                def f(g):
                    act.wait_ge(*a_used.upto(g, 2 * n + 2))
                    for i, (out_row, sum_row) in enumerate(((0, DH1), (3 * DH1, 2 * DH1))):
                        h = 2 * n + i
                        to = slice(h * DH1 % P, h * DH1 % P + DH1)
                        nc.scalar.activation(att1T[to, h * DH1 // P, :], obank[out_row:out_row + DH1, :], ACT.Copy)
                        last = nc.scalar.activation(rden1[to, h * DH1 // P, :], obank[sum_row:sum_row + DH1, :], ACT.Copy)
                    last.then_inc(o_copied.sem, 1)
                return f

            def b_take(g, u, dst, func=ACT.Copy, src=None, **more):
                p, n = b_unit(u)
                act.wait_ge(*b_filled[p].upto(g, n + 1))
                nc.scalar.activation(dst, bank[p][:, :] if src is None else src, func, **more).then_inc(b_copied[p].sem, 1)

            def b_hid(t):
                def f(g):
                    p, n = b_unit(V_HID + t)
                    act.wait_ge(*b_filled[p].upto(g, n + 1))
                    nc.scalar.activation(hid[:, t, :], bank[p][:, :], ACT.Identity, bias=b1_s[:, t:t + 1])
                    nc.scalar.activation(hsq[:, t, :], bank[p][:, :], ACT.Square,
                                         bias=b1_s[:, t:t + 1]).then_inc(b_copied[p].sem, 1)
                return f

            def b_tanhs(n):
                def f(g):
                    for t in (2 * n, 2 * n + 1):
                        act.wait_ge(*b_norm.upto(g, t + 1))
                        nc.scalar.activation(hsq[:, t, :], hid[:, t, :], ACT.Tanh,
                                             scale=half_rms[:, t:t + 1]).then_inc(b_tanh.sem, 1)
                return f

            def b_v3(i):
                def f(g):
                    b_take(g, V_V3 + i, v3[:, 2 * H3 * i:2 * H3 * (i + 1), 0:DH3],
                           src=bank[(V_V3 + i) % 3][:, :].rearrange("p (h d) -> p h d", d=DH3))
                return f

            def b_copy(u, dst, j):
                return lambda g: b_take(g, u + j, dst[:, j, :])

            def b_exps(g):
                act.wait_ge(*b_top.upto(g, 2))
                keys = slice(ROW_LOW, ROW_LOW + H3)
                nc.scalar.activation(vT[:, 0, :], bank[V_E % 3][keys, :], ACT.Exp, bias=top[keys, 0:1])
                nc.scalar.activation(vT[:, 1, :], bank[V_E % 3][keys, :], ACT.Exp, bias=top[keys, 1:2],
                                     scale=SLOPE).then_inc(b_copied[V_E % 3].sem, 1)
                act.wait_ge(*b_zz.upto(g, 1))
                nc.scalar.activation(uT[:, :, :], uT[:, :, :], ACT.Exp).then_inc(b_uT.sem, 1)
                act.wait_ge(*b_uT.upto(g, 1))
                nc.scalar.activation(u_parts[0:H3], uT[:, :, :], ACT.Copy).then_inc(b_uT.sem, 1)

            def b_low3(h):
                def f(g):
                    p, n = b_unit(V_HEAD + 3 * h + 1)
                    act.wait_ge(*b_filled[p].upto(g, n + 1))
                    for u in (V_VT, V_VT + 1):
                        act.wait_ge(*b_copied[u % 3].upto(g, u // 3 + 1))
                    if h >= 2:
                        for i in range(2):
                            act.wait_ge(*b_masked[i].upto(g, h - 1))
                    for k in range(T):
                        i = nc.scalar.activation(low[:, h % 2, k, :], bank[p][:, :], ACT.Copy, scale=vcol[:, 1, k, h:h + 1])
                    i.then_inc(b_copied[p].sem, 1)
                return f

            second_pass(act, {
                "p.norm": lambda g: normalise("a", g, a_h, a_o), "b.norm": lambda g: normalise("b", g, b_h, x_mid),
                "b.norm3": lambda g: normalise("d", g, d_h, x3),
                "p.flipc": lambda g: a_take(g, U_HT, a_hT[:, :, :]), "p.qhigh": a_high(0, U_Q, q_high),
                "p.khigh": a_high(1, U_K, k_high), "p.vc": a_v, "a.shiftc": a_shift,
                **{f"a.exp{h}{q}": a_exp(h, q) for h in range(H1) for q in range(2)},
                **{f"b.aggc{j}": b_copy(V_AGG, aggT, j) for j in range(K)},
                **{f"b.hidc{t}": b_hid(t) for t in range(KH)}, **{f"b.tanh{n}": b_tanhs(n) for n in range(4)},
                **{f"b.flip3c{j}": b_copy(V_HT, d_hT, j) for j in range(K)}, **{f"b.v3c{i}": b_v3(i) for i in range(2)},
                **{f"a.headc{n}": a_head(n) for n in range(H1 // 2)}, "b.exps": b_exps, **{f"h.low{h}": b_low3(h) for h in range(H3)}})

        @block.vector
        def _(dve):
            dve.wait_ge(weights_in.sem, n_loads * 16)
            dve.wait_ge(consts.sem, 13)
            nc.vector.tensor_scalar(eps_ident[:, :], ident[:, :], eps_s[:, 0:1], None, ALU.mult).then_inc(setup.sem, 1)
            nc.vector.tensor_scalar(half_rms[:, :], rms_s[:, :], 0.5, None, ALU.mult).then_inc(setup.sem, 1)
            dve.wait_ge(setup.sem, 2)
            for t in range(KH):
                nc.vector.tensor_scalar(w2_s[:, t, :], w2_s[:, t, :], half_rms[:, t:t + 1], None, ALU.mult)
            nc.vector.memset(att_w[:, :, :], 0.0).then_inc(setup.sem, 1)
            dve.wait_ge(setup.sem, 3)
            n = 3
            for s in range(2):
                for k in range(K):
                    if n > 3:
                        dve.wait_ge(setup.sem, n)
                    nc.vector.tensor_tensor(att_t[:, :, :], w3_s[:, k, :].rearrange("p (h d) -> p h d", d=DH3),
                                            att_s[:, :, s * DH3:(s + 1) * DH3], ALU.mult).then_inc(setup.sem, 1)
                    dve.wait_ge(setup.sem, n + 1)
                    nc.vector.tensor_reduce(att_w[:, k, s * ROW_LOW:s * ROW_LOW + H3], att_t[:, :, :], AX.X, ALU.add).then_inc(setup.sem, 1)
                    n += 2

            def stats(s, g, src):
                for t in range(T):
                    i = nc.vector.bn_stats(out=ln[s]["st"][:, t, :], in_=src[:, t, :])
                i.then_inc(lns[s]["st"].sem, 1)
                dve.wait_ge(*lns[s]["st"].upto(g, 1))
                st, mv, q4 = ln[s]["st"], ln[s]["mv"], ln[s]["rs"]
                nc.vector.tensor_tensor(mv[:, :, 0], st[:, :, 1], st[:, :, 4], ALU.add)
                nc.vector.scalar_tensor_tensor(out=mv[:, :, 1], in0=st[:, :, 2], scalar=D * LN_EPS, in1=st[:, :, 5],
                                               op0=ALU.add, op1=ALU.add)
                nc.vector.tensor_tensor(ln[s]["sh"][:, :, 0], st[:, :, 1], st[:, :, 4],
                                        ALU.subtract).then_inc(lns[s]["mv"].sem, 1)
                dve.wait_ge(*lns[s]["mv"].upto(g, 1))
                nc.vector.scalar_tensor_tensor(out=q4[:, :, 0], in0=ln[s]["sh"][:, :, 0], scalar=0.25,
                                               in1=ln[s]["sh"][:, :, 0], op0=ALU.mult,
                                               op1=ALU.mult).then_inc(lns[s]["mv"].sem, 1)
                dve.wait_ge(*lns[s]["mv"].upto(g, 2))
                nc.vector.scalar_tensor_tensor(out=ln[s]["ve"][:, :, 0], in0=mv[:, :, 1], scalar=1.0 / D,
                                               in1=q4[:, :, 0], op0=ALU.mult, op1=ALU.add).then_inc(lns[s]["ve"].sem, 1)

            def shift(s, g):
                dve.wait_ge(*lns[s]["rs"].upto(g, 1))
                nc.vector.scalar_tensor_tensor(out=ln[s]["sh"][:, :, 0], in0=ln[s]["mv"][:, :, 0], scalar=-0.5,
                                               in1=ln[s]["rs"][:, :, 0], op0=ALU.mult,
                                               op1=ALU.mult).then_inc(lns[s]["sh"].sem, 1)

            def eye(g, par):
                dve.wait_ge(*c_at_in[par].upto(g.half(), 1))
                for t in range(T):
                    d = c_at[:, par, t, t * P:(t + 1) * P]
                    i = nc.vector.tensor_tensor(d, d, ident[:, :], ALU.add)
                i.then_inc(c_eye.sem, 1)

            def c_stats(g, par):
                if not first(g):
                    dve.wait_ge(*lns["c"]["h"].upto(g, 0))
                dve.wait_ge(*c_x_in[par].upto(g.half(), 1))
                stats("c", g, c_x[:, par, :, :])

            def degrees(g, par):
                dve.wait_ge(*c_deg_sum.upto(g, 1))
                nc.vector.tensor_scalar(c_deg[:, 0, :], bank[0][:, 0:T], 0.0, None, ALU.is_equal).then_inc(c_deg_in.sem, 1)
                dve.wait_ge(*c_deg_in.upto(g, 1))
                nc.vector.tensor_scalar(c_deg[:, 2, :], c_deg[:, 0, :], -1.0, 1.0, ALU.mult, ALU.add).then_inc(c_deg_in.sem, 1)
                nc.vector.tensor_tensor(c_deg[:, 1, :], bank[0][:, 0:T], c_deg[:, 0, :], ALU.add).then_inc(c_deg_ok.sem, 1)
                dve.wait_ge(*c_pow.upto(g, 1))
                dve.wait_ge(*c_deg_in.upto(g, 2))
                nc.vector.tensor_tensor(c_dis[:, par, :], c_deg[:, 3, :], c_deg[:, 2, :], ALU.mult).then_inc(c_dis_ok.sem, 1)

            def residual(g, par):
                dve.wait_ge(*lns["c"]["h"].upto(g, 1))
                if not g.below(2):
                    dve.wait_ge(*c_xres_out[par].upto(g.half(), 0))
                nc.vector.scalar_tensor_tensor(out=c_xres[:, par], in0=c_h[:, :, :], scalar=resw_s[:, 0:1],
                                               in1=c_x[:, par], op0=ALU.mult, op1=ALU.add).then_inc(c_xres_ok.sem, 1)

            def bias_lin(g, par):
                for q in range(2):
                    dve.wait_ge(*c_scaled.upto(g, q + 1))
                    for t in (2 * q, 2 * q + 1):
                        i = nc.vector.scalar_tensor_tensor(out=c_hs[:, t, :], in0=b0_s[:, :], scalar=c_dis[:, par, t:t + 1],
                                                           in1=c_hs[:, t, :], op0=ALU.mult, op1=ALU.add)
                i.then_inc(c_hs_ok.sem, 1)

            first_pass(dve, [(0, bias_lin), (1, residual), (1, eye), (2, c_stats), (2, lambda g, par: shift("c", g)),
                             (1, degrees)])

            dve.wait_ge(c_sums.sem, 2)
            rows = 1.0 / (G * N)
            mean, var = bn_t[:, 0, :], bn_t[:, 2, :]
            nc.vector.tensor_scalar(mean, obank[:, 0:D], rows, None, ALU.mult).then_inc(bn_steps.sem, 1)
            dve.wait_ge(bn_steps.sem, 1)
            nc.vector.tensor_tensor(bn_t[:, 1, :], mean, mean, ALU.mult).then_inc(bn_steps.sem, 1)
            dve.wait_ge(bn_steps.sem, 2)
            nc.vector.scalar_tensor_tensor(out=var, in0=obank[:, D:2 * D], scalar=rows, in1=bn_t[:, 1, :], op0=ALU.mult,
                                           op1=ALU.subtract).then_inc(bn_steps.sem, 1)
            dve.wait_ge(bn_steps.sem, 3)
            nc.vector.tensor_scalar(var, var, 0.0, BN_EPS, ALU.max, ALU.add).then_inc(bn_steps.sem, 1)
            dve.wait_ge(bn_pow.sem, 1)
            nc.vector.tensor_tensor(bn_scale[:, :], bn_t[:, 3, :], bnw_s[:, :], ALU.mult).then_inc(bn_steps.sem, 1)
            dve.wait_ge(bn_steps.sem, 5)
            nc.vector.tensor_tensor(bn_t[:, 1, :], mean, bn_scale[:, :], ALU.mult).then_inc(bn_steps.sem, 1)
            dve.wait_ge(bn_steps.sem, 6)
            nc.vector.tensor_tensor(bn_shift[:, :], bnb_s[:, :], bn_t[:, 1, :], ALU.subtract).then_inc(bn_steps.sem, 1)
            dve.wait_ge(bn_steps.sem, 7)

            def a_ln(g):
                wide = [P, T, D]
                dve.wait_ge(*a_x_in.upto(g, 2))
                if not first(g):
                    dve.wait_ge(*lns["a"]["h"].upto(g, 0))
                nc.vector.tensor_tensor(a_o[:, :, :], a_o[:, :, :], bn_scale[:, None, :].broadcast_to(wide),
                                        ALU.mult).then_inc(a_x1_step.sem, 1)
                dve.wait_ge(*a_x1_step.upto(g, 1))
                nc.vector.tensor_tensor(a_o[:, :, :], a_o[:, :, :], bn_shift[:, None, :].broadcast_to(wide),
                                        ALU.add).then_inc(a_x1_step.sem, 1)
                dve.wait_ge(*a_x1_step.upto(g, 2))
                nc.vector.scalar_tensor_tensor(out=a_o[:, :, :], in0=a_o[:, :, :], scalar=0.0, in1=a_xr[:, :, :],
                                               op0=ALU.max, op1=ALU.add).then_inc(a_x1_step.sem, 1)
                dve.wait_ge(*a_x1_step.upto(g, 3))
                stats("a", g, a_o)

            def a_edges(g):
                dve.wait_ge(*a_at_in.upto(g, 1))
                nc.vector.tensor_scalar(node_edge[:, :, :], a_at[:, :, :], 0.0, None, ALU.not_equal).then_inc(a_mask_ok.sem, 1)

            def a_low(i, u, high, low_part):
                def f(g):
                    p, n = a_unit(u)
                    dve.wait_ge(*a_high_ok.upto(g, i + 1))
                    nc.vector.tensor_tensor(low_part.bitcast(f32r), pair[p][:, :, :], high,
                                            ALU.subtract).then_inc(a_copied[p].sem, 1)
                return f

            def a_mask(h):
                def f(g):
                    dve.wait_ge(*a_copied[1].upto(g, U_ST // 2 + h + 1))
                    dve.wait_ge(*a_mask_ok.upto(g, 1))
                    half = pT[:, h % 2, 2:4]
                    nc.vector.tensor_tensor(half, half, node_edge[:, 2:4, :], ALU.mult).then_inc(a_masked[1].sem, 1)
                return f

            def a_max(h, q):
                def f(g):
                    p, n = a_unit(U_NAT + 2 * h + q)
                    dve.wait_ge(*a_filled[p].upto(g, n + 1))
                    nc.vector.tensor_reduce(minus_max[:, 2 * q:2 * q + 2, h], pair[p][:, :, :], AX.X, ALU.max,
                                            negate=True).then_inc(a_copied[p].sem, 1)
                return f

            def a_div(k):
                def f(g):
                    dve.wait_ge(*o_copied.upto(g, 1 + H1 // 4 * (k + 1)))
                    nc.vector.reciprocal(rden1[:, k, :], rden1[:, k, :]).then_inc(a_rden.sem, 1)
                    dve.wait_ge(*a_rden.upto(g, k + 1))
                    nc.vector.tensor_tensor(att1T[:, k, :], att1T[:, k, :], rden1[:, k, :], ALU.mult).then_inc(a_divided.sem, 1)
                return f

            def a_wo(q):
                def f(g):
                    dve.wait_ge(*wo_sum.upto(g, q + 1))
                    dve.wait_ge(*a_xbo_ok.upto(g, 1))
                    if not first(g):
                        p, n = b_unit(V_OUT + q)
                        dve.wait_ge(*b_copied[p].upto(g.plus(-1), n + 1))
                    half = slice(2 * q, 2 * q + 2)
                    nc.vector.tensor_tensor(x_mid[:, half, :], obank[:, :].rearrange("p (b d) -> p b d", d=D),
                                            a_xbo[:, half, :], ALU.add).then_inc(o_copied.sem, 1)
                return f

            def b_ln(g):
                dve.wait_ge(*o_copied.upto(g, O_FILLS))
                stats("b", g, x_mid)

            def b_edges(g):
                dve.wait_ge(*b_at_in.upto(g, 1))
                if not first(g):
                    dve.wait_ge(*b_masked[0].upto(g, 0))
                nc.vector.tensor_scalar(edge[:, :, :], b_at[:, :, :], 0.0, None, ALU.is_gt).then_inc(b_edge_ok.sem, 1)
                dve.wait_ge(*b_edge_ok.upto(g, 1))
                for t in range(T):
                    d = b_at[:, t, t * P:(t + 1) * P]
                    i = nc.vector.tensor_tensor(d, d, eps_ident[:, :], ALU.add)
                i.then_inc(b_eye.sem, 1)

            def b_ms(g):
                p, n = b_unit(V_MS)
                dve.wait_ge(*b_filled[p].upto(g, n + 1))
                nc.vector.tensor_scalar(ms[:, :], bank[p][:, 0:T], 1.0 / HID, RMS_EPS, ALU.mult,
                                        ALU.add).then_inc(b_copied[p].sem, 1)

            def b_diags(g):
                dve.wait_ge(*b_rrms.upto(g, 1))
                for t in range(T):
                    i = nc.vector.tensor_scalar(diag[:, t, :], ident[:, :], rrms[:, t:t + 1], None, ALU.mult)
                i.then_inc(b_diag.sem, 1)

            def b_scale(n):
                def f(g):
                    p, c = b_unit(V_RB)
                    dve.wait_ge(*b_filled[p].upto(g, c + 1))
                    for t in (2 * n, 2 * n + 1):
                        nc.vector.tensor_tensor(hid[:, t, :], hid[:, t, :], bank[p][:, :], ALU.mult).then_inc(b_norm.sem, 1)
                return f

            def b_silu(n):
                def f(g):
                    for t in (2 * n, 2 * n + 1):
                        dve.wait_ge(*b_tanh.upto(g, t + 1))
                        i = nc.vector.scalar_tensor_tensor(out=hid[:, t, :], in0=hsq[:, t, :], scalar=1.0,
                                                           in1=hid[:, t, :], op0=ALU.add, op1=ALU.mult)
                    if n == 3:
                        i.then_inc(b_copied[V_RB % 3].sem, 1)
                return f

            def b_x3(q):
                def f(g):
                    dve.wait_ge(*b_xb2_ok.upto(g, 1))
                    if not first(g):
                        dve.wait_ge(*b_stored.upto(g, 0))
                    p, n = b_unit(V_OUT + q)
                    dve.wait_ge(*b_filled[p].upto(g, n + 1))
                    nc.vector.tensor_tensor(x3[:, 2 * q:2 * q + 2, :], bank[p][:, :].rearrange("p (b d) -> p b d", d=D),
                                            x_mid[:, 2 * q:2 * q + 2, :], ALU.add).then_inc(b_copied[p].sem, 1)
                return f

            def d_ln(g):
                for q in range(2):
                    p, n = b_unit(V_OUT + q)
                    dve.wait_ge(*b_copied[p].upto(g, n + 1))
                stats("d", g, x3)

            def b_factors(g):
                p, n = b_unit(V_E)
                keys = slice(ROW_LOW, ROW_LOW + H3)
                dve.wait_ge(*b_filled[p].upto(g, n + 1))
                nc.vector.tensor_reduce(top[0:H3, 0:1], bank[p][keys, :], AX.X, ALU.max, negate=True)
                nc.vector.tensor_reduce(top[keys, 0:1], bank[p][keys, :], AX.X, ALU.max, negate=True).then_inc(b_top.sem, 1)
                dve.wait_ge(*b_top.upto(g, 1))
                nc.vector.tensor_scalar(z8[:, :], bank[p][0:H3, :], top[0:H3, 0:1], 1.0 - SLOPE, ALU.subtract,
                                        ALU.mult).then_inc(b_z8.sem, 1)
                nc.vector.tensor_scalar(top[keys, 1:2], top[keys, 0:1], SLOPE, None, ALU.mult).then_inc(b_top.sem, 1)
                dve.wait_ge(*b_z8.upto(g, 1))
                nc.vector.tensor_scalar(uT[:, 0, :], z8[:, :], 0.0, None, ALU.min)
                nc.vector.tensor_scalar(uT[:, 1, :], z8[:, :], -1.0, 0.0, ALU.mult, ALU.min).then_inc(b_zz.sem, 1)

            def b_vcol(g):
                for i in range(2):
                    p, n = b_unit(V_VT + i)
                    dve.wait_ge(*b_filled[p].upto(g, n + 1))
                    nc.vector.tensor_copy(vcol[:, i].rearrange("p t h -> p (t h)"),
                                          bank[p][:, 0:T * H3]).then_inc(b_copied[p].sem, 1)
                dve.wait_ge(*b_uT.upto(g, 2))
                nc.vector.tensor_tensor(u_parts[ROW_LOW:ROW_LOW + H3], uT[:, :, :], u_parts[0:H3].bitcast(f32),
                                        ALU.subtract).then_inc(b_u_parts.sem, 1)

            def b_prob(h):
                def f(g):
                    p, n = b_unit(V_HEAD + 3 * h)
                    pl, nl = b_unit(V_HEAD + 3 * h + 1)
                    dve.wait_ge(*b_filled[p].upto(g, n + 1))
                    dve.wait_ge(*b_copied[pl].upto(g, nl + 1))
                    for u in (V_VT, V_VT + 1):
                        dve.wait_ge(*b_copied[u % 3].upto(g, u // 3 + 1))
                    for k in range(T):
                        i = nc.vector.scalar_tensor_tensor(out=low[:, h % 2, k, :], in0=bank[p][:, :],
                                                           scalar=vcol[:, 0, k, h:h + 1], in1=low[:, h % 2, k, :],
                                                           op0=ALU.mult, op1=ALU.max)
                    i.then_inc(b_copied[p].sem, 1)
                return f

            def b_mask(h):
                def f(g):
                    p, n = b_unit(V_HEAD + 3 * h)
                    dve.wait_ge(*b_copied[p].upto(g, n + 1))
                    if h >= 2:
                        po, no = b_unit(V_HEAD + 3 * (h - 2) + 2)
                        dve.wait_ge(*b_filled[po].upto(g, no + 1))
                    half = slice(2, 4)
                    nc.vector.tensor_tensor(p3T[:, h % 2, half], low[:, h % 2, half], edge[:, half, :],
                                            ALU.mult).then_inc(b_masked[1].sem, 1)
                return f

            def b_head(h):
                def f(g):
                    p, n = b_unit(V_HEAD + 3 * h + 2)
                    dve.wait_ge(*b_filled[p].upto(g, n + 1))
                    o = bank[p][:, 0:T * (DH3 + 1)].rearrange("p (t d) -> p t d", d=DH3 + 1)
                    nc.vector.reciprocal(rden3[:, h % 2], o[:, :, DH3:DH3 + 1]).then_inc(b_rden.sem, 1)
                    dve.wait_ge(*b_rden.upto(g, h + 1))
                    for t in range(T):
                        cols = x_out[:, t, h * DH3:(h + 1) * DH3]
                        last = nc.vector.scalar_tensor_tensor(out=cols, in0=o[:, t, 0:DH3], scalar=rden3[:, h % 2, t, :],
                                                              in1=cols, op0=ALU.mult, op1=ALU.add)
                    last.then_inc(b_copied[p].sem, 1)
                return f

            heads1, heads3, halves = range(H1), range(H3), range(2)
            second_pass(dve, {
                "p.x1": a_ln, "p.center": lambda g: shift("a", g), "a.edges": a_edges,
                "p.qlow": a_low(0, U_Q, q_high, q_low), "p.klow": a_low(1, U_K, k_high, k_low), **{f"a.xmid{q}": a_wo(q) for q in range(2)},
                **{f"a.max{h}{q}": a_max(h, q) for h in heads1 for q in halves},
                **{f"a.vmask{h}": a_mask(h) for h in heads1}, **{f"a.div{k}": a_div(k) for k in range(K)},
                "b.stats": b_ln, "b.center": lambda g: shift("b", g), "b.edges": b_edges, "b.ms": b_ms, "b.diag": b_diags,
                "b.stats3": d_ln, "b.center3": lambda g: shift("d", g), "b.factors": b_factors, "b.vcol": b_vcol,
                **{f"b.scale{n}": b_scale(n) for n in range(4)}, **{f"b.silu{n}": b_silu(n) for n in range(4)},
                **{f"b.x3{q}": b_x3(q) for q in halves},
                **{f"h.prob{h}": b_prob(h) for h in heads3}, **{f"h.vmask{h}": b_mask(h) for h in heads3},
                **{f"h.head{h}": b_head(h) for h in heads3}})

        @block.tensor
        def _(pe):
            pe.wait_ge(weights_in.sem, n_loads * 16)
            pe.wait_ge(setup.sem, 11)

            def flip(dst, src, k):
                for t in range(T):
                    i = nc.tensor.transpose(dst[:, t * P:(t + 1) * P], src[:, t, k * P:(k + 1) * P], ident[:, :])
                return i

            def lin(g, par):
                pe.wait_ge(*c_hT_ok.upto(g, 1))
                if not first(g):
                    pe.wait_ge(*c_scaled.upto(g, 0))
                for q in range(2):
                    for t in (2 * q, 2 * q + 1):
                        for k in range(K):
                            i = nc.tensor.matmul(pair[1][:, t // 2, (t % 2) * D:(t % 2 + 1) * D],
                                                 c_hT[:, k, t * P:(t + 1) * P], w0_s[:, k, :], start=k == 0, stop=k == K - 1)
                    i.then_inc(c_lin.sem, 1)

            def turn(g, par):
                pe.wait_ge(*lns["c"]["h"].upto(g, 1))
                if not first(g):
                    pe.wait_ge(*c_hT_ok.upto(g, 0))
                for k in range(K):
                    i = flip(pair[0][:, k, :], c_h, k)
                i.then_inc(c_hT_sum.sem, 1)

            def degree(g, par, t):
                if t == 0:
                    pe.wait_ge(*c_eye.upto(g, 1))
                    if not first(g):
                        pe.wait_ge(*c_deg_ok.upto(g, 0))
                for k in range(T):
                    i = nc.tensor.matmul(bank[0][:, t:t + 1], c_at[:, par, k, t * P:(t + 1) * P], ones[:, 0:1],
                                         start=k == 0, stop=k == T - 1)
                if t == T - 1:
                    i.then_inc(c_deg_sum.sem, 1)

            def aggregate(g, par):
                pe.wait_ge(*c_hs_ok.upto(g, 1))
                if not first(g):
                    pe.wait_ge(*c_o_ok.upto(g, 0))
                for t in range(T):
                    dst = (obank if t < 2 else bank[2])[:, (t % 2) * D:(t % 2 + 1) * D]
                    for k in range(T):
                        i = nc.tensor.matmul(dst, c_at[:, par, k, t * P:(t + 1) * P], c_hs[:, k, :],
                                             start=k == 0, stop=k == T - 1)
                    if t == T - 1:
                        i.then_inc(c_agg.sem, 1)
                    if t and (not isinstance(g.loop, int) or g.below(G - 1)):
                        for u in ((0,), (1,), (2, 3))[t - 1]:
                            degree(g.plus(1), 1 - par, u)

            def first_degrees(g, par):
                if first(g):
                    for t in range(T):
                        degree(g, par, t)

            first_pass(pe, [(0, lin), (1, turn), (1, first_degrees), (0, aggregate)])

            for par in range(2):
                pe.wait_ge(c_added[par].sem, G)
            pe.wait_ge(*c_o_ok.upto(Graph(G), 0))
            for n, s in enumerate((sum_o, sum_sq)):
                for t in range(T):
                    i = nc.tensor.matmul(obank[:, n * D:(n + 1) * D], ones[:, :], s[:, t, :], start=t == 0, stop=t == T - 1)
                i.then_inc(c_sums.sem, 1)
            pe.wait_ge(bn_steps.sem, 7)

            def a_free(g, u):
                p, n = a_unit(u)
                if n or not first(g):
                    pe.wait_ge(*a_copied[p].upto(g, n))
                return pair[p], a_filled[p].sem

            def b_free(g, u):
                p, n = b_unit(u)
                if n or not first(g):
                    pe.wait_ge(*b_copied[p].upto(g, n))
                return bank[p], b_filled[p].sem

            def a_flip(g):
                pe.wait_ge(*lns["a"]["h"].upto(g, 1))
                dst, full = a_free(g, U_HT)
                for k in range(K):
                    i = flip(dst[:, k, :], a_h, k)
                i.then_inc(full, 1)

            def rows(dst, hT, w, q):
                for t in (2 * q, 2 * q + 1):
                    for k in range(K):
                        i = nc.tensor.matmul(dst[:, t // 2, (t % 2) * D:(t % 2 + 1) * D], hT[:, k, t * P:(t + 1) * P],
                                             w[:, k, :], start=k == 0, stop=k == K - 1)
                return i

            def a_qk(u, w, j):
                def f(g):
                    if j == 0:
                        pe.wait_ge(*a_copied[0].upto(g, 1))
                    dst, full = a_free(g, u)
                    for k in range(K):
                        i = nc.tensor.matmul(dst[:, j, :], w[:, k, j * P:(j + 1) * P], a_hT[:, k, :],
                                             start=k == 0, stop=k == K - 1)
                    if j == K - 1:
                        i.then_inc(full, 1)
                return f

            def a_v(q):
                def f(g):
                    dst, full = a_free(g, U_V)
                    i = rows(dst, a_hT, wv_s, q)
                    if q == 1:
                        i.then_inc(full, 1)
                return f

            def a_nat(h, q):
                def f(g):
                    pe.wait_ge(*a_qk_in.upto(g, 24))
                    dst, full = a_free(g, U_NAT + 2 * h + q)
                    for b in range(2):
                        t = 2 * q + b
                        i = nc.tensor.matmul(dst[:, b, :], q_parts[0:ROW_SHIFT, h, t * P:(t + 1) * P],
                                             k_parts[0:ROW_SHIFT, h, :], start=True, stop=True)
                    i.then_inc(full, 1)
                return f

            def a_shift(g):
                for p in range(2):
                    pe.wait_ge(*a_copied[p].upto(g, U_ST // 2))
                if not first(g):
                    pe.wait_ge(*o_copied.upto(g, 0))
                for t in range(T):
                    i = nc.tensor.transpose(obank[0:H1, t * P:(t + 1) * P], minus_max[:, t, :], ident[:, :])
                i.then_inc(shift_sum.sem, 1)

            def a_scores(h, q):
                def f(g):
                    pe.wait_ge(*a_shift_in.upto(g, H1))
                    dst, full = a_free(g, U_ST + 2 * h + q)
                    for b in range(2):
                        k = 2 * q + b
                        i = nc.tensor.matmul(dst[:, b, :], k_parts[0:ROW_SHIFT + 1, h, k * P:(k + 1) * P],
                                             q_parts[0:ROW_SHIFT + 1, h, :], start=True, stop=True)
                    i.then_inc(full, 1)
                return f

            def a_values(n, q):
                def f(g):
                    pe.wait_ge(*a_masked[q].upto(g, 2 * n + 2))
                    if q == 0:
                        pe.wait_ge(*o_copied.upto(g, 1 + n))
                    for k in (2 * q, 2 * q + 1):
                        two_heads = v1[:, k * H1 // 2 + n].rearrange("p c d -> p (c d)")
                        for i in range(2):
                            last = nc.tensor.matmul(obank[2 * DH1 * i:2 * DH1 * (i + 1), :],
                                                    two_heads[:, DH1 * i:DH1 * (i + 2)], pT[:, i, k, :],
                                                    start=k == 0, stop=k == T - 1)
                    last.then_inc(a_used.sem, 1)
                return f

            def a_wo(q):
                def f(g):
                    if q == 0:
                        pe.wait_ge(*a_divided.upto(g, K))
                    pe.wait_ge(*o_copied.upto(g, O_FILLS - 2 + q))
                    for t in (2 * q, 2 * q + 1):
                        for k in range(K):
                            i = nc.tensor.matmul(obank[:, (t % 2) * D:(t % 2 + 1) * D], att1T[:, k, t * P:(t + 1) * P],
                                                 wo_s[:, k, :], start=k == 0, stop=k == K - 1)
                    i.then_inc(wo_sum.sem, 1)
                return f

            def b_agg(j):
                def f(g):
                    pe.wait_ge(*lns["b"]["h"].upto(g, 1))
                    pe.wait_ge(*b_eye.upto(g, 1))
                    dst, full = b_free(g, V_AGG + j)
                    for k in range(T):
                        i = nc.tensor.matmul(dst[:, :], b_h[:, k, j * P:(j + 1) * P], b_at[:, k, :],
                                             start=k == 0, stop=k == T - 1)
                    i.then_inc(full, 1)
                return f

            def b_hid(t):
                def f(g):
                    if t == 0:
                        for j in range(K):
                            pe.wait_ge(*b_copied[j].upto(g, 1))
                    dst, full = b_free(g, V_HID + t)
                    for k in range(K):
                        i = nc.tensor.matmul(dst[:, :], w1_s[:, k, t * P:(t + 1) * P], aggT[:, k, :],
                                             start=k == 0, stop=k == K - 1)
                    i.then_inc(full, 1)
                return f

            def b_ms(g):
                pe.wait_ge(*b_summed.upto(g, KH - 1))
                dst, full = b_free(g, V_MS)
                for t in range(T):
                    i = nc.tensor.matmul(dst[:, t:t + 1], hsum[:, t * P:(t + 1) * P], ones[:, 0:1], start=True, stop=True)
                i.then_inc(full, 1)

            def b_rb(g):
                pe.wait_ge(*b_diag.upto(g, 1))
                dst, full = b_free(g, V_RB)
                nc.tensor.matmul(dst[:, :], ones[:, :], diag[:, :, :].rearrange("p t n -> p (t n)"),
                                 start=True, stop=True).then_inc(full, 1)

            def b_out2(t):
                def f(g):
                    p, n = b_unit(V_RB)
                    pe.wait_ge(*b_copied[p].upto(g, n + 1))
                    dst, full = b_free(g, V_OUT + t // 2)
                    for k in range(KH):
                        i = nc.tensor.matmul(dst[:, (t % 2) * D:(t % 2 + 1) * D], hid[:, k, t * P:(t + 1) * P],
                                             w2_s[:, k, :], start=k == 0, stop=k == KH - 1)
                    if t % 2 == 1:
                        i.then_inc(full, 1)
                return f

            def d_flip(g):
                pe.wait_ge(*lns["d"]["h"].upto(g, 1))
                for k in range(K):
                    dst, full = b_free(g, V_HT + k)
                    flip(dst, d_h, k).then_inc(full, 1)

            def b_v3(q):
                def f(g):
                    for j in range(K):
                        p, n = b_unit(V_HT + j)
                        pe.wait_ge(*b_copied[p].upto(g, n + 1))
                    dst, full = b_free(g, V_V3 + q)
                    for t in (2 * q, 2 * q + 1):
                        for k in range(K):
                            i = nc.tensor.matmul(dst[:, (t % 2) * D:(t % 2 + 1) * D], d_hT[:, k, t * P:(t + 1) * P],
                                                 w3_s[:, k, :], start=k == 0, stop=k == K - 1)
                    i.then_inc(full, 1)
                return f

            def b_terms(g):
                for j in range(K):
                    p, n = b_unit(V_HT + j)
                    pe.wait_ge(*b_copied[p].upto(g, n + 1))
                dst, full = b_free(g, V_E)
                for k in range(K):
                    i = nc.tensor.matmul(dst[0:ROW_LOW + H3, :], att_w[:, k, :], d_hT[:, k, :], start=k == 0, stop=k == K - 1)
                i.then_inc(full, 1)

            def b_vt(g):
                p, n = b_unit(V_E)
                pe.wait_ge(*b_copied[p].upto(g, n + 1))
                keys = slice(ROW_LOW, ROW_LOW + H3)
                for i in range(2):
                    dst, full = b_free(g, V_VT + i)
                    for t in range(T):
                        last = nc.tensor.matmul(dst[:, t * H3:(t + 1) * H3], vT[:, i, t * P:(t + 1) * P], ident[keys, keys],
                                                start=True, stop=True)
                    last.then_inc(full, 1)

            def b_spread(h):
                def f(g):
                    pe.wait_ge(*b_u_parts.upto(g, 1))
                    for s in range(2):
                        dst, full = b_free(g, V_HEAD + 3 * h + s)
                        nc.tensor.matmul(dst[:, :], sel3[:, h, :], u_parts[:, s, :], start=True, stop=True).then_inc(full, 1)
                return f

            def b_values(h, q):
                def f(g):
                    if q == 0:
                        for i in range(2):
                            pe.wait_ge(*b_masked[i].upto(g, h + 1))
                    dst, full = b_free(g, V_HEAD + 3 * h + 2)
                    w = DH3 + 1
                    for t in (2 * q, 2 * q + 1):
                        for k in range(T):
                            i = nc.tensor.matmul(dst[:, t * w:(t + 1) * w], p3T[:, h % 2, k, t * P:(t + 1) * P],
                                                 v3[:, k * H3 + h, :], start=k == 0, stop=k == T - 1)
                    if q == 1:
                        i.then_inc(full, 1)
                return f

            heads1, heads3, halves = range(H1), range(H3), range(2)
            second_pass(pe, {
                "p.flip": a_flip, "a.shift": a_shift,
                **{f"p.q{j}": a_qk(U_Q, wq_s, j) for j in range(K)}, **{f"p.k{j}": a_qk(U_K, wk_s, j) for j in range(K)},
                **{f"p.v{q}": a_v(q) for q in halves}, **{f"a.wo{q}": a_wo(q) for q in halves},
                **{f"a.nat{h}{q}": a_nat(h, q) for h in heads1 for q in halves},
                **{f"a.scores{h}{q}": a_scores(h, q) for h in heads1 for q in halves},
                **{f"a.values{n}{q}": a_values(n, q) for n in range(H1 // 2) for q in halves},
                "b.sum": b_ms, "b.spread": b_rb, "b.flip3": d_flip, "b.e": b_terms, "b.vt": b_vt,
                **{f"b.agg{j}": b_agg(j) for j in range(K)}, **{f"b.hid{t}": b_hid(t) for t in range(KH)},
                **{f"b.out2{t}": b_out2(t) for t in range(T)}, **{f"b.v3{q}": b_v3(q) for q in halves},
                **{f"h.spread{h}": b_spread(h) for h in heads3},
                **{f"h.values{h}{q}": b_values(h, q) for h in heads3 for q in halves}})



def kernel(**inputs):
    import concourse.bacc as _bacc
    from concourse.bass_utils import run_bass_kernel_spmd as _run

    i = inputs
    t2 = lambda w: w.T
    laid = {
        "x": i["x"], "adjT": i["adj"].transpose(0, 2, 1), "w0T": t2(i["L0_gnn_W"]), "b0": i["L0_gnn_b"],
        "bn_w": i["L0_gnn_bn_weight"], "bn_b": i["L0_gnn_bn_bias"], "res_w": i["L0_gnn_res_weight"].reshape(1),
        "wqT": t2(i["L1_gnn_Wq"]), "wkT": t2(i["L1_gnn_Wk"]), "wvT": t2(i["L1_gnn_Wv"]), "woT": t2(i["L1_gnn_Wo"]),
        "bo": i["L1_gnn_bo"], "eps": i["L2_gnn_epsilon"].reshape(1), "w1": i["L2_gnn_W1"],
        "b1": i["L2_gnn_b1"].reshape(KH, P).T, "rms_w": i["L2_gnn_rms_weight"].reshape(KH, P).T, "w2": i["L2_gnn_W2"],
        "b2": i["L2_gnn_b2"], "w3": i["L3_gnn_W"], "att": i["L3_gnn_a"].reshape(-1),
    }
    nc = _bacc.Bacc("TRN2", target_bir_lowering=False, num_devices=1)
    arrays = {f"in_{k}": np.ascontiguousarray(v) for k, v in laid.items()}
    aps = [nc.dram_tensor(n, a.shape, mybir.dt.from_np(a.dtype), kind="ExternalInput").ap() for n, a in arrays.items()]
    aps.append(nc.dram_tensor("out_0", (G, N, D), mybir.dt.float32, kind="ExternalOutput").ap())
    gnn_stack(nc, *aps)
    return _run(nc, [arrays], core_ids=[0]).results[0]["out_0"]
```
